# Optimizing a Trainium2 kernel written in Bass

```python
import numpy as np
import jax
import jax.numpy as jnp

def _softmax(x, axis=-1):
    return jax.nn.softmax(x, axis=axis)

def _gelu(x):
    return jax.nn.gelu(x, approximate=True)

def _silu(x):
    return jax.nn.silu(x)

def _sigmoid(x):
    return jax.nn.sigmoid(x)

def _layernorm(x, axis=-1, eps=1e-05):
    m = jnp.mean(x, axis=axis, keepdims=True)
    v = jnp.var(x, axis=axis, keepdims=True)
    return (x - m) / jnp.sqrt(v + eps)

def _scatter_add(tgt, idx, src, axis=0):
    return tgt.at[idx].add(src)

def _segment_sum(src, seg, n):
    return jax.ops.segment_sum(src, seg, n)
kernel_name = 'mk_macaron_d1_jaxref_r8_1388b2'

def setup_inputs(seed: int=0):
    np.random.seed(seed)
    _w = jnp.asarray

    def _L0_attn_setup():
        import jax, jax.numpy as jnp
        import numpy as np
        N_EMBED = 128
        N_HEADS = 16
        HEAD_SIZE = N_EMBED // N_HEADS
        key = jax.random.key(seed)
        ks = jax.random.split(key, 9)
        d = N_EMBED
        s = 1.0 / np.sqrt(d)
        return {'x': jax.random.normal(ks[0], (2, 256, d), dtype=jnp.float32), 'Wq': jax.random.uniform(ks[1], (d, d), jnp.float32, -s, s), 'bq': jax.random.uniform(ks[2], (d,), jnp.float32, -s, s), 'Wk': jax.random.uniform(ks[3], (d, d), jnp.float32, -s, s), 'bk': jax.random.uniform(ks[4], (d,), jnp.float32, -s, s), 'Wv': jax.random.uniform(ks[5], (d, d), jnp.float32, -s, s), 'bv': jax.random.uniform(ks[6], (d,), jnp.float32, -s, s), 'Wo': jax.random.uniform(ks[7], (d, d), jnp.float32, -s, s), 'bo': jax.random.uniform(ks[8], (d,), jnp.float32, -s, s)}
    _L0_attn_in = _L0_attn_setup()

    def _L0_ffn_setup():
        import jax, jax.numpy as jnp
        import numpy as np
        B, S, D, F, E = (8, 128, 128, 512, 8)
        EPS = 1e-05
        key = jax.random.key(seed)
        ks = jax.random.split(key, 4)
        s = 0.02
        return {'input_features': jax.random.normal(ks[0], (B, S, D), jnp.float32), 'centroids': jax.random.normal(ks[1], (E, D), jnp.float32) * 0.1, 'ln_g': jnp.ones((E, D), jnp.float32), 'ln_b': jnp.zeros((E, D), jnp.float32), 'w1': jax.random.normal(ks[2], (E, D, F), jnp.float32) * s, 'b1': jnp.zeros((E, F), jnp.float32), 'w2': jax.random.normal(ks[3], (E, F, D), jnp.float32) * s, 'b2': jnp.zeros((E, D), jnp.float32)}
    _L0_ffn_in = _L0_ffn_setup()
    _d = {'L0_attn_x': _L0_attn_in['x'], 'L0_attn_Wq': _L0_attn_in['Wq'], 'L0_attn_bq': _L0_attn_in['bq'], 'L0_attn_Wk': _L0_attn_in['Wk'], 'L0_attn_bk': _L0_attn_in['bk'], 'L0_attn_Wv': _L0_attn_in['Wv'], 'L0_attn_bv': _L0_attn_in['bv'], 'L0_attn_Wo': _L0_attn_in['Wo'], 'L0_attn_bo': _L0_attn_in['bo'], 'L0_ffn_centroids': _L0_ffn_in['centroids'], 'L0_ffn_ln_g': _L0_ffn_in['ln_g'], 'L0_ffn_ln_b': _L0_ffn_in['ln_b'], 'L0_ffn_w1': _L0_ffn_in['w1'], 'L0_ffn_b1': _L0_ffn_in['b1'], 'L0_ffn_w2': _L0_ffn_in['w2'], 'L0_ffn_b2': _L0_ffn_in['b2']}
    _x0 = _d['L0_attn_x']
    _d['L0_attn_x'] = jax.random.normal(jax.random.fold_in(jax.random.key(seed), 1), (4, 1024, 128), dtype=_x0.dtype)
    del _x0
    return _d

def reference(L0_attn_x, L0_attn_Wq, L0_attn_bq, L0_attn_Wk, L0_attn_bk, L0_attn_Wv, L0_attn_bv, L0_attn_Wo, L0_attn_bo, L0_ffn_centroids, L0_ffn_ln_g, L0_ffn_ln_b, L0_ffn_w1, L0_ffn_b1, L0_ffn_w2, L0_ffn_b2):

    def _L0_attn_ref(x, Wq, bq, Wk, bk, Wv, bv, Wo, bo):
        import jax, jax.numpy as jnp
        import numpy as np
        N_EMBED = 128
        N_HEADS = 16
        HEAD_SIZE = N_EMBED // N_HEADS
        B, T, D = x.shape
        H, Hd = (N_HEADS, HEAD_SIZE)
        q = (x @ Wq + bq).reshape(B, T, H, Hd).transpose(0, 2, 1, 3)
        k = (x @ Wk + bk).reshape(B, T, H, Hd).transpose(0, 2, 1, 3)
        v = (x @ Wv + bv).reshape(B, T, H, Hd).transpose(0, 2, 1, 3)
        scores = jnp.einsum('bhqd,bhkd->bhqk', q, k) * Hd ** (-0.5)
        causal = jnp.tril(jnp.ones((T, T), dtype=bool))
        scores = jnp.where(causal[None, None], scores, -jnp.inf)
        probs = jax.nn.softmax(scores, axis=-1)
        out = jnp.einsum('bhqk,bhkd->bhqd', probs, v)
        out = out.transpose(0, 2, 1, 3).reshape(B, T, D)
        return out @ Wo + bo

    def _L0_ffn_ref(input_features, centroids, ln_g, ln_b, w1, b1, w2, b2):
        import jax, jax.numpy as jnp
        import numpy as np
        B, S, D, F, E = (8, 128, 128, 512, 8)
        EPS = 1e-05
        x = input_features.reshape(-1, D)
        aff = jax.lax.stop_gradient(x @ centroids.T)
        eid = jnp.argmax(aff, axis=-1)
        alpha = jax.nn.sigmoid(jnp.sum(x * centroids[eid], axis=-1, keepdims=True))
        mu = jnp.mean(x, axis=-1, keepdims=True)
        var = jnp.mean((x - mu) ** 2, axis=-1, keepdims=True)
        xn = (x - mu) * jax.lax.rsqrt(var + EPS)
        xln = xn * ln_g[eid] + ln_b[eid]
        onehot = jax.nn.one_hot(eid, E, dtype=x.dtype)
        ffn = jnp.zeros_like(x)
        for e in range(E):
            h = jax.nn.relu(xln @ w1[e] + b1[e])
            ffn = ffn + onehot[:, e:e + 1] * (h @ w2[e] + b2[e])
        out = x + alpha * ffn
        return out.reshape(input_features.shape)
    x = L0_attn_x
    x = x + 0.5 * _L0_ffn_ref(_layernorm(x, axis=-1), L0_ffn_centroids, L0_ffn_ln_g, L0_ffn_ln_b, L0_ffn_w1, L0_ffn_b1, L0_ffn_w2, L0_ffn_b2)
    x = x + _L0_attn_ref(_layernorm(x, axis=-1), L0_attn_Wq, L0_attn_bq, L0_attn_Wk, L0_attn_bk, L0_attn_Wv, L0_attn_bv, L0_attn_Wo, L0_attn_bo)
    x = x + 0.5 * _L0_ffn_ref(_layernorm(x, axis=-1), L0_ffn_centroids, L0_ffn_ln_g, L0_ffn_ln_b, L0_ffn_w1, L0_ffn_b1, L0_ffn_w2, L0_ffn_b2)
    return x

_drawn_inputs = setup_inputs


def setup_inputs(seed=0):
    import zlib

    import numpy as np

    out = dict(_drawn_inputs(seed))
    spreads = {'L0_ffn_ln_g': (1.0, 0.6),
     'L0_ffn_ln_b': (0.0, 0.8),
     'L0_ffn_b1': (0.0, 0.545),
     'L0_ffn_b2': (0.0, 0.1)}
    factors = {'L0_attn_Wq': 6.24,
     'L0_attn_bq': 8.0,
     'L0_attn_Wk': 6.267,
     'L0_attn_bk': 64.0,
     'L0_attn_Wv': 2.82,
     'L0_attn_bv': 2.72}
    for name, (base, spread) in spreads.items():
        noise = np.random.default_rng([zlib.crc32(name.encode()), seed]).standard_normal(out[name].shape)
        drawn = base * np.exp(spread * noise) if base else spread * noise
        out[name] = jnp.asarray(drawn.astype(out[name].dtype))
    for name, factor in factors.items():
        out[name] = (out[name] * factor).astype(out[name].dtype)
    return out
```

```python
import numpy as np
import concourse.bass as bass
from concourse import mybir
from concourse.alu_op_type import AluOpType as ALU
from contextlib import ExitStack

F32 = mybir.dt.float32
BF16 = mybir.dt.bfloat16
I32 = mybir.dt.int32
ACT = mybir.ActivationFunctionType
AX = mybir.AxisListType

B, T, D = 4, 1024, 128
H, HD = 16, 8
F, E = 512, 8
P = 128
N = B * T
NT = N // P
TB = T // P
FC = F // P
SLOTS = (N + E * (P - 1)) // P
SLOTS += SLOTS % 2
TRASH = N
EPS = 1e-5
BIG = -1.0e30
LOWEST = -3.0e38
GH = 4
NG = H // GH
TERMS = 6 * HD
MROWS = 3
SCALE = HD ** -0.5
QW = T // 2
HT = TB // 2


class Shared:
    pass


def serial(eng, sem):
    count = [0]

    def link(ins):
        count[0] += 1
        ins.then_inc(sem, 1)
        eng.wait_ge(sem, count[0])
    return link


def norm_finish(nc, link, sh):
    st = sh.stats
    link(nc.vector.tensor_tensor(sh.mean[:], st[:, :, 1], st[:, :, 4], ALU.add))
    link(nc.vector.tensor_tensor(sh.tmp_a[:], st[:, :, 1], st[:, :, 4], ALU.subtract))
    link(nc.vector.tensor_tensor(sh.tmp_b[:], st[:, :, 2], st[:, :, 5], ALU.add))
    link(nc.vector.tensor_scalar(sh.mean[:], sh.mean[:], 0.5, None, ALU.mult))
    link(nc.vector.scalar_tensor_tensor(out=sh.tmp_a[:], in0=sh.tmp_a[:], scalar=0.25, in1=sh.tmp_a[:],
                                        op0=ALU.mult, op1=ALU.mult))
    link(nc.vector.scalar_tensor_tensor(out=sh.tmp_b[:], in0=sh.tmp_b[:], scalar=1.0 / D, in1=sh.tmp_a[:],
                                        op0=ALU.mult, op1=ALU.add))


def setup_phase(nc, sh, a):
    with ExitStack() as ctx:
        sem = lambda n: ctx.enter_context(nc.semaphore(n))
        loads, cgb_in = sem("su_loads"), sem("su_cgb")
        pool_step, consts, dve_step = sem("su_pool_step"), sem("su_consts"), sem("su_dve_step")
        cgb_ps, dve_fill = sem("su_cgb_ps"), sem("su_dve_fill")
        cgb = ctx.enter_context(nc.sbuf_tensor("su_cgb_rows", [3 * E, D], F32))
        blk = ctx.enter_context(nc.Block())

        @blk.sync
        def _(sp):
            sp.dma_start(cgb[0:E, :], a["centroids"]).then_inc(cgb_in, 16)
            sp.dma_start(cgb[E:2 * E, :], a["ln_g"]).then_inc(cgb_in, 16)
            sp.dma_start(cgb[2 * E:3 * E, :], a["ln_b"]).then_inc(cgb_in, 16)
            sp.dma_start(sh.x[:], a["x"].rearrange("b (t p) d -> p (b t) d", p=P)).then_inc(loads, 16)
            for name in ("Wq", "Wk", "Wv", "Wo"):
                sp.dma_start(sh.w[name][:], a[name]).then_inc(loads, 16)
            sp.dma_start(sh.bqk[:, 0:1], a["bq"].rearrange("(p o) -> p o", o=1)).then_inc(loads, 16)
            sp.dma_start(sh.bqk[:, 1:2], a["bk"].rearrange("(p o) -> p o", o=1)).then_inc(loads, 16)
            sp.wait_ge(loads, 16 * 7)

        @blk.scalar
        def _(act):
            act.dma_start(sh.w1[:], a["w1"].rearrange("e d f -> d e f")).then_inc(sh.act_loads, 16)
            act.dma_start(sh.w2[:], a["w2"].rearrange("e (c p) d -> p e c d", p=P)).then_inc(sh.act_loads, 16)
            act.dma_start(sh.b1bc[:], a["b1"].rearrange("e f -> (e f)").rearrange("(o n) -> o n", o=1)
                          .to_broadcast([P, E * F])).then_inc(sh.act_loads, 16)
            act.dma_start(sh.b2bc[:], a["b2"].rearrange("e f -> (e f)").rearrange("(o n) -> o n", o=1)
                          .to_broadcast([P, E * D])).then_inc(sh.act_loads, 16)
            act.dma_start(sh.bvbc[:], a["bv"].rearrange("(o n) -> o n", o=1).to_broadcast([P, D])) \
               .then_inc(sh.act_loads, 16)
            act.dma_start(sh.bobc[:], a["bo"].rearrange("(o n) -> o n", o=1).to_broadcast([P, D])) \
               .then_inc(sh.act_loads, 16)
            act.wait_ge(sh.act_loads, 16 * 6)

        @blk.gpsimd
        def _(pool):
            link = serial(pool, pool_step)
            sel = nc.gpsimd.affine_select
            link(nc.gpsimd.memset(sh.ident[:], 0.0))
            link(sel(out=sh.ident[:], in_=sh.ident[:], compare_op=ALU.not_equal, fill=1.0, base=0,
                     pattern=[[-1, P]], channel_multiplier=1))
            nc.gpsimd.tensor_copy(sh.identb[:], sh.ident[:]).then_inc(consts, 1)
            link(nc.gpsimd.memset(sh.before[:], 1.0))
            sel(out=sh.before[:], in_=sh.before[:], compare_op=ALU.is_gt, fill=0.0, base=0,
                pattern=[[1, P]], channel_multiplier=-1).then_inc(consts, 1)
            link(nc.gpsimd.memset(sh.mask_qk[:], 0.0))
            sel(out=sh.mask_qk[:], in_=sh.mask_qk[:], compare_op=ALU.is_ge, fill=BIG, base=0,
                pattern=[[0, 4], [-1, P]], channel_multiplier=1).then_inc(consts, 1)
            link(nc.gpsimd.memset(sh.mask_kq[:], 0.0))
            sel(out=sh.mask_kq[:], in_=sh.mask_kq[:], compare_op=ALU.is_ge, fill=BIG, base=0,
                pattern=[[1, P]], channel_multiplier=-1).then_inc(consts, 1)
            iota = lambda out, pattern, base, cm: nc.gpsimd.iota(
                out, pattern, base=base, channel_multiplier=cm, allow_small_or_imprecise_dtypes=True)
            iota(sh.em8[:], [[1, E]], -E, 0).then_inc(consts, 1)
            iota(sh.thr[:], [[P, NT]], 0, 0).then_inc(consts, 1)
            iota(sh.slot_id[:], [[1, SLOTS], [0, E - 1]], 0, 0).then_inc(consts, 1)
            iota(sh.row128[:], [[1, P]], 0, 0).then_inc(consts, 1)
            iota(sh.row_slots[:], [[1, SLOTS]], 0, 0).then_inc(consts, 1)
            iota(sh.tile_id[:], [[1, NT]], 0, 0).then_inc(consts, 1)
            iota(sh.part_id[:], [[0, 1]], 0, 1).then_inc(consts, 1)
            iota(sh.trash[:], [[P, SLOTS]], TRASH, 1).then_inc(consts, 1)
            pool.wait_ge(consts, 12)

        @blk.vector
        def _(dve):
            nc.vector.memset(sh.onesb[:], 1.0).then_inc(dve_fill, 1)
            nc.vector.memset(sh.neg_half[:], -0.5).then_inc(dve_fill, 1)
            nc.vector.memset(sh.ones8[:], 1.0).then_inc(dve_fill, 1)
            link = serial(dve, dve_step)
            link(nc.vector.memset(sh.keep[:], 1.0))
            nc.vector.memset(sh.keep[:, :, 0:1], 0.0).then_inc(dve_fill, 1)
            nc.vector.memset(sh.block_max[:], LOWEST).then_inc(dve_fill, 1)
            nc.vector.memset(sh.o_sb[:], 1.0).then_inc(dve_fill, 1)
            for g in range(len(sh.k_op)):
                nc.vector.memset(sh.k_op[g][:], 1.0).then_inc(dve_fill, 1)
            for v in sh.v_aug:
                link(nc.vector.memset(v[:], 0.0))
                nc.vector.memset(v[:, :, :, HD:HD + 1], 1.0).then_inc(dve_fill, 1)
            dve.wait_ge(dve_fill, 6 + len(sh.k_op) + len(sh.v_aug))
            dve.wait_ge(cgb_ps, 1)
            link(nc.vector.tensor_copy(sh.cgbT[:], sh.bank[0][:, 0:3 * E]))

        @blk.tensor
        def _(pe):
            pe.wait_ge(consts, 12)
            pe.wait_ge(cgb_in, 48)
            nc.tensor.transpose(sh.bank[0][:, 0:3 * E], cgb[:], sh.ident[0:3 * E, 0:3 * E]).then_inc(cgb_ps, 1)


def norm_apply(nc, dve, link, sh, src, dst, tiles, ready):
    with dve.Fori(0, tiles // 4) as g:
        for k in range(4):
            t = g * 4
            ins = nc.vector.tensor_scalar(dst[:, bass.ds(t + k, 1), :].rearrange("p o d -> p (o d)"),
                                          src[:, bass.ds(t + k, 1), :].rearrange("p o d -> p (o d)"),
                                          sh.mean[:, bass.ds(t + k, 1)], sh.rstd[:, bass.ds(t + k, 1)],
                                          ALU.subtract, ALU.mult)
        ins.then_inc(ready, 1)


def norm_stats(nc, dve, sh, src, tiles, done):
    with dve.Fori(0, tiles // 4) as g:
        for k in range(4):
            t = g * 4
            ins = nc.vector.bn_stats(sh.stats[:, bass.ds(t + k, 1), :].rearrange("p o d -> p (o d)"),
                                     src[:, bass.ds(t + k, 1), :].rearrange("p o d -> p (o d)"))
        ins.then_inc(done, 1)


def route_phase(nc, sh, f):
    with ExitStack() as ctx:
        sem = lambda n: ctx.enter_context(nc.semaphore(f"r{f}_{n}"))
        sb = lambda n, s, d: ctx.enter_context(nc.sbuf_tensor(f"r{f}_{n}", s, d))
        dve_step, var_ready, rstd_ready = sem("dve_step"), sem("var_ready"), sem("rstd_ready")
        stats_done, y_ready, xn_ready, xn_stored = sem("stats_done"), sem("y_ready"), sem("xn_ready"), sem("xn_stored")
        yT_ps, yT_ready, aff_ready = sem("yT_ps"), sem("yT_ready"), sem("aff_ready")
        shift_ready = sem("shift_ready")
        mx_ready, exp_ready, onehot_ready, rank_ready = sem("mx_ready"), sem("exp_ready"), sem("onehot_ready"), sem("rank_ready")
        place_ready, inverse_ready = sem("place_ready"), sem("inverse_ready")
        yT = [sb(f"yT{i}", [P, 4 * P], F32) for i in range(2)]
        wide = lambda n, d=F32: sb(n, [P, NT, E], d)
        eq, cand, t1 = wide("eq"), wide("cand"), wide("t1")
        onehot = wide("onehot", BF16)
        tot, cum, before_tile, gt = [sb(n, [P, E, NT], F32) for n in ("tot", "cum", "before_tile", "gt")]
        cmin, lo, hi, ex = [sb(n, [P, NT], F32) for n in ("cmin", "lo", "hi", "ex")]
        ntiles, upto, base = [sb(n, [P, E], F32) for n in ("ntiles", "upto", "base")]
        place, lo_i, hi_i = [sb(n, [P, NT], I32) for n in ("place", "lo_i", "hi_i")]
        ge = sb("ge", [P, SLOTS, E - 1], F32)
        slot_e = sb("slot_e", [P, SLOTS], F32)
        at_lo = sb("at_lo", [P, NT, P], BF16)
        at_hi = sb("at_hi", [P, NT, 3, SLOTS], BF16)
        inv = sb("inv", [P, 3 * SLOTS], F32)
        tr, row = sb("tr", [P, SLOTS], F32), sb("row", [P, SLOTS], F32)
        psT, aff, cnt, invp = [sh.bank[0], sh.bank[1]], sh.bank[2], sh.bank[3], sh.bank[4]
        blk = ctx.enter_context(nc.Block())

        @blk.vector
        def _(dve):
            link = serial(dve, dve_step)
            norm_stats(nc, dve, sh, sh.x, NT, stats_done)
            dve.wait_ge(stats_done, NT // 4)
            norm_finish(nc, link, sh)
            nc.vector.tensor_scalar_add(sh.tmp_b[:], sh.tmp_b[:], EPS).then_inc(var_ready, 1)
            dve.wait_ge(rstd_ready, 1)
            norm_apply(nc, dve, link, sh, sh.x, sh.y, NT, y_ready)
            dve.wait_ge(y_ready, NT // 4)
            norm_stats(nc, dve, sh, sh.y, NT, stats_done)
            dve.wait_ge(stats_done, 2 * (NT // 4))
            norm_finish(nc, link, sh)
            nc.vector.tensor_scalar_add(sh.tmp_b[:], sh.tmp_b[:], EPS).then_inc(var_ready, 1)
            dve.wait_ge(rstd_ready, 2)
            nc.vector.scalar_tensor_tensor(out=sh.shift[:], in0=sh.mean[:], scalar=-1.0, in1=sh.rstd[:],
                                           op0=ALU.mult, op1=ALU.mult).then_inc(shift_ready, 1)
            dve.wait_ge(aff_ready, NT // 4)
            affv = aff[:, 0:NT * E].rearrange("p (t e) -> p t e", e=E)
            over_e = lambda x: x[:].rearrange("p (t o) -> p t o", o=1).to_broadcast([P, NT, E])
            nc.vector.tensor_reduce(sh.mx[:], affv, axis=AX.X, op=ALU.max).then_inc(mx_ready, 1)
            dve.wait_ge(mx_ready, 1)
            link(nc.vector.tensor_tensor(eq[:], affv, over_e(sh.mx), ALU.is_equal))
            link(nc.vector.tensor_tensor(cand[:], eq[:], sh.em8[:].rearrange("p (o e) -> p o e", o=1)
                                         .to_broadcast([P, NT, E]), ALU.mult))
            link(nc.vector.tensor_reduce(cmin[:], cand[:], axis=AX.X, op=ALU.min))
            nc.vector.tensor_tensor(onehot[:], cand[:], over_e(cmin), ALU.is_equal).then_inc(onehot_ready, 1)
            dve.wait_ge(exp_ready, 1)
            link(nc.vector.tensor_scalar_add(ex[:], sh.alpha[:], 1.0))
            link(nc.vector.reciprocal(sh.alpha[:], ex[:]))
            dve.wait_ge(rank_ready, 1)
            link(nc.vector.tensor_copy(tot[:].rearrange("p e t -> p t e"),
                                       cnt[:, NT * E:2 * NT * E].rearrange("p (t e) -> p t e", e=E)))
            link(nc.vector.tensor_tensor_scan(cum[:].rearrange("p e t -> p (e t)"),
                                              sh.keep[:].rearrange("p e t -> p (e t)"),
                                              tot[:].rearrange("p e t -> p (e t)"), 0.0, ALU.mult, ALU.add))
            link(nc.vector.tensor_tensor(before_tile[:], cum[:], tot[:], ALU.subtract))
            link(nc.vector.tensor_tensor(gt[:], cum[:, :, NT - 1:NT].to_broadcast([P, E, NT]),
                                         sh.thr[:].rearrange("p (o t) -> p o t", o=1).to_broadcast([P, E, NT]),
                                         ALU.is_gt))
            link(nc.vector.tensor_reduce(ntiles[:], gt[:], axis=AX.X, op=ALU.add))
            link(nc.vector.tensor_tensor_scan(upto[:], sh.ones8[:], ntiles[:], 0.0, ALU.mult, ALU.add))
            link(nc.vector.tensor_tensor(base[:], upto[:], ntiles[:], ALU.subtract))
            link(nc.vector.tensor_scalar(base[:], base[:], float(P), None, ALU.mult))
            link(nc.vector.tensor_tensor(t1[:], cnt[:, 0:NT * E].rearrange("p (t e) -> p t e", e=E),
                                         before_tile[:].rearrange("p e t -> p t e"), ALU.add))
            link(nc.vector.tensor_tensor(t1[:], t1[:], base[:].rearrange("p (o e) -> p o e", o=1)
                                         .to_broadcast([P, NT, E]), ALU.add))
            link(nc.vector.tensor_tensor(t1[:], t1[:], onehot[:], ALU.mult))
            link(nc.vector.tensor_reduce(cmin[:], t1[:], axis=AX.X, op=ALU.add))
            link(nc.vector.tensor_tensor(ge[:], sh.slot_id[:], upto[:, 0:E - 1].rearrange("p (o e) -> p o e", o=1)
                                         .to_broadcast([P, SLOTS, E - 1]), ALU.is_ge))
            link(nc.vector.tensor_reduce(slot_e[:], ge[:], axis=AX.X, op=ALU.add))
            link(nc.vector.tensor_copy(sh.slot_expert[:], slot_e[:]))
            link(nc.vector.tensor_copy(place[:], cmin[:]))
            link(nc.vector.tensor_single_scalar(lo_i[:], place[:], P - 1, ALU.bitwise_and))
            link(nc.vector.tensor_single_scalar(hi_i[:], place[:], 7, ALU.arith_shift_right))
            link(nc.vector.tensor_copy(lo[:], lo_i[:]))
            link(nc.vector.tensor_copy(hi[:], hi_i[:]))
            nc.vector.tensor_tensor(at_lo[:], sh.row128[:].rearrange("p (o n) -> p o n", o=1)
                                    .to_broadcast([P, NT, P]),
                                    lo[:].rearrange("p (t o) -> p t o", o=1).to_broadcast([P, NT, P]),
                                    ALU.is_equal).then_inc(place_ready, 1)
            link(nc.vector.tensor_tensor(at_hi[:, :, 0, :], sh.row_slots[:].rearrange("p (o n) -> p o n", o=1)
                                         .to_broadcast([P, NT, SLOTS]),
                                         hi[:].rearrange("p (t o) -> p t o", o=1).to_broadcast([P, NT, SLOTS]),
                                         ALU.is_equal))
            nc.vector.tensor_tensor(at_hi[:, :, 1, :], at_hi[:, :, 0, :],
                                    sh.tile_id[:].rearrange("p (t o) -> p t o", o=1)
                                    .to_broadcast([P, NT, SLOTS]), ALU.mult).then_inc(place_ready, 1)
            nc.vector.tensor_scalar(at_hi[:, :, 2, :], at_hi[:, :, 0, :], sh.part_id[:], None,
                                    ALU.mult).then_inc(place_ready, 1)
            dve.wait_ge(inverse_ready, 1)
            link(nc.vector.tensor_copy(inv[:], invp[:, 0:3 * SLOTS]))
            link(nc.vector.scalar_tensor_tensor(out=row[:], in0=inv[:, SLOTS:2 * SLOTS], scalar=float(P),
                                                in1=inv[:, 2 * SLOTS:3 * SLOTS], op0=ALU.mult, op1=ALU.add))
            link(nc.vector.tensor_tensor(tr[:], inv[:, 0:SLOTS], sh.trash[:], ALU.mult))
            link(nc.vector.tensor_tensor(tr[:], sh.trash[:], tr[:], ALU.subtract))
            link(nc.vector.tensor_copy(sh.gather_row[:], row[:]))
            link(nc.vector.tensor_tensor(sh.scatter_row[:], row[:], tr[:], ALU.add))

        @blk.gpsimd
        def _(pool):
            for n in range(2):
                pool.wait_ge(var_ready, n + 1)
                nc.gpsimd.tensor_tensor(sh.rstd[:], sh.tmp_b[:], sh.neg_half[:], ALU.pow).then_inc(rstd_ready, 1)

        @blk.scalar
        def _(act):
            with act.Fori(0, NT // 8) as g:
                for k in range(2):
                    act.wait_ge(yT_ps, g * 2 + k + 1)
                    nc.scalar.activation(yT[k][:], psT[k][:], ACT.Copy).then_inc(yT_ready, 1)
            act.wait_ge(shift_ready, 1)
            with act.Fori(0, NT // 4) as g:
                for k in range(4):
                    t = g * 4
                    ins = nc.scalar.activation(sh.xn[:, bass.ds(t + k, 1), :].rearrange("p o d -> p (o d)"),
                                               sh.y[:, bass.ds(t + k, 1), :].rearrange("p o d -> p (o d)"),
                                               ACT.Identity, bias=sh.shift[:, bass.ds(t + k, 1)],
                                               scale=sh.rstd[:, bass.ds(t + k, 1)])
                ins.then_inc(xn_ready, 1)
            act.wait_ge(mx_ready, 1)
            nc.scalar.activation(sh.alpha[:], sh.mx[:], ACT.Exp, scale=-1.0).then_inc(exp_ready, 1)

        @blk.sync
        def _(sp):
            dst = sh.xn_dram.rearrange("(t p) d -> p t d", p=P)
            with sp.Fori(0, NT // 4) as g:
                sp.wait_ge(xn_ready, g + 1)
                sp.dma_start(dst[:, bass.ds(g * 4, 4), :], sh.xn[:, bass.ds(g * 4, 4), :]).then_inc(xn_stored, 16)
            sp.wait_ge(xn_stored, 16 * (NT // 4))

        @blk.tensor
        def _(pe):
            for g in range(0, NT // 4, 2):
                for k in range(2):
                    pe.wait_ge(y_ready, g + k + 1)
                    for j in range(4):
                        ins = nc.tensor.transpose(psT[k][:, j * P:(j + 1) * P], sh.y[:, (g + k) * 4 + j, :],
                                                  sh.ident[:])
                    ins.then_inc(yT_ps, 1)
                for k in range(2):
                    pe.wait_ge(yT_ready, g + k + 1)
                    for j in range(4):
                        at = ((g + k) * 4 + j) * E
                        ins = nc.tensor.matmul(aff[:, at:at + E], yT[k][:, j * P:(j + 1) * P], sh.cgbT[:, 0:E],
                                               start=True, stop=True)
                    ins.then_inc(aff_ready, 1)
            pe.wait_ge(onehot_ready, 1)
            flat = onehot[:].rearrange("p t e -> p (t e)")
            nc.tensor.matmul(cnt[:, 0:NT * E], sh.before[:], flat, start=True, stop=True)
            nc.tensor.matmul(cnt[:, NT * E:2 * NT * E], sh.onesb[:], flat, start=True, stop=True) \
              .then_inc(rank_ready, 1)
            pe.wait_ge(place_ready, 3)
            for t in range(NT):
                ins = nc.tensor.matmul(invp[:, 0:3 * SLOTS], at_lo[:, t, :],
                                       at_hi[:, t, :, :].rearrange("p a s -> p (a s)"),
                                       start=(t == 0), stop=(t == NT - 1))
            ins.then_inc(inverse_ready, 1)


def expert_phase(nc, sh, f):
    with ExitStack() as ctx:
        sem = lambda n: ctx.enter_context(nc.semaphore(f"e{f}_{n}"))
        sb = lambda n, s, d: ctx.enter_context(nc.sbuf_tensor(f"e{f}_{n}", s, d))
        NX = 4
        gathered = [sem(f"gathered{k}") for k in range(NX)]
        scattered = [sem(f"scattered{k}") for k in range(NX)]
        xT_ps, xT_ready = sem("xT_ps"), sem("xT_ready")
        h_ps, h_ready, hT_ps, hT_ready = sem("h_ps"), sem("h_ready"), sem("hT_ps"), sem("hT_ready")
        out_ps, out_ready = sem("out_ps"), sem("out_ready")
        xg = [sb(f"xg{k}", [P, D], F32) for k in range(NX)]
        yo = [sb(f"yo{k}", [P, D], F32) for k in range(NX)]
        xT = [sb(f"xT{k}", [P, P], F32) for k in range(2)]
        hid = [sb(f"hid{k}", [P, F], F32) for k in range(2)]
        hT = [sb(f"hT{k}", [P, F], F32) for k in range(2)]
        ps_x, ps_h, ps_t, ps_o = sh.bank[0:2], sh.bank[2:4], sh.bank[4:6], sh.bank[6:8]
        GROUPS = SLOTS // NX
        blk = ctx.enter_context(nc.Block())
        expert_of = lambda eng, i: eng.value_load(sh.slot_expert[0:1, bass.ds(i, 1)], min_val=0, max_val=E - 1)

        def in_groups(eng, group):
            group(0, True, False)
            with eng.Fori(1, GROUPS - 1) as m:
                group(m, False, False)
            group(GROUPS - 1, False, True)

        @blk.gpsimd
        def _(pool):
            def gather(i):
                nc.gpsimd.indirect_dma_start(xg[i % NX][:], None, sh.xn_dram,
                                             bass.IndirectOffsetOnAxis(ap=sh.gather_row[:, i:i + 1], axis=0)) \
                  .then_inc(gathered[i % NX], 16)
            for i in range(NX):
                gather(i)
            for i in range(SLOTS):
                if i + NX < SLOTS:
                    pool.wait_ge(xT_ps, i + 1)
                    gather(i + NX)
                pool.wait_ge(out_ready, i + 1)
                nc.gpsimd.indirect_dma_start(sh.ys_dram,
                                             bass.IndirectOffsetOnAxis(ap=sh.scatter_row[:, i:i + 1], axis=0),
                                             yo[i % NX][:], None).then_inc(scattered[i % NX], 16)
            for k in range(NX):
                pool.wait_ge(scattered[k], 16 * GROUPS)

        @blk.scalar
        def _(act):
            def group(m, first, last):
                for k in range(NX):
                    act.wait_ge(hT_ps, m * NX + k + 1)
                    nc.scalar.activation(hT[k % 2][:], ps_t[k % 2][:], ACT.Relu).then_inc(hT_ready, 1)
            with act.Fori(0, GROUPS) as m:
                group(m, False, False)

        @blk.vector
        def _(dve):
            def xT_of(slot, k, wait):
                e = expert_of(dve, slot)
                dve.wait_ge(xT_ps, wait)
                nc.vector.tensor_scalar(xT[k % 2][:], ps_x[k % 2][:, 0:P], sh.cgbT[:, bass.ds(e + E, 1)],
                                        sh.cgbT[:, bass.ds(e + 2 * E, 1)], ALU.mult, ALU.add).then_inc(xT_ready, 1)

            def out_of(slot, k, wait, free):
                e = expert_of(dve, slot)
                if free is not None:
                    dve.wait_ge(scattered[k], free)
                dve.wait_ge(out_ps, wait)
                nc.vector.tensor_tensor(yo[k][:], ps_o[k % 2][:, 0:D],
                                        sh.b2bc[:, bass.ds(e * D, D)], ALU.add).then_inc(out_ready, 1)

            def group(m, first, last):
                for k in range(NX):
                    e = expert_of(dve, m * NX + k)
                    dve.wait_ge(h_ps, m * NX + k + 1)
                    nc.vector.tensor_tensor(hid[k % 2][:], ps_h[k % 2][:], sh.b1bc[:, bass.ds(e * F, F)],
                                            ALU.add).then_inc(h_ready, 1)
                    if k:
                        out_of(m * NX + k - 1, k - 1, m * NX + k, None if first else m * 16)
                    elif not first:
                        out_of(m * NX - 1, NX - 1, m * NX, None if isinstance(m, int) and m == 1 else (m - 1) * 16)
                    if not (last and k == NX - 1):
                        xT_of(m * NX + k + 1, k + 1, m * NX + k + 2)
            xT_of(0, 0, 1)
            group(0, True, False)
            group(1, False, False)
            with dve.Fori(2, GROUPS - 1) as m:
                group(m, False, False)
            group(GROUPS - 1, False, True)
            out_of(SLOTS - 1, NX - 1, SLOTS, (GROUPS - 1) * 16)

        @blk.tensor
        def _(pe):
            def transpose_rows(k, wait, gathers):
                pe.wait_ge(gathered[k], gathers)
                nc.tensor.transpose(ps_x[k % 2][:, 0:P], xg[k][:], sh.ident[:]).then_inc(xT_ps, 1)

            def second_product(slot, k, n, free):
                e = expert_of(pe, slot)
                pe.wait_ge(hT_ready, n)
                if free is not None:
                    pe.wait_ge(out_ready, free)
                for c in range(FC):
                    ins = nc.tensor.matmul(ps_o[k % 2][:, 0:D], hT[k % 2][:, c * P:(c + 1) * P],
                                           sh.w2[:, bass.ds(e, 1), c, :].rearrange("p o d -> p (o d)"),
                                           start=(c == 0), stop=(c == FC - 1))
                ins.then_inc(out_ps, 1)

            def group(m, first, last):
                for k in range(NX):
                    e = expert_of(pe, m * NX + k)
                    pe.wait_ge(xT_ready, m * NX + k + 1)
                    nc.tensor.matmul(ps_h[k % 2][:], xT[k % 2][:],
                                     sh.w1[:, bass.ds(e, 1), :].rearrange("p o f -> p (o f)"),
                                     start=True, stop=True).then_inc(h_ps, 1)
                    if not (first and k == 0):
                        second_product(m * NX + k - 1, (k - 1) % NX, m * NX + k,
                                       None if first and k < 3 else m * NX + k - 2)
                    if not (last and k == NX - 1):
                        nxt = (k + 1) % NX
                        transpose_rows(nxt, None, (m + 1 + (k + 1) // NX) * 16)
                    pe.wait_ge(h_ready, m * NX + k + 1)
                    for c in range(FC):
                        ins = nc.tensor.transpose(ps_t[k % 2][:, c * P:(c + 1) * P],
                                                  hid[k % 2][:, c * P:(c + 1) * P], sh.ident[:])
                    ins.then_inc(hT_ps, 1)
            transpose_rows(0, None, 16)
            in_groups(pe, group)
            second_product(SLOTS - 1, NX - 1, SLOTS, SLOTS - 2)


def combine_phase(nc, sh, f, out=None):
    with ExitStack() as ctx:
        sem = lambda n: ctx.enter_context(nc.semaphore(f"c{f}_{n}"))
        back, mixed, x_ready, stored = [sem(f"back{g}") for g in range(NT // 4)], sem("mixed"), sem("x_ready"), sem("stored")
        blk = ctx.enter_context(nc.Block())

        @blk.sync
        def _(sp):
            src = sh.ys_dram[0:N, :].rearrange("(t p) d -> p t d", p=P)
            for g in range(NT // 4):
                sp.dma_start(sh.xn[:, 4 * g:4 * g + 4, :], src[:, 4 * g:4 * g + 4, :]).then_inc(back[g], 16)
            if out is not None:
                dst = out.rearrange("b (t p) d -> p (b t) d", p=P)
                for g in range(NT // 4):
                    sp.wait_ge(x_ready, g + 1)
                    sp.dma_start(dst[:, 4 * g:4 * g + 4, :], sh.x[:, 4 * g:4 * g + 4, :]).then_inc(stored, 16)
                sp.wait_ge(stored, 16 * (NT // 4))

        @blk.vector
        def _(dve):
            for g in range(NT // 4):
                dve.wait_ge(back[g], 16)
                for t in range(4 * g, 4 * g + 4):
                    ins = nc.vector.scalar_tensor_tensor(out=sh.y[:, t, :], in0=sh.xn[:, t, :],
                                                         scalar=sh.alpha[:, t:t + 1], in1=sh.y[:, t, :],
                                                         op0=ALU.mult, op1=ALU.add)
                ins.then_inc(mixed, 1)
                dve.wait_ge(mixed, g + 1)
                nc.vector.scalar_tensor_tensor(out=sh.x[:, 4 * g:4 * g + 4, :].rearrange("p t d -> p (t d)"),
                                               in0=sh.y[:, 4 * g:4 * g + 4, :].rearrange("p t d -> p (t d)"),
                                               scalar=0.5,
                                               in1=sh.x[:, 4 * g:4 * g + 4, :].rearrange("p t d -> p (t d)"),
                                               op0=ALU.mult, op1=ALU.add).then_inc(x_ready, 1)


def qkv_phase(nc, sh):
    with ExitStack() as ctx:
        sem = lambda n: ctx.enter_context(nc.semaphore("q_" + n))
        sb = lambda n, s, d: ctx.enter_context(nc.sbuf_tensor("q_" + n, s, d))
        dve_step, var_ready, rstd_ready, stats_done = sem("dve_step"), sem("var_ready"), sem("rstd_ready"), sem("stats_done")
        z_ready, zT_ps, zT_ready = sem("z_ready"), sem("zT_ps"), sem("zT_ready")
        qk_ps, v_ps, v_ready = sem("qk_ps"), sem("v_ps"), sem("v_ready")
        full_ready, first_ready = sem("full_ready"), sem("first_ready")
        rest_ready, parts_ready = sem("rest_ready"), sem("parts_ready")
        parts_stored = [sem(f"parts_stored{k}") for k in range(2)]
        zT = [sb(f"zT{k}", [P, 4 * P], F32) for k in range(2)]
        full = [sb(f"full{k}", [P, 4 * P], F32) for k in range(2)]
        rest = [sb(f"rest{k}", [P, 4 * P], F32) for k in range(2)]
        parts = [sb(f"parts{k}", [P, 3, 4 * P], BF16) for k in range(2)]
        ps_z, ps_qk, ps_v = sh.bank[0:2], sh.bank[2:4], sh.bank[4]
        G = NT // 4
        blk = ctx.enter_context(nc.Block())

        @blk.vector
        def _(dve):
            link = serial(dve, dve_step)
            norm_stats(nc, dve, sh, sh.x, NT, stats_done)
            dve.wait_ge(stats_done, NT // 4)
            norm_finish(nc, link, sh)
            nc.vector.tensor_scalar_add(sh.tmp_b[:], sh.tmp_b[:], EPS).then_inc(var_ready, 1)
            dve.wait_ge(rstd_ready, 1)
            norm_apply(nc, dve, link, sh, sh.x, sh.y, NT, z_ready)
            with dve.Fori(0, G) as g:
                for n in range(2):
                    if n == 1:
                        dve.wait_ge(v_ps, g + 1)
                        nc.vector.tensor_tensor(sh.v[:, bass.ds(g * 4, 4), :],
                                                ps_v[:].rearrange("p (t d) -> p t d", d=D),
                                                sh.bvbc[:].rearrange("p (o d) -> p o d", o=1)
                                                .to_broadcast([P, 4, D]), ALU.add).then_inc(v_ready, 1)
                    dve.wait_ge(full_ready, g * 2 + n + 1)
                    dve.wait_ge(first_ready, g * 2 + n + 1)
                    nc.vector.tensor_tensor(rest[n][:], full[n][:], parts[n][:, 0, :], ALU.subtract) \
                      .then_inc(rest_ready, 1)
                    dve.wait_ge(rest_ready, g * 4 + n * 2 + 1)
                    nc.vector.tensor_copy(parts[n][:, 1, :], rest[n][:]).then_inc(rest_ready, 1)
                    dve.wait_ge(rest_ready, g * 4 + n * 2 + 2)
                    nc.vector.tensor_tensor(parts[n][:, 2, :], rest[n][:], parts[n][:, 1, :], ALU.subtract) \
                      .then_inc(parts_ready, 1)

        @blk.gpsimd
        def _(pool):
            pool.wait_ge(var_ready, 1)
            nc.gpsimd.tensor_tensor(sh.rstd[:], sh.tmp_b[:], sh.neg_half[:], ALU.pow).then_inc(rstd_ready, 1)

        @blk.scalar
        def _(act):
            act.wait_ge(zT_ps, 1)
            nc.scalar.activation(zT[0][:], ps_z[0][:], ACT.Copy).then_inc(zT_ready, 1)

            def qk_read(g, n):
                act.wait_ge(qk_ps, g * 2 + n + 1)
                if g:
                    act.wait_ge(parts_ready, 2 * g + n - 1)
                nc.scalar.activation(full[n][:], ps_qk[n][:], ACT.Identity, bias=sh.bqk[:, n:n + 1]) \
                  .then_inc(full_ready, 1)
                if g:
                    act.wait_ge(parts_stored[n], 48 * g)
                nc.scalar.activation(parts[n][:, 0, :], ps_qk[n][:], ACT.Identity, bias=sh.bqk[:, n:n + 1]) \
                  .then_inc(first_ready, 1)
            for g in range(G):
                qk_read(g, 0)
                if g < G - 1:
                    act.wait_ge(zT_ps, g + 2)
                    nc.scalar.activation(zT[(g + 1) % 2][:], ps_z[(g + 1) % 2][:], ACT.Copy).then_inc(zT_ready, 1)
                qk_read(g, 1)

        @blk.sync
        def _(sp):
            for g in range(G):
                b, half = g // 2, g % 2
                for n in range(2):
                    sp.wait_ge(parts_ready, 2 * g + n + 1)
                    for part in range(3):
                        row = HD * (part if n == 0 else 2 - part)
                        sp.dma_start((sh.q_dram, sh.k_dram)[n][b, :, row:row + HD, half * QW:(half + 1) * QW],
                                     parts[n][:, part, :]).then_inc(parts_stored[n], 16)
            for n in range(2):
                sp.wait_ge(parts_stored[n], 48 * G)

        @blk.tensor
        def _(pe):
            def transposes(g):
                pe.wait_ge(z_ready, g + 1)
                for j in range(4):
                    ins = nc.tensor.transpose(ps_z[g % 2][:, j * P:(j + 1) * P], sh.y[:, 4 * g + j, :], sh.ident[:])
                ins.then_inc(zT_ps, 1)
            transposes(0)
            for g in range(G):
                pe.wait_ge(zT_ready, g + 1)
                for n, name in enumerate(("Wq", "Wk")):
                    if g:
                        pe.wait_ge(first_ready, 2 * g + n - 1)
                    nc.tensor.matmul(ps_qk[n][:], sh.w[name][:], zT[g % 2][:], start=True, stop=True) \
                      .then_inc(qk_ps, 1)
                    if n == 0 and g < G - 1:
                        transposes(g + 1)
                if g:
                    pe.wait_ge(v_ready, g)
                for j in range(4):
                    ins = nc.tensor.matmul(ps_v[:, j * D:(j + 1) * D], zT[g % 2][:, j * P:(j + 1) * P],
                                           sh.w["Wv"][:], start=True, stop=True)
                ins.then_inc(v_ps, 1)


def maximum_units(half):
    t0 = HT * half
    rows = []
    for par in range(2):
        pair = (par, par + 2)
        row = [[(h, t, 0, 4)] for h in pair for t in range(t0, t0 + HT) if half]
        row += [[(h, t0 + 2, t0, 2), (h, t0 + 3, t0, 2)] for h in pair]
        row += [[(h, t0 + i, t0 + i, 1) for i in range(HT)] for h in pair]
        row.append([(h, t0 + i + 1, t0 + i, 1) for h in pair for i in (0, 2)])
        rows.append(row)
    return [u for both in zip(*rows) for u in both]


def attention_phase(nc, sh):
    low, high = maximum_units(0), maximum_units(1)
    prologue_ring = [("S", u) for u in low + high]
    prologue_ring.insert(len(low) + 3, ("M", 0))
    step_ring = list(prologue_ring)
    step_ring.insert(3, ("M", 1))
    step_ring.insert(9, ("E", 0))
    step_ring.insert(14, ("E", 1))
    NPRO, NRING = len(prologue_ring), len(step_ring)
    assert NRING % 2 == 0
    segments = [[(0, 0, 512)], [(1, 128, 384), (3, 384, 128)], [(0, 512, 512)], [(2, 256, 256), (6, 768, 256)],
                [(1, 512, 512)], [(2, 512, 512)], [(3, 512, 512)], [(4, 512, 512)], [(5, 640, 384), (7, 896, 128)]]
    NU = len(segments)
    FIRST_HIGH, LAST_LOW = 2, 3
    share = [(NRING * u // NU, NRING * (u + 1) // NU) for u in range(NU)]

    with ExitStack() as ctx:
        sem = lambda n: ctx.enter_context(nc.semaphore("a_" + n))
        sb = lambda n, s, d: ctx.enter_context(nc.sbuf_tensor("a_" + n, s, d))
        op_loaded = [sem(f"op_loaded{g}") for g in range(NG)]
        neg_max_loaded = [sem(f"neg_max_loaded{h}") for h in range(2)]
        neg_max_stored = [sem(f"neg_max_stored{h}") for h in range(2)]
        ring_full, ring_empty = sem("ring_full"), sem("ring_empty")
        split_step, split_ready, neg_maxT_ready, rden_ready = sem("split_step"), sem("split_ready"), sem("neg_maxT_ready"), sem("rden_ready")
        scores_ready, probs_ready = sem("scores_ready"), sem("probs_ready")
        o_low_done, o_high_done, o_low_read, o_high_read = sem("o_low_done"), sem("o_high_done"), sem("o_low_read"), sem("o_high_read")
        v_aug_ready, bias_added, split_cleared = sem("v_aug_ready"), sem("bias_added"), sem("split_cleared")
        q_op = [sb(f"q_op{g}", [P, 2, T], BF16) for g in range(NG)]
        neg_max = sb("neg_max", [P, 2, GH, HT], F32)
        remain = sb("remain", [P, 2, GH, HT], F32)
        split = sb("split", [P, 2, P], BF16)
        split_view = split[:, :, 0:GH * MROWS * HT].rearrange("p a (h m t) -> p a h m t", h=GH, m=MROWS)
        neg_maxT = [sb(f"neg_maxT{h}", [GH * MROWS * HT, P], BF16) for h in range(2)]
        probs = [sb(f"probs{k}", [P, 2, 2, QW], F32) for k in range(2)]
        rden = [sb(f"rden{h}", [P, HT * GH], F32) for h in range(2)]
        k_op, v_aug = sh.k_op, sh.v_aug
        nm_dram = [nc.dram_tensor(f"neg_max_dram{h}", (GH, MROWS, HT * P), BF16, kind="Internal").ap()
                   for h in range(2)]
        ring_bank, scores, o_bank = sh.bank[0:2], sh.two_banks[1:3], sh.bank[6:8]
        blk = ctx.enter_context(nc.Block())
        ADDED = P // 4

        @blk.sync
        def _(sp):
            def load_ops(b, g):
                for par in range(2):
                    for src, dst, skip in ((sh.q_dram, q_op[g], 0), (sh.k_dram, k_op[g], HD)):
                        rows = src[bass.ds(b, 1), g * GH:(g + 1) * GH, :, :] \
                            .rearrange("o (s r) d t -> r d (o s) t", r=2)[par]
                        at = 64 * par
                        for n, first in ((3, 0), (2, skip), (1, 2 * skip)):
                            sp.dma_start(dst[at:at + n * HD, :, :], rows[first:first + n * HD]) \
                              .then_inc(op_loaded[g], 16)
                            at += n * HD

            def move_max(group, g, half):
                sp.wait_ge(neg_maxT_ready, group * 2 + half + 1)
                sp.dma_start(nm_dram[half].rearrange("h m (t q) -> (h m t) q", q=P), neg_maxT[half][:]) \
                  .then_inc(neg_max_stored[half], 16)
                sp.wait_ge(neg_max_stored[half], group * 16 + 16)
                for par in range(2):
                    at = 64 * par + TERMS
                    sp.dma_start(q_op[g][at:at + MROWS, :, half * QW:(half + 1) * QW],
                                 nm_dram[half].rearrange("(s r) m q -> r m s q", r=2)[par]) \
                      .then_inc(neg_max_loaded[half], 16)
            load_ops(0, 0)
            load_ops(0, 1)
            move_max(0, 0, 0)
            with sp.Fori(0, B) as b:
                for g in range(NG):
                    n = b * NG + g
                    move_max(n, g, 1)
                    if g < NG - 2:
                        load_ops(b, g + 2)
                    else:
                        load_ops((b + 1) % B, g - (NG - 2))
                    move_max(n + 1, (g + 1) % NG, 0)
            for g in range(NG):
                sp.wait_ge(op_loaded[g], 16 * 12 * (B + (g < 2)))
            sp.wait_ge(neg_max_loaded[0], 32 * (B * NG + 1))
            sp.wait_ge(neg_max_loaded[1], 32 * B * NG)

        @blk.gpsimd
        def _(pool):
            def augment(b, g):
                nc.gpsimd.tensor_copy(v_aug[g % 2][:, :, :, 0:HD],
                                      sh.v[:, bass.ds(b * TB, TB), g * GH * HD:(g + 1) * GH * HD]
                                      .rearrange("p t (h d) -> p t h d", d=HD)).then_inc(v_aug_ready, 1)
            augment(0, 0)
            augment(0, 1)
            nc.gpsimd.tensor_tensor(sh.x[:], sh.x[:], sh.bobc[:].rearrange("p (o d) -> p o d", o=1)
                                    .to_broadcast([P, NT, D]), ALU.add).then_inc(bias_added, 1)
            with pool.Fori(0, B) as b:
                for g in range(NG):
                    pool.wait_ge(o_high_done, b * NG + g + 1)
                    if g < NG - 2:
                        augment(b, g + 2)
                    else:
                        augment((b + 1) % B, g - (NG - 2))

        @blk.scalar
        def _(act):
            act.sem_inc(o_low_read, 1)
            act.sem_inc(o_high_read, 1)
            with act.Fori(0, B) as b:
                for g in range(NG):
                    n = b * NG + g
                    for u in range(NU):
                        for pair in range(2):
                            act.wait_ge(scores_ready, (n * NU + u) * 2 + pair + 1)
                            nc.scalar.activation(probs[(g * NU + u) % 2][:, pair, :, :].rearrange("p h q -> p (h q)"),
                                                 scores[pair], ACT.Exp, scale=SCALE).then_inc(probs_ready, 1)
                        if u == LAST_LOW + 2:
                            act.wait_ge(o_low_done, n + 1)
                            nc.scalar.activation(sh.o_sb[:, 0:QW], o_bank[0], ACT.Copy).then_inc(o_low_read, 1)
                    act.wait_ge(o_high_done, n + 1)
                    nc.scalar.activation(sh.o_sb[:, QW:T], o_bank[1], ACT.Copy).then_inc(o_high_read, 1)

        @blk.vector
        def _(dve):
            flat = sh.block_max[:].rearrange("p h t j -> p (h t j)")

            def places(unit):
                h, t, j, width = unit[0]
                if width == 4:
                    return sh.block_max[:, h, t, j:j + 4]
                if width == 2:
                    return sh.block_max[:, h, t:t + 2, j:j + 2]
                first = t * TB + j
                if unit[2][0] == h:
                    return flat[:, h * TB * TB + first:h * TB * TB + first + 3 * (TB + 1) + 1:TB + 1]
                both = flat.rearrange("p (s r x) -> p s r x", r=2, x=TB * TB)[:, :, h % 2, :]
                return both[:, :, first:first + 2 * (TB + 1) + 1:2 * (TB + 1)]

            def split_max(group, half):
                done = (group * 2 + half) * 4
                keys = HT * (half + 1)
                nm, rm = neg_max[:, half], remain[:, half]
                part = lambda i: split_view[:, half, :, i, :]
                nc.vector.tensor_reduce(nm, sh.block_max[:, :, HT * half:HT * half + HT, 0:keys], axis=AX.X,
                                        op=ALU.max, negate=True).then_inc(split_step, 1)
                dve.wait_ge(split_step, done + 1)
                nc.vector.tensor_copy(part(0), nm).then_inc(split_step, 1)
                dve.wait_ge(split_step, done + 2)
                nc.vector.tensor_tensor(rm, nm, part(0), ALU.subtract).then_inc(split_step, 1)
                dve.wait_ge(split_step, done + 3)
                nc.vector.tensor_copy(part(1), rm).then_inc(split_step, 1)
                dve.wait_ge(split_step, done + 4)
                nc.vector.tensor_tensor(part(2), rm, part(1), ALU.subtract).then_inc(split_ready, 1)

            def empty(kind, what, count, at, group, slot, cols, n):
                bank = ring_bank[at % 2]
                dve.wait_ge(ring_full, count + 1)
                if kind == "S":
                    nc.vector.tensor_reduce(places(what), bank.rearrange("p (a q) -> p a q", q=P), axis=AX.X,
                                            op=ALU.max).then_inc(ring_empty, 1)
                elif kind == "M":
                    nc.vector.tensor_copy(neg_maxT[what][:], bank.bitcast(BF16)[0:GH * MROWS * HT, 0:P]) \
                      .then_inc(neg_maxT_ready, 1)
                    dve.wait_ge(neg_maxT_ready, group * 2 + what + 1)
                    dve.sem_inc(ring_empty, 1)
                else:
                    heads = bank.rearrange("p (t h c) -> p t h c", h=GH, c=ADDED)
                    recip = rden[what][:].rearrange("p (t h) -> p t h", h=GH)
                    nc.vector.reciprocal(recip, heads[:, :, :, HD]).then_inc(rden_ready, 1)
                    dve.wait_ge(rden_ready, 2 * n + what + 1)
                    nc.vector.tensor_tensor(sh.att[:, bass.ds(slot * TB + what * HT, HT), cols:cols + GH * HD]
                                            .rearrange("p t (h d) -> p t h d", d=HD),
                                            heads[:, :, :, 0:HD],
                                            rden[what][:].rearrange("p (t h o) -> p t h o", h=GH, o=1)
                                            .to_broadcast([P, HT, GH, HD]), ALU.mult).then_inc(ring_empty, 1)

            def empty_all(entries, first, at, group, own, slot, cols, n):
                seen = 0
                for i, (kind, what) in enumerate(entries):
                    whose = own if (kind, what) == ("M", 1) else group
                    empty(kind, what, first + i, at + i, whose, slot, cols, n)
                    seen += kind == "S"
                    if kind == "S" and seen in (len(low), len(low) + len(high)):
                        dve.wait_ge(ring_empty, first + i + 1)
                        split_max(group, int(seen > len(low)))
            nc.vector.memset(split[:], 0.0).then_inc(split_cleared, 1)
            dve.wait_ge(split_cleared, 1)
            empty_all(prologue_ring, 0, 0, 0, None, 0, 0, 0)
            with dve.Fori(0, B) as b:
                for g in range(NG):
                    n = b * NG + g
                    slot, cols = (b + 1, (g - 1) * GH * HD) if g else (b + 0, (NG - 1) * GH * HD)
                    empty_all(step_ring, n * NRING + NPRO, NPRO, n + 1, n, slot, cols, n)
            for i in range(2):
                empty("E", i, NPRO + B * NG * NRING + i, NPRO + i, None, B, (NG - 1) * GH * HD, B * NG)

        @blk.tensor
        def _(pe):
            def fill(kind, what, count, at, group, g, loads, n):
                bank = ring_bank[at % 2]
                if not (isinstance(count, int) and count < 2):
                    pe.wait_ge(ring_empty, count - 1)
                if kind == "S":
                    pe.wait_ge(op_loaded[g], loads)
                    col = 0
                    diagonal = what[0][1] == what[0][2]
                    for i, (h, t, j, width) in enumerate(what):
                        rows = slice(64 * (h % 2), 64 * (h % 2) + TERMS)
                        ins = nc.tensor.matmul(bank[:, col:col + width * P], q_op[g][rows, h // 2, t * P:(t + 1) * P],
                                               k_op[g][rows, h // 2, j * P:(j + width) * P], start=(i == 0),
                                               stop=(i == len(what) - 1 and not diagonal))
                        col += width * P
                    if diagonal:
                        ins = nc.tensor.matmul(bank, sh.identb[:], sh.mask_qk[:].rearrange("p a q -> p (a q)"),
                                               start=False, stop=True)
                elif kind == "M":
                    pe.wait_ge(split_ready, group * 2 + what + 1)
                    ins = nc.tensor.transpose(bank.bitcast(BF16)[:, 0:P], split[:, what, :], sh.identb[:])
                else:
                    pe.wait_ge((o_low_read, o_high_read)[what], n + 1)
                    for j in range(HT):
                        ins = nc.tensor.transpose(bank[:, j * P:(j + 1) * P],
                                                  sh.o_sb[:, what * QW + j * P:what * QW + (j + 1) * P], sh.ident[:])
                ins.then_inc(ring_full, 1)

            def score_pair(n, g, u, pair):
                if u:
                    pe.wait_ge(probs_ready, (n * NU + u) * 2 + pair - 1)
                diagonal = [q0 == kt * P for kt, q0, width in segments[u]]
                for r in range(2):
                    rows = slice(64 * r, 64 * r + TERMS + MROWS)
                    col = r * QW
                    for i, (kt, q0, width) in enumerate(segments[u]):
                        ins = nc.tensor.matmul(scores[pair][:, col:col + width],
                                               k_op[g][rows, pair, kt * P:(kt + 1) * P],
                                               q_op[g][rows, pair, q0:q0 + width], start=(i == 0),
                                               stop=(i == len(segments[u]) - 1 and not any(diagonal)))
                        col += width
                for r in range(2):
                    col = r * QW
                    for i, (kt, q0, width) in enumerate(segments[u]):
                        if diagonal[i]:
                            ins = nc.tensor.matmul(scores[pair][:, col:col + P], sh.identb[:], sh.mask_kq[:],
                                                   start=False, stop=not any(diagonal[i + 1:]))
                        col += width
                ins.then_inc(scores_ready, 1)

            def products(n, g, u):
                pe.wait_ge(probs_ready, (n * NU + u) * 2 + 2)
                if u == 0:
                    pe.wait_ge(v_aug_ready, n + 1)
                    pe.wait_ge(o_low_read, n + 1)
                if u == FIRST_HIGH:
                    pe.wait_ge(o_high_read, n + 1)
                col = 0
                for kt, q0, width in segments[u]:
                    half = q0 // QW
                    last_kt = HT * (half + 1) - 1
                    at = q0 % QW
                    stop = (half == 0 and u == LAST_LOW) or (half == 1 and u == NU - 1 and kt == last_kt)
                    for h in range(GH):
                        ins = nc.tensor.matmul(o_bank[half][ADDED * h:ADDED * (h + 1), at:at + width],
                                               v_aug[g % 2][:, kt, h, :],
                                               probs[(g * NU + u) % 2][:, h // 2, h % 2, col:col + width],
                                               start=(kt == 0), stop=stop, tile_position=(0, ADDED * h))
                    col += width
                    if u == LAST_LOW and half == 0:
                        ins.then_inc(o_low_done, 1)
                if u == NU - 1:
                    ins.then_inc(o_high_done, 1)

            for i, (kind, what) in enumerate(prologue_ring):
                fill(kind, what, i, i, 0, 0, 16 * 12, 0)
            with pe.Fori(0, B) as b:
                for g in range(NG):
                    n = b * NG + g
                    loads = (b + 1 + (g == NG - 1)) * (16 * 12)
                    for u in range(NU):
                        if u == 0:
                            pe.wait_ge(neg_max_loaded[0], n * 32 + 32)
                        if u == FIRST_HIGH:
                            pe.wait_ge(neg_max_loaded[1], n * 32 + 32)
                        for pair in range(2):
                            score_pair(n, g, u, pair)
                        for i in range(*share[u]):
                            kind, what = step_ring[i]
                            own = (kind, what) == ("M", 1)
                            fill(kind, what, n * NRING + (NPRO + i), NPRO + i, n if own else n + 1, (g + 1) % NG,
                                 loads, n)
                        if u:
                            products(n, g, u - 1)
                    products(n, g, NU - 1)
            for i in range(2):
                fill("E", i, NPRO + B * NG * NRING + i, NPRO + i, None, None, None, B * NG)


def projection_phase(nc, sh):
    with ExitStack() as ctx:
        sem = lambda n: ctx.enter_context(nc.semaphore("p_" + n))
        attT_ps, attT_ready, proj_ps, x_ready = sem("attT_ps"), sem("attT_ready"), sem("proj_ps"), sem("x_ready")
        attT = [ctx.enter_context(nc.sbuf_tensor(f"p_attT{k}", [P, 4 * P], F32)) for k in range(2)]
        ps_t, ps_o = sh.bank[0:2], sh.bank[2:4]
        G = NT // 4
        blk = ctx.enter_context(nc.Block())

        @blk.tensor
        def _(pe):
            def transposes(g):
                for j in range(4):
                    ins = nc.tensor.transpose(ps_t[g % 2][:, j * P:(j + 1) * P], sh.att[:, TB + 4 * g + j, :],
                                              sh.ident[:])
                ins.then_inc(attT_ps, 1)
            transposes(0)
            for g in range(G):
                if g < G - 1:
                    transposes(g + 1)
                pe.wait_ge(attT_ready, g + 1)
                if g >= 2:
                    pe.wait_ge(x_ready, g - 1)
                for j in range(4):
                    ins = nc.tensor.matmul(ps_o[g % 2][:, j * D:(j + 1) * D], attT[g % 2][:, j * P:(j + 1) * P],
                                           sh.w["Wo"][:], start=True, stop=True)
                ins.then_inc(proj_ps, 1)

        @blk.scalar
        def _(act):
            for g in range(G):
                act.wait_ge(attT_ps, g + 1)
                nc.scalar.activation(attT[g % 2][:], ps_t[g % 2], ACT.Copy).then_inc(attT_ready, 1)

        @blk.vector
        def _(dve):
            for g in range(G):
                dve.wait_ge(proj_ps, g + 1)
                xg = sh.x[:, 4 * g:4 * g + 4, :].rearrange("p t d -> p (t d)")
                nc.vector.tensor_tensor(xg, ps_o[g % 2], xg, ALU.add).then_inc(x_ready, 1)


def build(nc, a, out):
    with ExitStack() as ctx:
        sh = Shared()
        sb = lambda n, s, d: ctx.enter_context(nc.sbuf_tensor(n, s, d))
        psum = ctx.enter_context(nc.psum_tensor("psum", [P, 8 * 512], F32))
        sh.bank = [psum[:, 512 * i:512 * (i + 1)] for i in range(8)]
        sh.two_banks = [psum[:, 1024 * i:1024 * (i + 1)] for i in range(4)]
        sh.act_loads = ctx.enter_context(nc.semaphore("act_loads"))
        sh.x, sh.y, sh.v = [sb(n, [P, NT, D], F32) for n in ("x_sb", "y_sb", "v_sb")]
        sh.att = sb("att_sb", [P, (B + 1) * TB, D], F32)
        sh.xn = sh.att[:, 0:NT, :]
        sh.w = {n: sb(n + "_sb", [D, D], F32) for n in ("Wq", "Wk", "Wv", "Wo")}
        sh.bqk, sh.bvbc, sh.bobc = sb("bqk", [P, 2], F32), sb("bv_bc", [P, D], F32), sb("bo_bc", [P, D], F32)
        sh.w1, sh.w2 = sb("w1_sb", [P, E, F], F32), sb("w2_sb", [P, E, FC, D], F32)
        sh.b1bc, sh.b2bc = sb("b1_bc", [P, E * F], F32), sb("b2_bc", [P, E * D], F32)
        sh.cgbT = sb("cgbT", [P, 3 * E], F32)
        sh.ident, sh.identb = sb("ident", [P, P], F32), sb("identb", [P, P], BF16)
        sh.before, sh.onesb = sb("before", [P, P], BF16), sb("onesb", [P, P], BF16)
        sh.mask_qk, sh.mask_kq = sb("mask_qk", [P, 4, P], BF16), sb("mask_kq", [P, P], BF16)
        sh.em8, sh.ones8 = sb("em8", [P, E], F32), sb("ones8", [P, E], F32)
        sh.thr, sh.tile_id, sh.neg_half = [sb(n, [P, NT], F32) for n in ("thr", "tile_id", "neg_half")]
        sh.slot_id = sb("slot_id", [P, SLOTS, E - 1], F32)
        sh.row128, sh.row_slots, sh.part_id = sb("row128", [P, P], F32), sb("row_slots", [P, SLOTS], F32), sb("part_id", [P, 1], F32)
        sh.trash, sh.keep = sb("trash", [P, SLOTS], F32), sb("keep", [P, E, NT], F32)
        sh.stats = sb("stats", [P, NT, 6], F32)
        sh.mean, sh.rstd, sh.shift, sh.tmp_a, sh.tmp_b, sh.mx, sh.alpha = [
            sb(n, [P, NT], F32) for n in ("mean", "rstd", "shift", "tmp_a", "tmp_b", "mx", "alpha")]
        sh.gather_row, sh.scatter_row = sb("gather_row", [P, SLOTS], I32), sb("scatter_row", [P, SLOTS], I32)
        sh.slot_expert = sb("slot_expert", [P, SLOTS], I32)
        sh.block_max = sb("block_max", [P, GH, TB, TB], F32)
        sh.k_op = [sb(f"k_op{g}", [P, 2, T], BF16) for g in range(NG)]
        sh.v_aug = [sb(f"v_aug{k}", [P, TB, GH, P // 4], F32) for k in range(2)]
        sh.o_sb = sb("o_sb", [P, T], F32)
        sh.q_dram, sh.k_dram = [nc.dram_tensor(n, (B, H, 3 * HD, T), BF16, kind="Internal").ap()
                                for n in ("q_dram", "k_dram")]
        sh.xn_dram = nc.dram_tensor("xn_dram", (N, D), F32, kind="Internal").ap()
        sh.ys_dram = nc.dram_tensor("ys_dram", (N + SLOTS * P, D), F32, kind="Internal").ap()
        setup_phase(nc, sh, a)
        route_phase(nc, sh, 0)
        expert_phase(nc, sh, 0)
        combine_phase(nc, sh, 0)
        qkv_phase(nc, sh)
        attention_phase(nc, sh)
        projection_phase(nc, sh)
        route_phase(nc, sh, 1)
        expert_phase(nc, sh, 1)
        combine_phase(nc, sh, 1, out)


_INS = {"x": "L0_attn_x", "Wq": "L0_attn_Wq", "bq": "L0_attn_bq", "Wk": "L0_attn_Wk", "bk": "L0_attn_bk",
        "Wv": "L0_attn_Wv", "bv": "L0_attn_bv", "Wo": "L0_attn_Wo", "bo": "L0_attn_bo",
        "centroids": "L0_ffn_centroids", "ln_g": "L0_ffn_ln_g", "ln_b": "L0_ffn_ln_b", "w1": "L0_ffn_w1",
        "b1": "L0_ffn_b1", "w2": "L0_ffn_w2", "b2": "L0_ffn_b2"}


def kernel(**inputs):
    import concourse.bacc as bacc
    from concourse.bass_utils import run_bass_kernel_spmd

    nc = bacc.Bacc("TRN2", target_bir_lowering=False, num_devices=1)
    arrays, args = {}, {}
    for short, name in _INS.items():
        arrays[f"in_{short}"] = np.ascontiguousarray(inputs[name])
        args[short] = nc.dram_tensor(f"in_{short}", arrays[f"in_{short}"].shape, F32, kind="ExternalInput").ap()
    out = nc.dram_tensor("out", (B, T, D), F32, kind="ExternalOutput").ap()
    build(nc, args, out)
    return run_bass_kernel_spmd(nc, [arrays], core_ids=[0]).results[0]["out"]
```

```python
import numpy as np
import concourse.bass as bass
from concourse import mybir
from concourse.alu_op_type import AluOpType as ALU
from contextlib import ExitStack

F32 = mybir.dt.float32
BF16 = mybir.dt.bfloat16
I32 = mybir.dt.int32
ACT = mybir.ActivationFunctionType
AX = mybir.AxisListType

B, T, D = 4, 1024, 128
H, HD = 16, 8
F, E = 512, 8
P = 128
N = B * T
NT = N // P
TB = T // P
FC = F // P
SLOTS = (N + E * (P - 1)) // P
SLOTS += SLOTS % 2
TRASH = N
EPS = 1e-5
BIG = -1.0e30
LOWEST = -3.0e38
GH = 4
NG = H // GH
TERMS = 6 * HD
MROWS = 3
SCALE = HD ** -0.5
QW = T // 2
HT = TB // 2


class Shared:
    pass


def serial(eng, sem):
    count = [0]

    def link(ins):
        count[0] += 1
        ins.then_inc(sem, 1)
        eng.wait_ge(sem, count[0])
    return link


def norm_finish(nc, link, sh):
    st = sh.stats
    link(nc.vector.tensor_tensor(sh.mean[:], st[:, :, 1], st[:, :, 4], ALU.add))
    link(nc.vector.tensor_tensor(sh.tmp_a[:], st[:, :, 1], st[:, :, 4], ALU.subtract))
    link(nc.vector.tensor_tensor(sh.tmp_b[:], st[:, :, 2], st[:, :, 5], ALU.add))
    link(nc.vector.tensor_scalar(sh.mean[:], sh.mean[:], 0.5, None, ALU.mult))
    link(nc.vector.scalar_tensor_tensor(out=sh.tmp_a[:], in0=sh.tmp_a[:], scalar=0.25, in1=sh.tmp_a[:],
                                        op0=ALU.mult, op1=ALU.mult))
    link(nc.vector.scalar_tensor_tensor(out=sh.tmp_b[:], in0=sh.tmp_b[:], scalar=1.0 / D, in1=sh.tmp_a[:],
                                        op0=ALU.mult, op1=ALU.add))


def setup_phase(nc, sh, a):
    with ExitStack() as ctx:
        sem = lambda n: ctx.enter_context(nc.semaphore(n))
        loads, cgb_in = sem("su_loads"), sem("su_cgb")
        pool_step, consts, dve_step = sem("su_pool_step"), sem("su_consts"), sem("su_dve_step")
        cgb_ps, dve_fill = sem("su_cgb_ps"), sem("su_dve_fill")
        cgb = ctx.enter_context(nc.sbuf_tensor("su_cgb_rows", [3 * E, D], F32))
        blk = ctx.enter_context(nc.Block())

        @blk.sync
        def _(sp):
            sp.dma_start(cgb[0:E, :], a["centroids"]).then_inc(cgb_in, 16)
            sp.dma_start(cgb[E:2 * E, :], a["ln_g"]).then_inc(cgb_in, 16)
            sp.dma_start(cgb[2 * E:3 * E, :], a["ln_b"]).then_inc(cgb_in, 16)
            sp.dma_start(sh.x[:], a["x"].rearrange("b (t p) d -> p (b t) d", p=P)).then_inc(loads, 16)
            for name in ("Wq", "Wk", "Wv", "Wo"):
                sp.dma_start(sh.w[name][:], a[name]).then_inc(loads, 16)
            sp.dma_start(sh.bqk[:, 0:1], a["bq"].rearrange("(p o) -> p o", o=1)).then_inc(loads, 16)
            sp.dma_start(sh.bqk[:, 1:2], a["bk"].rearrange("(p o) -> p o", o=1)).then_inc(loads, 16)
            sp.wait_ge(loads, 16 * 7)

        @blk.scalar
        def _(act):
            act.dma_start(sh.w1[:], a["w1"].rearrange("e d f -> d e f")).then_inc(sh.act_loads, 16)
            act.dma_start(sh.w2[:], a["w2"].rearrange("e (c p) d -> p e c d", p=P)).then_inc(sh.act_loads, 16)
            act.dma_start(sh.b1bc[:], a["b1"].rearrange("e f -> (e f)").rearrange("(o n) -> o n", o=1)
                          .to_broadcast([P, E * F])).then_inc(sh.act_loads, 16)
            act.dma_start(sh.b2bc[:], a["b2"].rearrange("e f -> (e f)").rearrange("(o n) -> o n", o=1)
                          .to_broadcast([P, E * D])).then_inc(sh.act_loads, 16)
            act.dma_start(sh.bvbc[:], a["bv"].rearrange("(o n) -> o n", o=1).to_broadcast([P, D])) \
               .then_inc(sh.act_loads, 16)
            act.dma_start(sh.bobc[:], a["bo"].rearrange("(o n) -> o n", o=1).to_broadcast([P, D])) \
               .then_inc(sh.act_loads, 16)
            act.wait_ge(sh.act_loads, 16 * 6)

        @blk.gpsimd
        def _(pool):
            link = serial(pool, pool_step)
            sel = nc.gpsimd.affine_select
            link(nc.gpsimd.memset(sh.ident[:], 0.0))
            link(sel(out=sh.ident[:], in_=sh.ident[:], compare_op=ALU.not_equal, fill=1.0, base=0,
                     pattern=[[-1, P]], channel_multiplier=1))
            nc.gpsimd.tensor_copy(sh.identb[:], sh.ident[:]).then_inc(consts, 1)
            link(nc.gpsimd.memset(sh.before[:], 1.0))
            sel(out=sh.before[:], in_=sh.before[:], compare_op=ALU.is_gt, fill=0.0, base=0,
                pattern=[[1, P]], channel_multiplier=-1).then_inc(consts, 1)
            link(nc.gpsimd.memset(sh.mask_qk[:], 0.0))
            sel(out=sh.mask_qk[:], in_=sh.mask_qk[:], compare_op=ALU.is_ge, fill=BIG, base=0,
                pattern=[[0, 4], [-1, P]], channel_multiplier=1).then_inc(consts, 1)
            link(nc.gpsimd.memset(sh.mask_kq[:], 0.0))
            sel(out=sh.mask_kq[:], in_=sh.mask_kq[:], compare_op=ALU.is_ge, fill=BIG, base=0,
                pattern=[[1, P]], channel_multiplier=-1).then_inc(consts, 1)
            iota = lambda out, pattern, base, cm: nc.gpsimd.iota(
                out, pattern, base=base, channel_multiplier=cm, allow_small_or_imprecise_dtypes=True)
            iota(sh.em8[:], [[1, E]], -E, 0).then_inc(consts, 1)
            iota(sh.thr[:], [[P, NT]], 0, 0).then_inc(consts, 1)
            iota(sh.slot_id[:], [[1, SLOTS], [0, E - 1]], 0, 0).then_inc(consts, 1)
            iota(sh.row128[:], [[1, P]], 0, 0).then_inc(consts, 1)
            iota(sh.row_slots[:], [[1, SLOTS]], 0, 0).then_inc(consts, 1)
            iota(sh.tile_id[:], [[1, NT]], 0, 0).then_inc(consts, 1)
            iota(sh.part_id[:], [[0, 1]], 0, 1).then_inc(consts, 1)
            iota(sh.trash[:], [[P, SLOTS]], TRASH, 1).then_inc(consts, 1)
            pool.wait_ge(consts, 12)

        @blk.vector
        def _(dve):
            nc.vector.memset(sh.onesb[:], 1.0).then_inc(dve_fill, 1)
            nc.vector.memset(sh.neg_half[:], -0.5).then_inc(dve_fill, 1)
            nc.vector.memset(sh.ones8[:], 1.0).then_inc(dve_fill, 1)
            link = serial(dve, dve_step)
            link(nc.vector.memset(sh.keep[:], 1.0))
            nc.vector.memset(sh.keep[:, :, 0:1], 0.0).then_inc(dve_fill, 1)
            nc.vector.memset(sh.block_max[:], LOWEST).then_inc(dve_fill, 1)
            nc.vector.memset(sh.o_sb[:], 1.0).then_inc(dve_fill, 1)
            for g in range(len(sh.k_op)):
                nc.vector.memset(sh.k_op[g][:], 1.0).then_inc(dve_fill, 1)
            for v in sh.v_aug:
                link(nc.vector.memset(v[:], 0.0))
                nc.vector.memset(v[:, :, :, HD:HD + 1], 1.0).then_inc(dve_fill, 1)
            dve.wait_ge(dve_fill, 6 + len(sh.k_op) + len(sh.v_aug))
            dve.wait_ge(cgb_ps, 1)
            link(nc.vector.tensor_copy(sh.cgbT[:], sh.bank[0][:, 0:3 * E]))

        @blk.tensor
        def _(pe):
            pe.wait_ge(consts, 12)
            pe.wait_ge(cgb_in, 48)
            nc.tensor.transpose(sh.bank[0][:, 0:3 * E], cgb[:], sh.ident[0:3 * E, 0:3 * E]).then_inc(cgb_ps, 1)


def norm_apply(nc, dve, link, sh, src, dst, tiles, ready):
    with dve.Fori(0, tiles // 4) as g:
        for k in range(4):
            t = g * 4
            ins = nc.vector.tensor_scalar(dst[:, bass.ds(t + k, 1), :].rearrange("p o d -> p (o d)"),
                                          src[:, bass.ds(t + k, 1), :].rearrange("p o d -> p (o d)"),
                                          sh.mean[:, bass.ds(t + k, 1)], sh.rstd[:, bass.ds(t + k, 1)],
                                          ALU.subtract, ALU.mult)
        ins.then_inc(ready, 1)


def norm_stats(nc, dve, sh, src, tiles, done):
    with dve.Fori(0, tiles // 4) as g:
        for k in range(4):
            t = g * 4
            ins = nc.vector.bn_stats(sh.stats[:, bass.ds(t + k, 1), :].rearrange("p o d -> p (o d)"),
                                     src[:, bass.ds(t + k, 1), :].rearrange("p o d -> p (o d)"))
        ins.then_inc(done, 1)


def route_phase(nc, sh, f):
    with ExitStack() as ctx:
        sem = lambda n: ctx.enter_context(nc.semaphore(f"r{f}_{n}"))
        sb = lambda n, s, d: ctx.enter_context(nc.sbuf_tensor(f"r{f}_{n}", s, d))
        dve_step, var_ready, rstd_ready = sem("dve_step"), sem("var_ready"), sem("rstd_ready")
        stats_done, y_ready, xn_ready, xn_stored = sem("stats_done"), sem("y_ready"), sem("xn_ready"), sem("xn_stored")
        yT_ps, yT_ready, aff_ready = sem("yT_ps"), sem("yT_ready"), sem("aff_ready")
        shift_ready = sem("shift_ready")
        mx_ready, exp_ready, onehot_ready, rank_ready = sem("mx_ready"), sem("exp_ready"), sem("onehot_ready"), sem("rank_ready")
        place_ready, inverse_ready = sem("place_ready"), sem("inverse_ready")
        yT = [sb(f"yT{i}", [P, 4 * P], F32) for i in range(2)]
        wide = lambda n, d=F32: sb(n, [P, NT, E], d)
        eq, cand, t1 = wide("eq"), wide("cand"), wide("t1")
        onehot = wide("onehot", BF16)
        tot, cum, before_tile, gt = [sb(n, [P, E, NT], F32) for n in ("tot", "cum", "before_tile", "gt")]
        cmin, lo, hi, ex = [sb(n, [P, NT], F32) for n in ("cmin", "lo", "hi", "ex")]
        ntiles, upto, base = [sb(n, [P, E], F32) for n in ("ntiles", "upto", "base")]
        place, lo_i, hi_i = [sb(n, [P, NT], I32) for n in ("place", "lo_i", "hi_i")]
        ge = sb("ge", [P, SLOTS, E - 1], F32)
        slot_e = sb("slot_e", [P, SLOTS], F32)
        at_lo = sb("at_lo", [P, NT, P], BF16)
        at_hi = sb("at_hi", [P, NT, 3, SLOTS], BF16)
        inv = sb("inv", [P, 3 * SLOTS], F32)
        tr, row = sb("tr", [P, SLOTS], F32), sb("row", [P, SLOTS], F32)
        psT, aff, cnt, invp = [sh.bank[0], sh.bank[1]], sh.bank[2], sh.bank[3], sh.bank[4]
        blk = ctx.enter_context(nc.Block())

        @blk.vector
        def _(dve):
            link = serial(dve, dve_step)
            norm_stats(nc, dve, sh, sh.x, NT, stats_done)
            dve.wait_ge(stats_done, NT // 4)
            norm_finish(nc, link, sh)
            nc.vector.tensor_scalar_add(sh.tmp_b[:], sh.tmp_b[:], EPS).then_inc(var_ready, 1)
            dve.wait_ge(rstd_ready, 1)
            norm_apply(nc, dve, link, sh, sh.x, sh.y, NT, y_ready)
            dve.wait_ge(y_ready, NT // 4)
            norm_stats(nc, dve, sh, sh.y, NT, stats_done)
            dve.wait_ge(stats_done, 2 * (NT // 4))
            norm_finish(nc, link, sh)
            nc.vector.tensor_scalar_add(sh.tmp_b[:], sh.tmp_b[:], EPS).then_inc(var_ready, 1)
            dve.wait_ge(rstd_ready, 2)
            nc.vector.scalar_tensor_tensor(out=sh.shift[:], in0=sh.mean[:], scalar=-1.0, in1=sh.rstd[:],
                                           op0=ALU.mult, op1=ALU.mult).then_inc(shift_ready, 1)
            dve.wait_ge(aff_ready, NT // 4)
            affv = aff[:, 0:NT * E].rearrange("p (t e) -> p t e", e=E)
            over_e = lambda x: x[:].rearrange("p (t o) -> p t o", o=1).to_broadcast([P, NT, E])
            nc.vector.tensor_reduce(sh.mx[:], affv, axis=AX.X, op=ALU.max).then_inc(mx_ready, 1)
            dve.wait_ge(mx_ready, 1)
            link(nc.vector.tensor_tensor(eq[:], affv, over_e(sh.mx), ALU.is_equal))
            link(nc.vector.tensor_tensor(cand[:], eq[:], sh.em8[:].rearrange("p (o e) -> p o e", o=1)
                                         .to_broadcast([P, NT, E]), ALU.mult))
            link(nc.vector.tensor_reduce(cmin[:], cand[:], axis=AX.X, op=ALU.min))
            nc.vector.tensor_tensor(onehot[:], cand[:], over_e(cmin), ALU.is_equal).then_inc(onehot_ready, 1)
            dve.wait_ge(exp_ready, 1)
            link(nc.vector.tensor_scalar_add(ex[:], sh.alpha[:], 1.0))
            link(nc.vector.reciprocal(sh.alpha[:], ex[:]))
            dve.wait_ge(rank_ready, 1)
            link(nc.vector.tensor_copy(tot[:].rearrange("p e t -> p t e"),
                                       cnt[:, NT * E:2 * NT * E].rearrange("p (t e) -> p t e", e=E)))
            link(nc.vector.tensor_tensor_scan(cum[:].rearrange("p e t -> p (e t)"),
                                              sh.keep[:].rearrange("p e t -> p (e t)"),
                                              tot[:].rearrange("p e t -> p (e t)"), 0.0, ALU.mult, ALU.add))
            link(nc.vector.tensor_tensor(before_tile[:], cum[:], tot[:], ALU.subtract))
            link(nc.vector.tensor_tensor(gt[:], cum[:, :, NT - 1:NT].to_broadcast([P, E, NT]),
                                         sh.thr[:].rearrange("p (o t) -> p o t", o=1).to_broadcast([P, E, NT]),
                                         ALU.is_gt))
            link(nc.vector.tensor_reduce(ntiles[:], gt[:], axis=AX.X, op=ALU.add))
            link(nc.vector.tensor_tensor_scan(upto[:], sh.ones8[:], ntiles[:], 0.0, ALU.mult, ALU.add))
            link(nc.vector.tensor_tensor(base[:], upto[:], ntiles[:], ALU.subtract))
            link(nc.vector.tensor_scalar(base[:], base[:], float(P), None, ALU.mult))
            link(nc.vector.tensor_tensor(t1[:], cnt[:, 0:NT * E].rearrange("p (t e) -> p t e", e=E),
                                         before_tile[:].rearrange("p e t -> p t e"), ALU.add))
            link(nc.vector.tensor_tensor(t1[:], t1[:], base[:].rearrange("p (o e) -> p o e", o=1)
                                         .to_broadcast([P, NT, E]), ALU.add))
            link(nc.vector.tensor_tensor(t1[:], t1[:], onehot[:], ALU.mult))
            link(nc.vector.tensor_reduce(cmin[:], t1[:], axis=AX.X, op=ALU.add))
            link(nc.vector.tensor_tensor(ge[:], sh.slot_id[:], upto[:, 0:E - 1].rearrange("p (o e) -> p o e", o=1)
                                         .to_broadcast([P, SLOTS, E - 1]), ALU.is_ge))
            link(nc.vector.tensor_reduce(slot_e[:], ge[:], axis=AX.X, op=ALU.add))
            link(nc.vector.tensor_copy(sh.slot_expert[:], slot_e[:]))
            link(nc.vector.tensor_copy(place[:], cmin[:]))
            link(nc.vector.tensor_single_scalar(lo_i[:], place[:], P - 1, ALU.bitwise_and))
            link(nc.vector.tensor_single_scalar(hi_i[:], place[:], 7, ALU.arith_shift_right))
            link(nc.vector.tensor_copy(lo[:], lo_i[:]))
            link(nc.vector.tensor_copy(hi[:], hi_i[:]))
            nc.vector.tensor_tensor(at_lo[:], sh.row128[:].rearrange("p (o n) -> p o n", o=1)
                                    .to_broadcast([P, NT, P]),
                                    lo[:].rearrange("p (t o) -> p t o", o=1).to_broadcast([P, NT, P]),
                                    ALU.is_equal).then_inc(place_ready, 1)
            link(nc.vector.tensor_tensor(at_hi[:, :, 0, :], sh.row_slots[:].rearrange("p (o n) -> p o n", o=1)
                                         .to_broadcast([P, NT, SLOTS]),
                                         hi[:].rearrange("p (t o) -> p t o", o=1).to_broadcast([P, NT, SLOTS]),
                                         ALU.is_equal))
            nc.vector.tensor_tensor(at_hi[:, :, 1, :], at_hi[:, :, 0, :],
                                    sh.tile_id[:].rearrange("p (t o) -> p t o", o=1)
                                    .to_broadcast([P, NT, SLOTS]), ALU.mult).then_inc(place_ready, 1)
            nc.vector.tensor_scalar(at_hi[:, :, 2, :], at_hi[:, :, 0, :], sh.part_id[:], None,
                                    ALU.mult).then_inc(place_ready, 1)
            dve.wait_ge(inverse_ready, 1)
            link(nc.vector.tensor_copy(inv[:], invp[:, 0:3 * SLOTS]))
            link(nc.vector.scalar_tensor_tensor(out=row[:], in0=inv[:, SLOTS:2 * SLOTS], scalar=float(P),
                                                in1=inv[:, 2 * SLOTS:3 * SLOTS], op0=ALU.mult, op1=ALU.add))
            link(nc.vector.tensor_tensor(tr[:], inv[:, 0:SLOTS], sh.trash[:], ALU.mult))
            link(nc.vector.tensor_tensor(tr[:], sh.trash[:], tr[:], ALU.subtract))
            link(nc.vector.tensor_copy(sh.gather_row[:], row[:]))
            link(nc.vector.tensor_tensor(sh.scatter_row[:], row[:], tr[:], ALU.add))

        @blk.gpsimd
        def _(pool):
            for n in range(2):
                pool.wait_ge(var_ready, n + 1)
                nc.gpsimd.tensor_tensor(sh.rstd[:], sh.tmp_b[:], sh.neg_half[:], ALU.pow).then_inc(rstd_ready, 1)

        @blk.scalar
        def _(act):
            with act.Fori(0, NT // 8) as g:
                for k in range(2):
                    act.wait_ge(yT_ps, g * 2 + k + 1)
                    nc.scalar.activation(yT[k][:], psT[k][:], ACT.Copy).then_inc(yT_ready, 1)
            act.wait_ge(shift_ready, 1)
            with act.Fori(0, NT // 4) as g:
                for k in range(4):
                    t = g * 4
                    ins = nc.scalar.activation(sh.xn[:, bass.ds(t + k, 1), :].rearrange("p o d -> p (o d)"),
                                               sh.y[:, bass.ds(t + k, 1), :].rearrange("p o d -> p (o d)"),
                                               ACT.Identity, bias=sh.shift[:, bass.ds(t + k, 1)],
                                               scale=sh.rstd[:, bass.ds(t + k, 1)])
                ins.then_inc(xn_ready, 1)
            act.wait_ge(mx_ready, 1)
            nc.scalar.activation(sh.alpha[:], sh.mx[:], ACT.Exp, scale=-1.0).then_inc(exp_ready, 1)

        @blk.sync
        def _(sp):
            dst = sh.xn_dram.rearrange("(t p) d -> p t d", p=P)
            with sp.Fori(0, NT // 4) as g:
                sp.wait_ge(xn_ready, g + 1)
                sp.dma_start(dst[:, bass.ds(g * 4, 4), :], sh.xn[:, bass.ds(g * 4, 4), :]).then_inc(xn_stored, 16)
            sp.wait_ge(xn_stored, 16 * (NT // 4))

        @blk.tensor
        def _(pe):
            for g in range(0, NT // 4, 2):
                for k in range(2):
                    pe.wait_ge(y_ready, g + k + 1)
                    for j in range(4):
                        ins = nc.tensor.transpose(psT[k][:, j * P:(j + 1) * P], sh.y[:, (g + k) * 4 + j, :],
                                                  sh.ident[:])
                    ins.then_inc(yT_ps, 1)
                for k in range(2):
                    pe.wait_ge(yT_ready, g + k + 1)
                    for j in range(4):
                        at = ((g + k) * 4 + j) * E
                        ins = nc.tensor.matmul(aff[:, at:at + E], yT[k][:, j * P:(j + 1) * P], sh.cgbT[:, 0:E],
                                               start=True, stop=True)
                    ins.then_inc(aff_ready, 1)
            pe.wait_ge(onehot_ready, 1)
            flat = onehot[:].rearrange("p t e -> p (t e)")
            nc.tensor.matmul(cnt[:, 0:NT * E], sh.before[:], flat, start=True, stop=True)
            nc.tensor.matmul(cnt[:, NT * E:2 * NT * E], sh.onesb[:], flat, start=True, stop=True) \
              .then_inc(rank_ready, 1)
            pe.wait_ge(place_ready, 3)
            for t in range(NT):
                ins = nc.tensor.matmul(invp[:, 0:3 * SLOTS], at_lo[:, t, :],
                                       at_hi[:, t, :, :].rearrange("p a s -> p (a s)"),
                                       start=(t == 0), stop=(t == NT - 1))
            ins.then_inc(inverse_ready, 1)


def expert_phase(nc, sh, f):
    with ExitStack() as ctx:
        sem = lambda n: ctx.enter_context(nc.semaphore(f"e{f}_{n}"))
        sb = lambda n, s, d: ctx.enter_context(nc.sbuf_tensor(f"e{f}_{n}", s, d))
        NX = 4
        gathered = [sem(f"gathered{k}") for k in range(NX)]
        scattered = [sem(f"scattered{k}") for k in range(NX)]
        xT_ps, xT_ready = sem("xT_ps"), sem("xT_ready")
        h_ps, h_ready, hT_ps, hT_ready = sem("h_ps"), sem("h_ready"), sem("hT_ps"), sem("hT_ready")
        out_ps, out_ready = sem("out_ps"), sem("out_ready")
        xg = [sb(f"xg{k}", [P, D], F32) for k in range(NX)]
        yo = [sb(f"yo{k}", [P, D], F32) for k in range(NX)]
        xT = [sb(f"xT{k}", [P, P], F32) for k in range(2)]
        hid = [sb(f"hid{k}", [P, F], F32) for k in range(2)]
        hT = [sb(f"hT{k}", [P, F], F32) for k in range(2)]
        ps_x, ps_h, ps_t, ps_o = sh.bank[0:2], sh.bank[2:4], sh.bank[4:6], sh.bank[6:8]
        GROUPS = SLOTS // NX
        blk = ctx.enter_context(nc.Block())
        expert_of = lambda eng, i: eng.value_load(sh.slot_expert[0:1, bass.ds(i, 1)], min_val=0, max_val=E - 1)
        AHEAD = 3

        def in_groups(eng, group):
            group(0, True, False)
            with eng.Fori(1, GROUPS - 1) as m:
                group(m, False, False)
            group(GROUPS - 1, False, True)

        @blk.gpsimd
        def _(pool):
            def gather(i):
                if i >= NX:
                    pool.wait_ge(xT_ps, i - NX + 1)
                nc.gpsimd.indirect_dma_start(xg[i % NX][:], None, sh.xn_dram,
                                             bass.IndirectOffsetOnAxis(ap=sh.gather_row[:, i:i + 1], axis=0)) \
                  .then_inc(gathered[i % NX], 16)
            for i in range(NX + AHEAD - 1):
                gather(i)
            for i in range(SLOTS):
                if i + NX + AHEAD - 1 < SLOTS:
                    gather(i + NX + AHEAD - 1)
                pool.wait_ge(out_ready, i + 1)
                nc.gpsimd.indirect_dma_start(sh.ys_dram,
                                             bass.IndirectOffsetOnAxis(ap=sh.scatter_row[:, i:i + 1], axis=0),
                                             yo[i % NX][:], None).then_inc(scattered[i % NX], 16)
            for k in range(NX):
                pool.wait_ge(scattered[k], 16 * GROUPS)

        @blk.scalar
        def _(act):
            def xT_of(e, k, n):
                act.wait_ge(xT_ps, n)
                nc.scalar.activation(xT[k % 2][:], ps_x[k % 2][:, 0:P], ACT.Identity,
                                     bias=sh.cgbT[:, bass.ds(e + 2 * E, 1)],
                                     scale=sh.cgbT[:, bass.ds(e + E, 1)]).then_inc(xT_ready, 1)

            def group(m, first, last):
                for k in range(NX):
                    ahead = not (last and k + AHEAD >= NX)
                    if ahead:
                        e = expert_of(act, m * NX + k + AHEAD)
                    act.wait_ge(hT_ps, m * NX + k + 1)
                    nc.scalar.activation(hT[k % 2][:], ps_t[k % 2][:], ACT.Relu).then_inc(hT_ready, 1)
                    if ahead:
                        act.wait_ge(h_ps, m * NX + k + 2)
                        xT_of(e, k + AHEAD, m * NX + k + AHEAD + 1)
            for i in range(AHEAD):
                e = expert_of(act, i)
                if i == 2:
                    act.wait_ge(h_ps, 1)
                xT_of(e, i, i + 1)
            in_groups(act, group)

        @blk.vector
        def _(dve):
            def hidden_of(e, k, n):
                dve.wait_ge(h_ps, n)
                nc.vector.tensor_tensor(hid[k % 2][:], ps_h[k % 2][:], sh.b1bc[:, bass.ds(e * F, F)],
                                        ALU.add).then_inc(h_ready, 1)

            def group(m, first, last):
                e = {}
                for k in range(NX):
                    if not (last and k == NX - 1):
                        e[k + 1] = expert_of(dve, m * NX + k + 1)
                        hidden_of(e[k + 1], k + 1, m * NX + k + 2)
                    if k == 0:
                        e[0] = expert_of(dve, m * NX)
                    if not first:
                        dve.wait_ge(scattered[k], m * 16)
                    dve.wait_ge(out_ps, m * NX + k + 1)
                    nc.vector.tensor_tensor(yo[k][:], ps_o[k % 2][:, 0:D],
                                            sh.b2bc[:, bass.ds(e[k] * D, D)], ALU.add).then_inc(out_ready, 1)
            hidden_of(expert_of(dve, 0), 0, 1)
            in_groups(dve, group)

        @blk.tensor
        def _(pe):
            def transpose_rows(k, gathers):
                pe.wait_ge(gathered[k % NX], gathers)
                nc.tensor.transpose(ps_x[k % 2][:, 0:P], xg[k % NX][:], sh.ident[:]).then_inc(xT_ps, 1)

            def first_product(e, k, n):
                pe.wait_ge(xT_ready, n)
                nc.tensor.matmul(ps_h[k % 2][:], xT[k % 2][:],
                                 sh.w1[:, bass.ds(e, 1), :].rearrange("p o f -> p (o f)"),
                                 start=True, stop=True).then_inc(h_ps, 1)

            def group(m, first, last):
                e = {}
                for k in range(NX):
                    more = not (last and k == NX - 1)
                    if more:
                        e[k + 1] = expert_of(pe, m * NX + k + 1)
                    pe.wait_ge(h_ready, m * NX + k + 1)
                    for c in range(FC):
                        ins = nc.tensor.transpose(ps_t[k % 2][:, c * P:(c + 1) * P],
                                                  hid[k % 2][:, c * P:(c + 1) * P], sh.ident[:])
                    ins.then_inc(hT_ps, 1)
                    if more:
                        first_product(e[k + 1], k + 1, m * NX + k + 2)
                    if k == 0:
                        e[0] = expert_of(pe, m * NX)
                    if not (last and k + AHEAD >= NX):
                        transpose_rows(k + AHEAD, (m + 1 + (k + AHEAD) // NX) * 16)
                    pe.wait_ge(hT_ready, m * NX + k + 1)
                    if not (first and k < 2):
                        pe.wait_ge(out_ready, m * NX + k - 1)
                    for c in range(FC):
                        ins = nc.tensor.matmul(ps_o[k % 2][:, 0:D], hT[k % 2][:, c * P:(c + 1) * P],
                                               sh.w2[:, bass.ds(e[k], 1), c, :].rearrange("p o d -> p (o d)"),
                                               start=(c == 0), stop=(c == FC - 1))
                    ins.then_inc(out_ps, 1)
            e = expert_of(pe, 0)
            transpose_rows(0, 16)
            transpose_rows(1, 16)
            first_product(e, 0, 1)
            transpose_rows(2, 16)
            in_groups(pe, group)


def combine_phase(nc, sh, f, out=None):
    with ExitStack() as ctx:
        sem = lambda n: ctx.enter_context(nc.semaphore(f"c{f}_{n}"))
        back, mixed, x_ready, stored = [sem(f"back{g}") for g in range(NT // 4)], sem("mixed"), sem("x_ready"), sem("stored")
        blk = ctx.enter_context(nc.Block())

        @blk.sync
        def _(sp):
            src = sh.ys_dram[0:N, :].rearrange("(t p) d -> p t d", p=P)
            for g in range(NT // 4):
                sp.dma_start(sh.xn[:, 4 * g:4 * g + 4, :], src[:, 4 * g:4 * g + 4, :]).then_inc(back[g], 16)
            if out is not None:
                dst = out.rearrange("b (t p) d -> p (b t) d", p=P)
                for g in range(NT // 4):
                    sp.wait_ge(x_ready, g + 1)
                    sp.dma_start(dst[:, 4 * g:4 * g + 4, :], sh.x[:, 4 * g:4 * g + 4, :]).then_inc(stored, 16)
                sp.wait_ge(stored, 16 * (NT // 4))

        @blk.vector
        def _(dve):
            for g in range(NT // 4):
                dve.wait_ge(back[g], 16)
                for t in range(4 * g, 4 * g + 4):
                    ins = nc.vector.scalar_tensor_tensor(out=sh.y[:, t, :], in0=sh.xn[:, t, :],
                                                         scalar=sh.alpha[:, t:t + 1], in1=sh.y[:, t, :],
                                                         op0=ALU.mult, op1=ALU.add)
                ins.then_inc(mixed, 1)
                dve.wait_ge(mixed, g + 1)
                nc.vector.scalar_tensor_tensor(out=sh.x[:, 4 * g:4 * g + 4, :].rearrange("p t d -> p (t d)"),
                                               in0=sh.y[:, 4 * g:4 * g + 4, :].rearrange("p t d -> p (t d)"),
                                               scalar=0.5,
                                               in1=sh.x[:, 4 * g:4 * g + 4, :].rearrange("p t d -> p (t d)"),
                                               op0=ALU.mult, op1=ALU.add).then_inc(x_ready, 1)


def qkv_phase(nc, sh):
    with ExitStack() as ctx:
        sem = lambda n: ctx.enter_context(nc.semaphore("q_" + n))
        sb = lambda n, s, d: ctx.enter_context(nc.sbuf_tensor("q_" + n, s, d))
        dve_step, var_ready, rstd_ready, stats_done = sem("dve_step"), sem("var_ready"), sem("rstd_ready"), sem("stats_done")
        z_ready, zT_ps, zT_ready = sem("z_ready"), sem("zT_ps"), sem("zT_ready")
        qk_ps, v_ps, v_ready = sem("qk_ps"), sem("v_ps"), sem("v_ready")
        full_ready, first_ready = sem("full_ready"), sem("first_ready")
        rest_ready, parts_ready = sem("rest_ready"), sem("parts_ready")
        parts_stored = [sem(f"parts_stored{k}") for k in range(2)]
        zT = [sb(f"zT{k}", [P, 4 * P], F32) for k in range(2)]
        full = [sb(f"full{k}", [P, 4 * P], F32) for k in range(2)]
        rest = [sb(f"rest{k}", [P, 4 * P], F32) for k in range(2)]
        parts = [sb(f"parts{k}", [P, 3, 4 * P], BF16) for k in range(2)]
        ps_z, ps_qk, ps_v = sh.bank[0:2], sh.bank[2:4], sh.bank[4]
        G = NT // 4
        blk = ctx.enter_context(nc.Block())

        @blk.vector
        def _(dve):
            link = serial(dve, dve_step)
            norm_stats(nc, dve, sh, sh.x, NT, stats_done)
            dve.wait_ge(stats_done, NT // 4)
            norm_finish(nc, link, sh)
            nc.vector.tensor_scalar_add(sh.tmp_b[:], sh.tmp_b[:], EPS).then_inc(var_ready, 1)
            dve.wait_ge(rstd_ready, 1)
            norm_apply(nc, dve, link, sh, sh.x, sh.y, NT, z_ready)
            with dve.Fori(0, G) as g:
                for n in range(2):
                    if n == 1:
                        dve.wait_ge(v_ps, g + 1)
                        nc.vector.tensor_tensor(sh.v[:, bass.ds(g * 4, 4), :],
                                                ps_v[:].rearrange("p (t d) -> p t d", d=D),
                                                sh.bvbc[:].rearrange("p (o d) -> p o d", o=1)
                                                .to_broadcast([P, 4, D]), ALU.add).then_inc(v_ready, 1)
                    dve.wait_ge(full_ready, g * 2 + n + 1)
                    dve.wait_ge(first_ready, g * 2 + n + 1)
                    nc.vector.tensor_tensor(rest[n][:], full[n][:], parts[n][:, 0, :], ALU.subtract) \
                      .then_inc(rest_ready, 1)
                    dve.wait_ge(rest_ready, g * 4 + n * 2 + 1)
                    nc.vector.tensor_copy(parts[n][:, 1, :], rest[n][:]).then_inc(rest_ready, 1)
                    dve.wait_ge(rest_ready, g * 4 + n * 2 + 2)
                    nc.vector.tensor_tensor(parts[n][:, 2, :], rest[n][:], parts[n][:, 1, :], ALU.subtract) \
                      .then_inc(parts_ready, 1)

        @blk.gpsimd
        def _(pool):
            pool.wait_ge(var_ready, 1)
            nc.gpsimd.tensor_tensor(sh.rstd[:], sh.tmp_b[:], sh.neg_half[:], ALU.pow).then_inc(rstd_ready, 1)

        @blk.scalar
        def _(act):
            act.wait_ge(zT_ps, 1)
            nc.scalar.activation(zT[0][:], ps_z[0][:], ACT.Copy).then_inc(zT_ready, 1)

            def qk_read(g, n):
                act.wait_ge(qk_ps, g * 2 + n + 1)
                if g:
                    act.wait_ge(parts_ready, 2 * g + n - 1)
                nc.scalar.activation(full[n][:], ps_qk[n][:], ACT.Identity, bias=sh.bqk[:, n:n + 1]) \
                  .then_inc(full_ready, 1)
                if g:
                    act.wait_ge(parts_stored[n], 48 * g)
                nc.scalar.activation(parts[n][:, 0, :], ps_qk[n][:], ACT.Identity, bias=sh.bqk[:, n:n + 1]) \
                  .then_inc(first_ready, 1)
            for g in range(G):
                qk_read(g, 0)
                if g < G - 1:
                    act.wait_ge(zT_ps, g + 2)
                    nc.scalar.activation(zT[(g + 1) % 2][:], ps_z[(g + 1) % 2][:], ACT.Copy).then_inc(zT_ready, 1)
                qk_read(g, 1)

        @blk.sync
        def _(sp):
            for g in range(G):
                b, half = g // 2, g % 2
                for n in range(2):
                    sp.wait_ge(parts_ready, 2 * g + n + 1)
                    for part in range(3):
                        row = HD * (part if n == 0 else 2 - part)
                        sp.dma_start((sh.q_dram, sh.k_dram)[n][b, :, row:row + HD, half * QW:(half + 1) * QW],
                                     parts[n][:, part, :]).then_inc(parts_stored[n], 16)
            for n in range(2):
                sp.wait_ge(parts_stored[n], 48 * G)

        @blk.tensor
        def _(pe):
            def transposes(g):
                pe.wait_ge(z_ready, g + 1)
                for j in range(4):
                    ins = nc.tensor.transpose(ps_z[g % 2][:, j * P:(j + 1) * P], sh.y[:, 4 * g + j, :], sh.ident[:])
                ins.then_inc(zT_ps, 1)
            transposes(0)
            for g in range(G):
                pe.wait_ge(zT_ready, g + 1)
                for n, name in enumerate(("Wq", "Wk")):
                    if g:
                        pe.wait_ge(first_ready, 2 * g + n - 1)
                    nc.tensor.matmul(ps_qk[n][:], sh.w[name][:], zT[g % 2][:], start=True, stop=True) \
                      .then_inc(qk_ps, 1)
                    if n == 0 and g < G - 1:
                        transposes(g + 1)
                if g:
                    pe.wait_ge(v_ready, g)
                for j in range(4):
                    ins = nc.tensor.matmul(ps_v[:, j * D:(j + 1) * D], zT[g % 2][:, j * P:(j + 1) * P],
                                           sh.w["Wv"][:], start=True, stop=True)
                ins.then_inc(v_ps, 1)


def maximum_units(half):
    t0 = HT * half
    rows = []
    for par in range(2):
        pair = (par, par + 2)
        row = [[(h, t, 0, 4)] for h in pair for t in range(t0, t0 + HT) if half]
        row += [[(h, t0 + 2, t0, 2), (h, t0 + 3, t0, 2)] for h in pair]
        row += [[(h, t0 + i, t0 + i, 1) for i in range(HT)] for h in pair]
        row.append([(h, t0 + i + 1, t0 + i, 1) for h in pair for i in (0, 2)])
        rows.append(row)
    return [u for both in zip(*rows) for u in both]


def attention_phase(nc, sh):
    low, high = maximum_units(0), maximum_units(1)
    prologue_ring = [("S", u) for u in low + high]
    prologue_ring.insert(len(low) + 3, ("M", 0))
    step_ring = list(prologue_ring)
    step_ring.insert(3, ("M", 1))
    step_ring.insert(6, ("E", 0))
    step_ring.insert(9, ("E", 1))
    NPRO, NRING = len(prologue_ring), len(step_ring)
    prologue_banks = [i % 3 for i in range(NPRO - 1)] + [1]
    step_banks = [i % 3 for i in range(NRING - 1)] + [1]
    assert prologue_banks[-4:] == step_banks[-4:] == [0, 1, 2, 1]

    def since(banks, i, before):
        line = before + banks[:i]
        return line[::-1].index(banks[i]) + 1 if banks[i] in line else None
    segments = [[(0, 0, 512)], [(1, 128, 384), (3, 384, 128)], [(2, 256, 256)],
                [(0, 512, 512)], [(1, 512, 512)], [(2, 512, 512)], [(3, 512, 512)], [(4, 512, 512)],
                [(5, 640, 384), (7, 896, 128)], [(6, 768, 256)]]
    NU = len(segments)
    FIRST_HIGH, LAST_LOW = 3, 2
    unit_columns = [sum(width for _, _, width in unit) for unit in segments]
    share = [(NRING * u // NU, NRING * (u + 1) // NU) for u in range(NU)]

    with ExitStack() as ctx:
        sem = lambda n: ctx.enter_context(nc.semaphore("a_" + n))
        sb = lambda n, s, d: ctx.enter_context(nc.sbuf_tensor("a_" + n, s, d))
        op_loaded = [sem(f"op_loaded{g}") for g in range(NG)]
        neg_max_loaded = [sem(f"neg_max_loaded{h}") for h in range(2)]
        neg_max_stored = [sem(f"neg_max_stored{h}") for h in range(2)]
        ring_full, ring_empty = sem("ring_full"), sem("ring_empty")
        split_step, split_ready, neg_maxT_ready, rden_ready = sem("split_step"), sem("split_ready"), sem("neg_maxT_ready"), sem("rden_ready")
        scores_ready, probs_ready = sem("scores_ready"), sem("probs_ready")
        o_low_done, o_high_done, o_low_read, o_high_read = sem("o_low_done"), sem("o_high_done"), sem("o_low_read"), sem("o_high_read")
        v_aug_ready, bias_added, split_cleared = sem("v_aug_ready"), sem("bias_added"), sem("split_cleared")
        cleared = sem("cleared")
        q_op = [sb(f"q_op{g}", [P, 2, T], BF16) for g in range(NG)]
        neg_max = sb("neg_max", [P, 2, GH, HT], F32)
        remain = sb("remain", [P, 2, GH, HT], F32)
        split = sb("split", [P, 2, P], BF16)
        split_view = split[:, :, 0:GH * MROWS * HT].rearrange("p a (h m t) -> p a h m t", h=GH, m=MROWS)
        neg_maxT = [sb(f"neg_maxT{h}", [GH * MROWS * HT, P], BF16) for h in range(2)]
        probs = [sb(f"probs{k}", [P, 2, 2, QW], F32) for k in range(2)]
        rden = [sb(f"rden{h}", [P, HT * GH], F32) for h in range(2)]
        k_op, v_aug = sh.k_op, sh.v_aug
        nm_dram = [nc.dram_tensor(f"neg_max_dram{h}", (GH, MROWS, HT * P), BF16, kind="Internal").ap()
                   for h in range(2)]
        ring_bank, o_bank, scores = sh.bank[0:3], sh.bank[3], sh.two_banks[2:4]
        blk = ctx.enter_context(nc.Block())
        ADDED = P // 4

        @blk.sync
        def _(sp):
            def load_ops(b, g):
                for par in range(2):
                    for src, dst, skip in ((sh.q_dram, q_op[g], 0), (sh.k_dram, k_op[g], HD)):
                        rows = src[bass.ds(b, 1), g * GH:(g + 1) * GH, :, :] \
                            .rearrange("o (s r) d t -> r d (o s) t", r=2)[par]
                        at = 64 * par
                        for n, first in ((3, 0), (2, skip), (1, 2 * skip)):
                            sp.dma_start(dst[at:at + n * HD, :, :], rows[first:first + n * HD]) \
                              .then_inc(op_loaded[g], 16)
                            at += n * HD

            def move_max(group, g, half):
                sp.wait_ge(neg_maxT_ready, group * 2 + half + 1)
                sp.dma_start(nm_dram[half].rearrange("h m (t q) -> (h m t) q", q=P), neg_maxT[half][:]) \
                  .then_inc(neg_max_stored[half], 16)
                sp.wait_ge(neg_max_stored[half], group * 16 + 16)
                for par in range(2):
                    at = 64 * par + TERMS
                    sp.dma_start(q_op[g][at:at + MROWS, :, half * QW:(half + 1) * QW],
                                 nm_dram[half].rearrange("(s r) m q -> r m s q", r=2)[par]) \
                      .then_inc(neg_max_loaded[half], 16)
            for g in range(2):
                sp.wait_ge(cleared, g + 1)
                load_ops(0, g)
            sp.wait_ge(cleared, NG)
            move_max(0, 0, 0)
            with sp.Fori(0, B) as b:
                for g in range(NG):
                    n = b * NG + g
                    move_max(n, g, 1)
                    if g < NG - 2:
                        load_ops(b, g + 2)
                    else:
                        load_ops((b + 1) % B, g - (NG - 2))
                    move_max(n + 1, (g + 1) % NG, 0)
            for g in range(NG):
                sp.wait_ge(op_loaded[g], 16 * 12 * (B + (g < 2)))
            sp.wait_ge(neg_max_loaded[0], 32 * (B * NG + 1))
            sp.wait_ge(neg_max_loaded[1], 32 * B * NG)

        @blk.gpsimd
        def _(pool):
            def augment(b, g):
                nc.gpsimd.tensor_copy(v_aug[g % 2][:, :, :, 0:HD],
                                      sh.v[:, bass.ds(b * TB, TB), g * GH * HD:(g + 1) * GH * HD]
                                      .rearrange("p t (h d) -> p t h d", d=HD)).then_inc(v_aug_ready, 1)
            augment(0, 0)
            augment(0, 1)
            nc.gpsimd.tensor_tensor(sh.x[:], sh.x[:], sh.bobc[:].rearrange("p (o d) -> p o d", o=1)
                                    .to_broadcast([P, NT, D]), ALU.add).then_inc(bias_added, 1)
            with pool.Fori(0, B) as b:
                for g in range(NG):
                    pool.wait_ge(o_high_done, b * NG + g + 1)
                    if g < NG - 2:
                        augment(b, g + 2)
                    else:
                        augment((b + 1) % B, g - (NG - 2))

        @blk.scalar
        def _(act):
            act.sem_inc(o_low_read, 1)
            act.sem_inc(o_high_read, 1)
            with act.Fori(0, B) as b:
                for g in range(NG):
                    n = b * NG + g
                    for u in range(NU):
                        for pair in range(2):
                            act.wait_ge(scores_ready, (n * NU + u) * 2 + pair + 1)
                            cols = slice(0, unit_columns[u])
                            nc.scalar.activation(probs[u % 2][:, pair, :, cols],
                                                 scores[pair].rearrange("p (h q) -> p h q", q=QW)[:, :, cols],
                                                 ACT.Exp, scale=SCALE).then_inc(probs_ready, 1)
                        if u == LAST_LOW + 1:
                            act.wait_ge(o_low_done, n + 1)
                            nc.scalar.activation(sh.o_sb[:, 0:QW], o_bank, ACT.Copy).then_inc(o_low_read, 1)
                    act.wait_ge(o_high_done, n + 1)
                    nc.scalar.activation(sh.o_sb[:, QW:T], o_bank, ACT.Copy).then_inc(o_high_read, 1)

        @blk.vector
        def _(dve):
            flat = sh.block_max[:].rearrange("p h t j -> p (h t j)")

            def places(unit):
                h, t, j, width = unit[0]
                if width == 4:
                    return sh.block_max[:, h, t, j:j + 4]
                if width == 2:
                    return sh.block_max[:, h, t:t + 2, j:j + 2]
                first = t * TB + j
                if unit[2][0] == h:
                    return flat[:, h * TB * TB + first:h * TB * TB + first + 3 * (TB + 1) + 1:TB + 1]
                both = flat.rearrange("p (s r x) -> p s r x", r=2, x=TB * TB)[:, :, h % 2, :]
                return both[:, :, first:first + 2 * (TB + 1) + 1:2 * (TB + 1)]

            def split_max(group, half):
                done = (group * 2 + half) * 4
                keys = HT * (half + 1)
                nm, rm = neg_max[:, half], remain[:, half]
                part = lambda i: split_view[:, half, :, i, :]
                nc.vector.tensor_reduce(nm, sh.block_max[:, :, HT * half:HT * half + HT, 0:keys], axis=AX.X,
                                        op=ALU.max, negate=True).then_inc(split_step, 1)
                dve.wait_ge(split_step, done + 1)
                nc.vector.tensor_copy(part(0), nm).then_inc(split_step, 1)
                dve.wait_ge(split_step, done + 2)
                nc.vector.tensor_tensor(rm, nm, part(0), ALU.subtract).then_inc(split_step, 1)
                dve.wait_ge(split_step, done + 3)
                nc.vector.tensor_copy(part(1), rm).then_inc(split_step, 1)
                dve.wait_ge(split_step, done + 4)
                nc.vector.tensor_tensor(part(2), rm, part(1), ALU.subtract).then_inc(split_ready, 1)

            def empty(kind, what, count, at, group, slot, cols, n):
                bank = ring_bank[at]
                dve.wait_ge(ring_full, count + 1)
                if kind == "S":
                    nc.vector.tensor_reduce(places(what), bank.rearrange("p (a q) -> p a q", q=P), axis=AX.X,
                                            op=ALU.max).then_inc(ring_empty, 1)
                elif kind == "M":
                    nc.vector.tensor_copy(neg_maxT[what][:], bank.bitcast(BF16)[0:GH * MROWS * HT, 0:P]) \
                      .then_inc(neg_maxT_ready, 1)
                    dve.wait_ge(neg_maxT_ready, group * 2 + what + 1)
                    dve.sem_inc(ring_empty, 1)
                else:
                    heads = bank.rearrange("p (t h c) -> p t h c", h=GH, c=ADDED)
                    recip = rden[what][:].rearrange("p (t h) -> p t h", h=GH)
                    nc.vector.reciprocal(recip, heads[:, :, :, HD]).then_inc(rden_ready, 1)
                    dve.wait_ge(rden_ready, 2 * n + what + 1)
                    nc.vector.tensor_tensor(sh.att[:, bass.ds(slot * TB + what * HT, HT), cols:cols + GH * HD]
                                            .rearrange("p t (h d) -> p t h d", d=HD),
                                            heads[:, :, :, 0:HD],
                                            rden[what][:].rearrange("p (t h o) -> p t h o", h=GH, o=1)
                                            .to_broadcast([P, HT, GH, HD]), ALU.mult).then_inc(ring_empty, 1)

            def empty_all(entries, banks, first, group, own, slot, cols, n):
                seen = 0
                for i, (kind, what) in enumerate(entries):
                    whose = own if (kind, what) == ("M", 1) else group
                    empty(kind, what, first + i, banks[i], whose, slot, cols, n)
                    seen += kind == "S"
                    if kind == "S" and seen in (len(low), len(low) + len(high)):
                        dve.wait_ge(ring_empty, first + i + 1)
                        split_max(group, int(seen > len(low)))
            for g in range(NG):
                nc.vector.memset(q_op[g][:], 0.0).then_inc(cleared, 1)
            nc.vector.memset(split[:], 0.0).then_inc(split_cleared, 1)
            dve.wait_ge(split_cleared, 1)
            empty_all(prologue_ring, prologue_banks, 0, 0, None, 0, 0, 0)
            with dve.Fori(0, B) as b:
                for g in range(NG):
                    n = b * NG + g
                    slot, cols = (b + 1, (g - 1) * GH * HD) if g else (b + 0, (NG - 1) * GH * HD)
                    empty_all(step_ring, step_banks, n * NRING + NPRO, n + 1, n, slot, cols, n)
            for i in range(2):
                empty("E", i, NPRO + B * NG * NRING + i, i, None, B, (NG - 1) * GH * HD, B * NG)

        @blk.tensor
        def _(pe):
            def fill(kind, what, count, at, lag, group, g, loads, n):
                bank = ring_bank[at]
                if lag is not None:
                    pe.wait_ge(ring_empty, count - lag + 1)
                if kind == "S":
                    pe.wait_ge(op_loaded[g], loads)
                    col = 0
                    diagonal = what[0][1] == what[0][2]
                    for i, (h, t, j, width) in enumerate(what):
                        rows = slice(64 * (h % 2), 64 * (h % 2) + TERMS)
                        ins = nc.tensor.matmul(bank[:, col:col + width * P], q_op[g][rows, h // 2, t * P:(t + 1) * P],
                                               k_op[g][rows, h // 2, j * P:(j + width) * P], start=(i == 0),
                                               stop=(i == len(what) - 1 and not diagonal))
                        col += width * P
                    if diagonal:
                        ins = nc.tensor.matmul(bank, sh.identb[:], sh.mask_qk[:].rearrange("p a q -> p (a q)"),
                                               start=False, stop=True)
                elif kind == "M":
                    pe.wait_ge(split_ready, group * 2 + what + 1)
                    ins = nc.tensor.transpose(bank.bitcast(BF16)[:, 0:P], split[:, what, :], sh.identb[:])
                else:
                    pe.wait_ge((o_low_read, o_high_read)[what], n + 1)
                    for j in range(HT):
                        ins = nc.tensor.transpose(bank[:, j * P:(j + 1) * P],
                                                  sh.o_sb[:, what * QW + j * P:what * QW + (j + 1) * P], sh.ident[:])
                ins.then_inc(ring_full, 1)

            def score_pair(n, g, u, pair):
                if u:
                    pe.wait_ge(probs_ready, (n * NU + u) * 2 + pair - 1)
                diagonal = [q0 == kt * P for kt, q0, width in segments[u]]
                for r in range(2):
                    rows = slice(64 * r, 64 * r + 64)
                    col = r * QW
                    for i, (kt, q0, width) in enumerate(segments[u]):
                        ins = nc.tensor.matmul(scores[pair][:, col:col + width],
                                               k_op[g][rows, pair, kt * P:(kt + 1) * P],
                                               q_op[g][rows, pair, q0:q0 + width], start=(i == 0),
                                               stop=(i == len(segments[u]) - 1 and not any(diagonal)))
                        col += width
                for r in range(2):
                    col = r * QW
                    for i, (kt, q0, width) in enumerate(segments[u]):
                        if diagonal[i]:
                            ins = nc.tensor.matmul(scores[pair][:, col:col + P], sh.identb[:], sh.mask_kq[:],
                                                   start=False, stop=not any(diagonal[i + 1:]))
                        col += width
                ins.then_inc(scores_ready, 1)

            def products(n, g, u):
                pe.wait_ge(probs_ready, (n * NU + u) * 2 + 2)
                if u == 0:
                    pe.wait_ge(v_aug_ready, n + 1)
                    pe.wait_ge(o_high_read, n + 1)
                if u == FIRST_HIGH:
                    pe.wait_ge(o_low_read, n + 2)
                col = 0
                for kt, q0, width in segments[u]:
                    half = q0 // QW
                    at = q0 % QW
                    stop = u in (LAST_LOW, NU - 1)
                    for h in range(GH):
                        ins = nc.tensor.matmul(o_bank[ADDED * h:ADDED * (h + 1), at:at + width],
                                               v_aug[g % 2][:, kt, h, :],
                                               probs[u % 2][:, h // 2, h % 2, col:col + width],
                                               start=(kt == 0), stop=stop, tile_position=(0, ADDED * h))
                    col += width
                    if u == LAST_LOW and half == 0:
                        ins.then_inc(o_low_done, 1)
                if u == NU - 1:
                    ins.then_inc(o_high_done, 1)

            for i, (kind, what) in enumerate(prologue_ring):
                fill(kind, what, i, prologue_banks[i], since(prologue_banks, i, []), 0, 0, 16 * 12, 0)
            with pe.Fori(0, B) as b:
                for g in range(NG):
                    n = b * NG + g
                    loads = (b + 1 + (g == NG - 1)) * (16 * 12)

                    def fill_next(entries, count):
                        for _ in range(count):
                            i = entries.pop(0)
                            kind, what = step_ring[i]
                            own = (kind, what) == ("M", 1)
                            fill(kind, what, n * NRING + (NPRO + i), step_banks[i],
                                 since(step_banks, i, step_banks), n if own else n + 1, (g + 1) % NG, loads, n)
                    for u in range(NU):
                        if u == 0:
                            pe.wait_ge(neg_max_loaded[0], n * 32 + 32)
                        if u == FIRST_HIGH:
                            pe.wait_ge(neg_max_loaded[1], n * 32 + 32)
                        beside = list(range(*share[u]))
                        score_pair(n, g, u, 0)
                        fill_next(beside, 1)
                        score_pair(n, g, u, 1)
                        fill_next(beside, 1)
                        if u:
                            products(n, g, u - 1)
                        fill_next(beside, len(beside))
                    products(n, g, NU - 1)
            for i in range(2):
                fill("E", i, NPRO + B * NG * NRING + i, i, since([0, 1], i, step_banks), None, None, None, B * NG)


def projection_phase(nc, sh):
    with ExitStack() as ctx:
        sem = lambda n: ctx.enter_context(nc.semaphore("p_" + n))
        attT_ps, attT_ready, proj_ps, x_ready = sem("attT_ps"), sem("attT_ready"), sem("proj_ps"), sem("x_ready")
        attT = [ctx.enter_context(nc.sbuf_tensor(f"p_attT{k}", [P, 4 * P], F32)) for k in range(2)]
        ps_t, ps_o = sh.bank[0:2], sh.bank[2:4]
        G = NT // 4
        blk = ctx.enter_context(nc.Block())

        @blk.tensor
        def _(pe):
            def transposes(g):
                for j in range(4):
                    ins = nc.tensor.transpose(ps_t[g % 2][:, j * P:(j + 1) * P], sh.att[:, TB + 4 * g + j, :],
                                              sh.ident[:])
                ins.then_inc(attT_ps, 1)
            transposes(0)
            for g in range(G):
                if g < G - 1:
                    transposes(g + 1)
                pe.wait_ge(attT_ready, g + 1)
                if g >= 2:
                    pe.wait_ge(x_ready, g - 1)
                for j in range(4):
                    ins = nc.tensor.matmul(ps_o[g % 2][:, j * D:(j + 1) * D], attT[g % 2][:, j * P:(j + 1) * P],
                                           sh.w["Wo"][:], start=True, stop=True)
                ins.then_inc(proj_ps, 1)

        @blk.scalar
        def _(act):
            for g in range(G):
                act.wait_ge(attT_ps, g + 1)
                nc.scalar.activation(attT[g % 2][:], ps_t[g % 2], ACT.Copy).then_inc(attT_ready, 1)

        @blk.vector
        def _(dve):
            for g in range(G):
                dve.wait_ge(proj_ps, g + 1)
                xg = sh.x[:, 4 * g:4 * g + 4, :].rearrange("p t d -> p (t d)")
                nc.vector.tensor_tensor(xg, ps_o[g % 2], xg, ALU.add).then_inc(x_ready, 1)


def build(nc, a, out):
    with ExitStack() as ctx:
        sh = Shared()
        sb = lambda n, s, d: ctx.enter_context(nc.sbuf_tensor(n, s, d))
        psum = ctx.enter_context(nc.psum_tensor("psum", [P, 8 * 512], F32))
        sh.bank = [psum[:, 512 * i:512 * (i + 1)] for i in range(8)]
        sh.two_banks = [psum[:, 1024 * i:1024 * (i + 1)] for i in range(4)]
        sh.act_loads = ctx.enter_context(nc.semaphore("act_loads"))
        sh.x, sh.y, sh.v = [sb(n, [P, NT, D], F32) for n in ("x_sb", "y_sb", "v_sb")]
        sh.att = sb("att_sb", [P, (B + 1) * TB, D], F32)
        sh.xn = sh.att[:, 0:NT, :]
        sh.w = {n: sb(n + "_sb", [D, D], F32) for n in ("Wq", "Wk", "Wv", "Wo")}
        sh.bqk, sh.bvbc, sh.bobc = sb("bqk", [P, 2], F32), sb("bv_bc", [P, D], F32), sb("bo_bc", [P, D], F32)
        sh.w1, sh.w2 = sb("w1_sb", [P, E, F], F32), sb("w2_sb", [P, E, FC, D], F32)
        sh.b1bc, sh.b2bc = sb("b1_bc", [P, E * F], F32), sb("b2_bc", [P, E * D], F32)
        sh.cgbT = sb("cgbT", [P, 3 * E], F32)
        sh.ident, sh.identb = sb("ident", [P, P], F32), sb("identb", [P, P], BF16)
        sh.before, sh.onesb = sb("before", [P, P], BF16), sb("onesb", [P, P], BF16)
        sh.mask_qk, sh.mask_kq = sb("mask_qk", [P, 4, P], BF16), sb("mask_kq", [P, P], BF16)
        sh.em8, sh.ones8 = sb("em8", [P, E], F32), sb("ones8", [P, E], F32)
        sh.thr, sh.tile_id, sh.neg_half = [sb(n, [P, NT], F32) for n in ("thr", "tile_id", "neg_half")]
        sh.slot_id = sb("slot_id", [P, SLOTS, E - 1], F32)
        sh.row128, sh.row_slots, sh.part_id = sb("row128", [P, P], F32), sb("row_slots", [P, SLOTS], F32), sb("part_id", [P, 1], F32)
        sh.trash, sh.keep = sb("trash", [P, SLOTS], F32), sb("keep", [P, E, NT], F32)
        sh.stats = sb("stats", [P, NT, 6], F32)
        sh.mean, sh.rstd, sh.shift, sh.tmp_a, sh.tmp_b, sh.mx, sh.alpha = [
            sb(n, [P, NT], F32) for n in ("mean", "rstd", "shift", "tmp_a", "tmp_b", "mx", "alpha")]
        sh.gather_row, sh.scatter_row = sb("gather_row", [P, SLOTS], I32), sb("scatter_row", [P, SLOTS], I32)
        sh.slot_expert = sb("slot_expert", [P, SLOTS], I32)
        sh.block_max = sb("block_max", [P, GH, TB, TB], F32)
        sh.k_op = [sb(f"k_op{g}", [P, 2, T], BF16) for g in range(NG)]
        sh.v_aug = [sb(f"v_aug{k}", [P, TB, GH, P // 4], F32) for k in range(2)]
        sh.o_sb = sb("o_sb", [P, T], F32)
        sh.q_dram, sh.k_dram = [nc.dram_tensor(n, (B, H, 3 * HD, T), BF16, kind="Internal").ap()
                                for n in ("q_dram", "k_dram")]
        sh.xn_dram = nc.dram_tensor("xn_dram", (N, D), F32, kind="Internal").ap()
        sh.ys_dram = nc.dram_tensor("ys_dram", (N + SLOTS * P, D), F32, kind="Internal").ap()
        setup_phase(nc, sh, a)
        route_phase(nc, sh, 0)
        expert_phase(nc, sh, 0)
        combine_phase(nc, sh, 0)
        qkv_phase(nc, sh)
        attention_phase(nc, sh)
        projection_phase(nc, sh)
        route_phase(nc, sh, 1)
        expert_phase(nc, sh, 1)
        combine_phase(nc, sh, 1, out)


_INS = {"x": "L0_attn_x", "Wq": "L0_attn_Wq", "bq": "L0_attn_bq", "Wk": "L0_attn_Wk", "bk": "L0_attn_bk",
        "Wv": "L0_attn_Wv", "bv": "L0_attn_bv", "Wo": "L0_attn_Wo", "bo": "L0_attn_bo",
        "centroids": "L0_ffn_centroids", "ln_g": "L0_ffn_ln_g", "ln_b": "L0_ffn_ln_b", "w1": "L0_ffn_w1",
        "b1": "L0_ffn_b1", "w2": "L0_ffn_w2", "b2": "L0_ffn_b2"}


def kernel(**inputs):
    import concourse.bacc as bacc
    from concourse.bass_utils import run_bass_kernel_spmd

    nc = bacc.Bacc("TRN2", target_bir_lowering=False, num_devices=1)
    arrays, args = {}, {}
    for short, name in _INS.items():
        arrays[f"in_{short}"] = np.ascontiguousarray(inputs[name])
        args[short] = nc.dram_tensor(f"in_{short}", arrays[f"in_{short}"].shape, F32, kind="ExternalInput").ap()
    out = nc.dram_tensor("out", (B, T, D), F32, kind="ExternalOutput").ap()
    build(nc, args, out)
    return run_bass_kernel_spmd(nc, [arrays], core_ids=[0]).results[0]["out"]
```

```python
import numpy as np
import concourse.bass as bass
from concourse import mybir
from concourse.alu_op_type import AluOpType as ALU
from contextlib import ExitStack

F32 = mybir.dt.float32
BF16 = mybir.dt.bfloat16
I32 = mybir.dt.int32
ACT = mybir.ActivationFunctionType
AX = mybir.AxisListType

B, T, D = 4, 1024, 128
H, HD = 16, 8
F, E = 512, 8
P = 128
N = B * T
NT = N // P
TB = T // P
FC = F // P
SLOTS = (N + E * (P - 1)) // P
TRASH = N
EPS = 1e-5
BIG = -1.0e30
LOWEST = -3.0e38
GH = 4
NG = H // GH
TERMS = 6 * HD
OP_LOADS = 18
MROWS = 3
SCALE = HD ** -0.5
CONSTS = 10
EXPERT_LOADS, ATTN_LOADS = 4, 8
NCHUNK = 4
CT = NT // NCHUNK
QW = T // 2
HT = TB // 2


def chunk(c):
    return slice(CT * c, CT * (c + 1))


class Shared:
    pass


def serial(eng, sem):
    count = [0]

    def link(ins):
        count[0] += 1
        ins.then_inc(sem, 1)
        eng.wait_ge(sem, count[0])
    return link


class Norm:

    def __init__(self, sb, name):
        self.stats = sb(name + "_stats", [P, NT, 6], F32)
        self.mean_var = sb(name + "_mean_var", [P, NT, 2], F32)
        self.neg_mean, self.var_eps, self.rstd, self.shift = [
            sb(f"{name}_{n}", [P, NT], F32) for n in ("neg_mean", "var_eps", "rstd", "shift")]


def norm_stats(nc, link, norm, src, tiles, var_ready):
    for t in tiles:
        ins = nc.vector.bn_stats(norm.stats[:, t, :], src[:, t, :])
    link(ins)
    for t in tiles:
        ins = nc.vector.bn_aggr(norm.mean_var[:, t, :], norm.stats[:, t, :])
    link(ins)
    at = slice(tiles[0], tiles[-1] + 1)
    nc.vector.tensor_scalar(norm.neg_mean[:, at], norm.mean_var[:, at, 0], -1.0, None, ALU.mult)
    nc.vector.tensor_scalar_add(norm.var_eps[:, at], norm.mean_var[:, at, 1], EPS).then_inc(var_ready, 1)


def norm_scale(nc, link, sh, norm, tiles, scale_ready):
    at = slice(tiles[0], tiles[-1] + 1)
    link(nc.gpsimd.tensor_tensor(norm.rstd[:, at], norm.var_eps[:, at], sh.neg_half[:, at], ALU.pow))
    nc.gpsimd.tensor_tensor(norm.shift[:, at], norm.neg_mean[:, at], norm.rstd[:, at], ALU.mult) \
      .then_inc(scale_ready, 1)


def norm_rows(nc, norm, src, dst, tiles, rows_ready):
    for t in tiles:
        ins = nc.scalar.activation(dst[:, t, :], src[:, t, :], ACT.Identity, bias=norm.shift[:, t:t + 1],
                                   scale=norm.rstd[:, t:t + 1])
    ins.then_inc(rows_ready, 1)


def setup_phase(nc, sh, a):
    with ExitStack() as ctx:
        sem = lambda n: ctx.enter_context(nc.semaphore(n))
        cgb_in = sem("su_cgb")
        pool_step, consts, dve_step = sem("su_pool_step"), sem("su_consts"), sem("su_dve_step")
        cgb_ps, dve_fill = sem("su_cgb_ps"), sem("su_dve_fill")
        cgb = ctx.enter_context(nc.sbuf_tensor("su_cgb_rows", [3 * E, D], F32))
        blk = ctx.enter_context(nc.Block())

        @blk.sync
        def _(sp):
            sp.dma_start(cgb[0:E, :], a["centroids"]).then_inc(cgb_in, 16)
            sp.dma_start(cgb[E:2 * E, :], a["ln_g"]).then_inc(cgb_in, 16)
            sp.dma_start(cgb[2 * E:3 * E, :], a["ln_b"]).then_inc(cgb_in, 16)
            x_rows = a["x"].rearrange("b (t p) d -> p (b t) d", p=P)
            for c in range(NCHUNK):
                sp.dma_start(sh.x[:, chunk(c), :], x_rows[:, chunk(c), :]).then_inc(sh.x_loaded[c], 16)

        @blk.gpsimd
        def _(pool):
            link = serial(pool, pool_step)
            sel = nc.gpsimd.affine_select
            link(nc.gpsimd.memset(sh.ident[:], 0.0))
            link(sel(out=sh.ident[:], in_=sh.ident[:], compare_op=ALU.not_equal, fill=1.0, base=0,
                     pattern=[[-1, P]], channel_multiplier=1))
            nc.gpsimd.tensor_copy(sh.identb[:], sh.ident[:]).then_inc(consts, 1)
            pool.wait_ge(consts, 1)

        @blk.vector
        def _(dve):
            nc.vector.memset(sh.onesb[:], 1.0).then_inc(dve_fill, 1)
            nc.vector.memset(sh.neg_half[:], -0.5).then_inc(dve_fill, 1)
            nc.vector.memset(sh.ones8[:], 1.0).then_inc(dve_fill, 1)
            nc.vector.memset(sh.block_max[:], LOWEST).then_inc(dve_fill, 1)
            nc.vector.memset(sh.cgbT[:], 0.0).then_inc(dve_fill, 1)
            link = serial(dve, dve_step)
            link(nc.vector.memset(sh.keep[:], 1.0))
            nc.vector.memset(sh.keep[:, :, 0:1], 0.0).then_inc(dve_fill, 1)
            dve.wait_ge(dve_fill, 6)
            dve.wait_ge(cgb_ps, 1)
            link(nc.vector.tensor_copy(sh.cgbT[:, 0:3 * E], sh.bank[0][:, 0:3 * E]))

        @blk.tensor
        def _(pe):
            pe.wait_ge(consts, 1)
            pe.wait_ge(cgb_in, 48)
            nc.tensor.transpose(sh.bank[0][:, 0:3 * E], cgb[:], sh.ident[0:3 * E, 0:3 * E]).then_inc(cgb_ps, 1)


def build_constants(nc, pool, sh, link, consts):
    link(nc.gpsimd.memset(sh.before[:], 1.0))
    nc.gpsimd.affine_select(out=sh.before[:], in_=sh.before[:], compare_op=ALU.is_gt, fill=0.0, base=0,
                            pattern=[[1, P]], channel_multiplier=-1).then_inc(consts, 1)
    link(nc.gpsimd.memset(sh.mask_qk[:], 0.0))
    nc.gpsimd.affine_select(out=sh.mask_qk[:], in_=sh.mask_qk[:], compare_op=ALU.is_ge, fill=BIG, base=0,
        pattern=[[0, 4], [-1, P]], channel_multiplier=1).then_inc(consts, 1)
    iota = lambda out, pattern, base, cm: nc.gpsimd.iota(
        out, pattern, base=base, channel_multiplier=cm, allow_small_or_imprecise_dtypes=True)
    iota(sh.em8[:], [[1, E]], -E, 0).then_inc(consts, 1)
    iota(sh.thr[:], [[P, NT]], 0, 0).then_inc(consts, 1)
    iota(sh.slot_id[:], [[1, SLOTS], [0, E - 1]], 0, 0).then_inc(consts, 1)
    iota(sh.row128[:], [[1, P]], 0, 0).then_inc(consts, 1)
    iota(sh.row_slots[:], [[1, SLOTS]], 0, 0).then_inc(consts, 1)
    iota(sh.tile_id[:], [[1, NT]], 0, 0).then_inc(consts, 1)
    iota(sh.part_id[:], [[0, 1]], 0, 1).then_inc(consts, 1)
    iota(sh.trash[:], [[P, SLOTS]], TRASH, 1).then_inc(consts, 1)
    pool.wait_ge(consts, CONSTS)


def load_weights(sp, sh, a):
    sp.dma_start(sh.w1[:], a["w1"].rearrange("e d f -> d e f")).then_inc(sh.expert_loads, 16)
    sp.dma_start(sh.w2[:], a["w2"].rearrange("e (c p) d -> p e c d", p=P)).then_inc(sh.expert_loads, 16)
    for dst, name in ((sh.b1bc, "b1"), (sh.b2bc, "b2")):
        sp.dma_start(dst[:], a[name].rearrange("e f -> (e f)").rearrange("(o n) -> o n", o=1)
                     .to_broadcast(list(dst.shape))).then_inc(sh.expert_loads, 16)
    for name in ("Wq", "Wk", "Wv", "Wo"):
        sp.dma_start(sh.w[name][:], a[name]).then_inc(sh.attn_loads, 16)
    for i, name in enumerate(("bq", "bk")):
        sp.dma_start(sh.bqk[:, i:i + 1], a[name].rearrange("(p o) -> p o", o=1)).then_inc(sh.attn_loads, 16)
    for dst, name in ((sh.bvbc, "bv"), (sh.bobc, "bo")):
        sp.dma_start(dst[:], a[name].rearrange("(o n) -> o n", o=1).to_broadcast([P, D])) \
          .then_inc(sh.attn_loads, 16)


def fill_first(nc, sh, fills):
    for k_op in sh.k_op[0:3]:
        nc.scalar.activation(k_op[:].rearrange("p s t -> p (s t)"), sh.onesb[:, 0:1].to_broadcast([P, 2 * T]),
                             ACT.Copy).then_inc(fills, 1)


def fill_last(nc, act, link, sh, fills):
    ones = lambda shape: sh.onesb[:, 0:1].to_broadcast(shape)
    for k_op in sh.k_op[3:]:
        nc.scalar.activation(k_op[:].rearrange("p s t -> p (s t)"), ones([P, 2 * T]), ACT.Copy).then_inc(fills, 1)
    nc.scalar.activation(sh.o_sb[:], ones([P, T]), ACT.Copy).then_inc(fills, 1)
    for v in sh.v_aug:
        link(nc.scalar.activation(v[:].rearrange("p t h c -> p (t h c)"), ones([P, TB * P]), ACT.Copy, scale=0.0))
        nc.scalar.activation(v[:, :, :, HD:HD + 1].rearrange("p t h o -> p (t h o)"), ones([P, TB * GH]), ACT.Copy) \
          .then_inc(fills, 1)
    act.wait_ge(fills, len(sh.k_op) + 1 + len(sh.v_aug))


def route_phase(nc, sh, f, a):
    with ExitStack() as ctx:
        sem = lambda n: ctx.enter_context(nc.semaphore(f"r{f}_{n}"))
        sb = lambda n, s, d: ctx.enter_context(nc.sbuf_tensor(f"r{f}_{n}", s, d))
        dve_step, pool_step = sem("dve_step"), sem("pool_step")
        var_ready, scale_ready, y_ready = sem("var_ready"), sem("scale_ready"), sem("y_ready")
        xn_ready, xn_stored = sem("xn_ready"), sem("xn_stored")
        yT_ps, yT_ready, aff_ready = sem("yT_ps"), sem("yT_ready"), sem("aff_ready")
        mx_ready, exp_ready, onehot_ready, rank_ready = sem("mx_ready"), sem("exp_ready"), sem("onehot_ready"), sem("rank_ready")
        hi_ready, hi_parts, lo_ready, inverse_ready = sem("hi_ready"), sem("hi_parts"), sem("lo_ready"), sem("inverse_ready")
        if f == 0:
            act_step, fills, consts = sem("act_step"), sem("fills"), sem("consts")
        else:
            attT_ps, attT_ready, proj_ps, x_ready = sem("attT_ps"), sem("attT_ready"), sem("proj_ps"), sem("x_ready")
        affT_ps, affT_ready, last_y_ready = sem("affT_ps"), sem("affT_ready"), sem("last_y_ready")
        hi_times_tile = sem("hi_times_tile")
        yT = [sb(f"yT{i}", [P, 4 * P], F32) for i in range(2)]
        wide = lambda n, d=F32: sb(n, [P, NT, E], d)
        eq, cand, t1 = wide("eq"), wide("cand"), wide("t1")
        onehot = wide("onehot", BF16)
        cum, before_tile, gt = [sb(n, [P, E, NT], F32) for n in ("cum", "before_tile", "gt")]
        cmin, lo, hi, ex = [sb(n, [P, NT], F32) for n in ("cmin", "lo", "hi", "ex")]
        ntiles, upto, base = [sb(n, [P, E], F32) for n in ("ntiles", "upto", "base")]
        place, lo_i, hi_i = [sb(n, [P, NT], I32) for n in ("place", "lo_i", "hi_i")]
        ge = sb("ge", [P, SLOTS, E - 1], F32)
        slot_e = sb("slot_e", [P, SLOTS], F32)
        at_lo = sb("at_lo", [P, NT, P], BF16)
        at_hi = sb("at_hi", [P, NT, 3, SLOTS], BF16)
        inv = sb("inv", [P, 3 * SLOTS], F32)
        tr, row = sb("tr", [P, SLOTS], F32), sb("row", [P, SLOTS], F32)
        affT = [sb(f"affT{i}", [P, P], F32) for i in range(2)]
        AW = P // 4
        psT, ps_affT, aff, cnt, invp = sh.bank[0:2], sh.bank[2:4], sh.two_banks[2], sh.bank[6], sh.bank[7]
        ps_att, ps_proj = sh.bank[4:6], sh.bank[6:8]
        attT = yT
        norm_y, norm_xn = sh.norms
        NG4 = NT // 4
        blk = ctx.enter_context(nc.Block())

        @blk.vector
        def _(dve):
            link = serial(dve, dve_step)
            for c in range(NCHUNK):
                if f == 0:
                    dve.wait_ge(sh.x_loaded[c], 16)
                else:
                    for g in range(2 * c, 2 * c + 2):
                        dve.wait_ge(proj_ps, g + 1)
                        xg = sh.x[:, 4 * g:4 * g + 4, :].rearrange("p t d -> p (t d)")
                        nc.vector.tensor_tensor(xg, ps_proj[g % 2], xg, ALU.add).then_inc(x_ready, 1)
                    dve.wait_ge(x_ready, 2 * c + 2)
                norm_stats(nc, link, norm_y, sh.x, range(CT * c, CT * c + CT), var_ready)
            for c in range(NCHUNK):
                if c == 1:
                    dve.wait_ge(scale_ready, NCHUNK)
                    for t in range(NT - CT, NT):
                        ins = nc.vector.tensor_scalar(sh.y[:, t, :], sh.x[:, t, :], norm_y.mean_var[:, t, 0:1],
                                                      norm_y.rstd[:, t:t + 1], ALU.subtract, ALU.mult)
                    ins.then_inc(last_y_ready, 1)
                dve.wait_ge(*((y_ready, c + 1) if c < NCHUNK - 1 else (last_y_ready, 1)))
                norm_stats(nc, link, norm_xn, sh.y, range(CT * c, CT * c + CT), var_ready)
            if f == 0:
                dve.wait_ge(consts, CONSTS)
            dve.wait_ge(aff_ready, NG4)
            affv = aff.rearrange("p (t e) -> p t e", e=AW)[:, :, 0:E]
            over_e = lambda x: x[:].rearrange("p (t o) -> p t o", o=1).to_broadcast([P, NT, E])
            nc.vector.tensor_reduce(sh.mx[:], affv, axis=AX.X, op=ALU.max).then_inc(mx_ready, 1)
            dve.wait_ge(mx_ready, 1)
            link(nc.vector.tensor_tensor(eq[:], affv, over_e(sh.mx), ALU.is_equal))
            link(nc.vector.tensor_tensor(cand[:], eq[:], sh.em8[:].rearrange("p (o e) -> p o e", o=1)
                                         .to_broadcast([P, NT, E]), ALU.mult))
            link(nc.vector.tensor_reduce(cmin[:], cand[:], axis=AX.X, op=ALU.min))
            nc.vector.tensor_tensor(onehot[:], cand[:], over_e(cmin), ALU.is_equal).then_inc(onehot_ready, 1)
            dve.wait_ge(rank_ready, 1)
            tot = cnt[:, NT * E:2 * NT * E]
            link(nc.vector.tensor_tensor_scan(cum[:].rearrange("p e t -> p (e t)"),
                                              sh.keep[:].rearrange("p e t -> p (e t)"), tot, 0.0,
                                              ALU.mult, ALU.add))
            link(nc.vector.tensor_tensor(before_tile[:], cum[:], tot.rearrange("p (e t) -> p e t", e=E),
                                         ALU.subtract))
            link(nc.vector.tensor_tensor(gt[:], cum[:, :, NT - 1:NT].to_broadcast([P, E, NT]),
                                         sh.thr[:].rearrange("p (o t) -> p o t", o=1).to_broadcast([P, E, NT]),
                                         ALU.is_gt))
            link(nc.vector.tensor_reduce(ntiles[:], gt[:], axis=AX.X, op=ALU.add))
            link(nc.vector.tensor_tensor_scan(upto[:], sh.ones8[:], ntiles[:], 0.0, ALU.mult, ALU.add))
            link(nc.vector.tensor_tensor(base[:], upto[:], ntiles[:], ALU.subtract))
            link(nc.vector.tensor_scalar(base[:], base[:], float(P), None, ALU.mult))
            link(nc.vector.tensor_tensor(t1[:], cnt[:, 0:NT * E].rearrange("p (t e) -> p t e", e=E),
                                         before_tile[:].rearrange("p e t -> p t e"), ALU.add))
            link(nc.vector.tensor_tensor(t1[:], t1[:], base[:].rearrange("p (o e) -> p o e", o=1)
                                         .to_broadcast([P, NT, E]), ALU.add))
            link(nc.vector.tensor_tensor(t1[:], t1[:], onehot[:], ALU.mult))
            link(nc.vector.tensor_reduce(cmin[:], t1[:], axis=AX.X, op=ALU.add))
            link(nc.vector.tensor_copy(place[:], cmin[:]))
            nc.vector.tensor_single_scalar(lo_i[:], place[:], P - 1, ALU.bitwise_and)
            link(nc.vector.tensor_single_scalar(hi_i[:], place[:], 7, ALU.arith_shift_right))
            nc.vector.tensor_copy(lo[:], lo_i[:])
            link(nc.vector.tensor_copy(hi[:], hi_i[:]))
            nc.vector.tensor_tensor(at_hi[:, :, 0, :], sh.row_slots[:].rearrange("p (o n) -> p o n", o=1)
                                    .to_broadcast([P, NT, SLOTS]),
                                    hi[:].rearrange("p (t o) -> p t o", o=1).to_broadcast([P, NT, SLOTS]),
                                    ALU.is_equal).then_inc(hi_ready, 1)
            for c in range(NCHUNK):
                nc.vector.tensor_tensor(at_lo[:, chunk(c), :], sh.row128[:].rearrange("p (o n) -> p o n", o=1)
                                        .to_broadcast([P, CT, P]),
                                        lo[:, chunk(c)].rearrange("p (t o) -> p t o", o=1)
                                        .to_broadcast([P, CT, P]), ALU.is_equal).then_inc(lo_ready, 1)
            link(nc.vector.tensor_tensor(ge[:], sh.slot_id[:], upto[:, 0:E - 1].rearrange("p (o e) -> p o e", o=1)
                                         .to_broadcast([P, SLOTS, E - 1]), ALU.is_ge))
            link(nc.vector.tensor_reduce(slot_e[:], ge[:], axis=AX.X, op=ALU.add))
            link(nc.vector.tensor_copy(sh.slot_expert[:], slot_e[:]))
            dve.wait_ge(inverse_ready, 1)
            link(nc.vector.tensor_copy(inv[:], invp[:, 0:3 * SLOTS]))
            nc.vector.tensor_tensor(tr[:], inv[:, 0:SLOTS], sh.trash[:], ALU.mult)
            link(nc.vector.scalar_tensor_tensor(out=row[:], in0=inv[:, SLOTS:2 * SLOTS], scalar=float(P),
                                                in1=inv[:, 2 * SLOTS:3 * SLOTS], op0=ALU.mult, op1=ALU.add))
            nc.vector.tensor_copy(sh.gather_row[:], row[:])
            link(nc.vector.tensor_tensor(tr[:], sh.trash[:], tr[:], ALU.subtract))
            link(nc.vector.tensor_tensor(sh.scatter_row[:], row[:], tr[:], ALU.add))
            dve.wait_ge(exp_ready, 1)
            link(nc.vector.tensor_scalar(ex[:], sh.half_alpha[:], 2.0, 2.0, ALU.mult, ALU.add))
            link(nc.vector.reciprocal(sh.half_alpha[:], ex[:]))

        @blk.gpsimd
        def _(pool):
            link = serial(pool, pool_step)
            if f == 0:
                build_constants(nc, pool, sh, link, consts)
            for i, norm in enumerate(sh.norms):
                for c in range(NCHUNK):
                    pool.wait_ge(var_ready, NCHUNK * i + c + 1)
                    norm_scale(nc, link, sh, norm, range(CT * c, CT * c + CT), scale_ready)
            pool.wait_ge(hi_ready, 1)
            nc.gpsimd.tensor_tensor(at_hi[:, :, 1, :], at_hi[:, :, 0, :],
                                    sh.tile_id[:].rearrange("p (t o) -> p t o", o=1)
                                    .to_broadcast([P, NT, SLOTS]), ALU.mult).then_inc(hi_times_tile, 1)

        @blk.scalar
        def _(act):
            def att_transposed(g):
                act.wait_ge(attT_ps, g + 1)
                if g >= 2:
                    act.wait_ge(proj_ps, g - 1)
                nc.scalar.activation(attT[g % 2][:], ps_att[g % 2], ACT.Copy).then_inc(attT_ready, 1)

            def rows(i, c, src, dst, ready):
                act.wait_ge(scale_ready, NCHUNK * i + c + 1)
                norm_rows(nc, sh.norms[i], src, dst, range(CT * c, CT * c + CT), ready)

            def y_transposed(g):
                act.wait_ge(yT_ps, g + 1)
                if g >= 2:
                    act.wait_ge(affT_ps, g - 1)
                nc.scalar.activation(yT[g % 2][:], psT[g % 2][:], ACT.Copy).then_inc(yT_ready, 1)
            if f == 0:
                fill_first(nc, sh, fills)
            else:
                for g in range(6):
                    att_transposed(g)
            rows(0, 0, sh.x, sh.y, y_ready)
            if f == 1:
                for g in range(6, NG4):
                    att_transposed(g)
                act.wait_ge(proj_ps, NG4)
            def aff_transposed(g):
                act.wait_ge(affT_ps, g + 1)
                if g >= 2:
                    act.wait_ge(aff_ready, g - 1)
                nc.scalar.activation(affT[g % 2][:], ps_affT[g % 2][:, 0:P], ACT.Copy).then_inc(affT_ready, 1)
            for c in range(1, NCHUNK + 1):
                if c < NCHUNK - 1:
                    rows(0, c, sh.x, sh.y, y_ready)
                for g in range(2 * c - 2, 2 * c):
                    y_transposed(g)
                    if g:
                        aff_transposed(g - 1)
            aff_transposed(NG4 - 1)
            for c in range(NCHUNK - 1):
                rows(1, c, sh.y, sh.xn, xn_ready)
            if f == 0:
                act.wait_ge(consts, CONSTS)
            act.wait_ge(hi_ready, 1)
            nc.scalar.activation(at_hi[:, :, 2, :], at_hi[:, :, 0, :], ACT.Copy, scale=sh.part_id[:]) \
              .then_inc(hi_parts, 1)
            rows(1, NCHUNK - 1, sh.y, sh.xn, xn_ready)
            act.wait_ge(mx_ready, 1)
            nc.scalar.activation(sh.half_alpha[:], sh.mx[:], ACT.Exp, scale=-1.0).then_inc(exp_ready, 1)
            if f == 0:
                fill_last(nc, act, serial(act, act_step), sh, fills)

        @blk.sync
        def _(sp):
            if f == 0:
                load_weights(sp, sh, a)
            dst = sh.xn_dram.rearrange("(t p) d -> p t d", p=P)
            for c in range(NCHUNK):
                sp.wait_ge(xn_ready, c + 1)
                sp.dma_start(dst[:, chunk(c), :], sh.xn[:, chunk(c), :]).then_inc(xn_stored, 16)
            sp.wait_ge(xn_stored, 16 * NCHUNK)

        @blk.tensor
        def _(pe):
            def att_transposes(g):
                if g >= 2:
                    pe.wait_ge(attT_ready, g - 1)
                for j in range(4):
                    ins = nc.tensor.transpose(ps_att[g % 2][:, j * P:(j + 1) * P], sh.att[:, TB + 4 * g + j, :],
                                              sh.ident[:])
                ins.then_inc(attT_ps, 1)

            def y_transposes(g):
                if g < NG4 - 2:
                    pe.wait_ge(y_ready, g // 2 + 1)
                else:
                    pe.wait_ge(last_y_ready, 1)
                if g >= 2:
                    pe.wait_ge(yT_ready, g - 1)
                for j in range(4):
                    ins = nc.tensor.transpose(psT[g % 2][:, j * P:(j + 1) * P], sh.y[:, 4 * g + j, :], sh.ident[:])
                ins.then_inc(yT_ps, 1)
            if f == 1:
                att_transposes(0)
                for g in range(NG4):
                    if g < NG4 - 1:
                        att_transposes(g + 1)
                    pe.wait_ge(attT_ready, g + 1)
                    if g >= 2:
                        pe.wait_ge(x_ready, g - 1)
                    for j in range(4):
                        ins = nc.tensor.matmul(ps_proj[g % 2][:, j * D:(j + 1) * D], attT[g % 2][:, j * P:(j + 1) * P],
                                               sh.w["Wo"][:], start=True, stop=True)
                    ins.then_inc(proj_ps, 1)
                pe.wait_ge(x_ready, NG4)
            y_transposes(0)
            for g in range(NG4 + 1):
                if g < NG4 - 1:
                    y_transposes(g + 1)
                if g < NG4:
                    pe.wait_ge(yT_ready, g + 1)
                    if g >= 2:
                        pe.wait_ge(affT_ready, g - 1)
                    for j in range(4):
                        ins = nc.tensor.matmul(ps_affT[g % 2][AW * j:AW * (j + 1), 0:P], sh.cgbT[:],
                                               yT[g % 2][:, j * P:(j + 1) * P], start=True, stop=True,
                                               tile_position=(0, AW * j))
                    ins.then_inc(affT_ps, 1)
                if g:
                    pe.wait_ge(affT_ready, g)
                    nc.tensor.transpose(aff[:, (g - 1) * P:g * P], affT[(g - 1) % 2][:], sh.ident[:]) \
                      .then_inc(aff_ready, 1)
            if f == 0:
                pe.wait_ge(consts, CONSTS)
            pe.wait_ge(onehot_ready, 1)
            nc.tensor.matmul(cnt[:, 0:NT * E], sh.before[:], onehot[:].rearrange("p t e -> p (t e)"),
                             start=True, stop=True)
            nc.tensor.matmul(cnt[:, NT * E:2 * NT * E].rearrange("p (e t) -> p e t", e=E), sh.onesb[:],
                             onehot[:].rearrange("p t e -> p e t"), start=True, stop=True) \
              .then_inc(rank_ready, 1)
            pe.wait_ge(hi_parts, 1)
            pe.wait_ge(hi_times_tile, 1)
            for t in range(NT):
                if t % CT == 0:
                    pe.wait_ge(lo_ready, t // CT + 1)
                ins = nc.tensor.matmul(invp[:, 0:3 * SLOTS], at_lo[:, t, :],
                                       at_hi[:, t, :, :].rearrange("p a s -> p (a s)"),
                                       start=(t == 0), stop=(t == NT - 1))
            ins.then_inc(inverse_ready, 1)


def expert_phase(nc, sh, f):
    with ExitStack() as ctx:
        sem = lambda n: ctx.enter_context(nc.semaphore(f"e{f}_{n}"))
        sb = lambda n, s, d: ctx.enter_context(nc.sbuf_tensor(f"e{f}_{n}", s, d))
        AHEAD = 3
        NX = 4
        gathered = [sem(f"gathered{k}") for k in range(NX)]
        scattered = [sem(f"scattered{k}") for k in range(NX)]
        xT_ps, xT_ready = sem("xT_ps"), sem("xT_ready")
        h_ps, h_ready, hT_ps, hT_ready = sem("h_ps"), sem("h_ready"), sem("hT_ps"), sem("hT_ready")
        out_ps, out_ready, x_half = sem("out_ps"), sem("out_ready"), sem("x_half")
        EARLY = 4
        xg = [sb(f"xg{k}", [P, D], F32) for k in range(NX)]
        yo = [sb(f"yo{k}", [P, D], F32) for k in range(NX)]
        xT = [sb(f"xT{k}", [P, P], F32) for k in range(2)]
        hid = [sb(f"hid{k}", [P, F], F32) for k in range(2)]
        hT = [sb(f"hT{k}", [P, F], F32) for k in range(2)]
        ps_x, ps_h, ps_t, ps_o = sh.bank[0:2], sh.bank[2:4], sh.bank[4:6], sh.bank[6:8]
        GT = 2 * NX
        GROUPS = (SLOTS + GT - 1) // GT
        count = lambda last: SLOTS - (GROUPS - 1) * GT if last else GT
        turn = lambda m, k: m * (GT // NX) + k // NX
        assert AHEAD <= count(True)
        blk = ctx.enter_context(nc.Block())
        expert_of = lambda eng, i: eng.value_load(sh.slot_expert[0:1, bass.ds(i, 1)], min_val=0, max_val=E - 1)

        def in_groups(eng, group):
            group(0, True, False)
            with eng.Fori(1, GROUPS - 1) as m:
                group(m, False, False)
            group(GROUPS - 1, False, True)

        @blk.gpsimd
        def _(pool):
            def gather(i):
                if i >= NX:
                    pool.wait_ge(xT_ps, i - NX + 1)
                nc.gpsimd.indirect_dma_start(xg[i % NX][:], None, sh.xn_dram,
                                             bass.IndirectOffsetOnAxis(ap=sh.gather_row[:, i:i + 1], axis=0)) \
                  .then_inc(gathered[i % NX], 16)
            for i in range(NX + AHEAD - 1):
                gather(i)
            for i in range(SLOTS):
                if i + NX + AHEAD - 1 < SLOTS:
                    gather(i + NX + AHEAD - 1)
                pool.wait_ge(out_ready, i + 1)
                nc.gpsimd.indirect_dma_start(sh.ys_dram,
                                             bass.IndirectOffsetOnAxis(ap=sh.scatter_row[:, i:i + 1], axis=0),
                                             yo[i % NX][:], None).then_inc(scattered[i % NX], 16)
            for k in range(NX):
                pool.wait_ge(scattered[k], 16 * len(range(k, SLOTS, NX)))

        @blk.scalar
        def _(act):
            def xT_of(e, k, n):
                act.wait_ge(xT_ps, n)
                nc.scalar.activation(xT[k % 2][:], ps_x[k % 2][:, 0:P], ACT.Identity,
                                     bias=sh.cgbT[:, bass.ds(e + 2 * E, 1)],
                                     scale=sh.cgbT[:, bass.ds(e + E, 1)]).then_inc(xT_ready, 1)

            def group(m, first, last):
                for k in range(count(last)):
                    ahead = not (last and k + AHEAD >= count(last))
                    if ahead:
                        e = expert_of(act, m * GT + k + AHEAD)
                    act.wait_ge(hT_ps, m * GT + k + 1)
                    nc.scalar.activation(hT[k % 2][:], ps_t[k % 2][:], ACT.Relu).then_inc(hT_ready, 1)
                    if ahead:
                        act.wait_ge(h_ps, m * GT + k + 2)
                        xT_of(e, k + AHEAD, m * GT + k + AHEAD + 1)
            for i in range(AHEAD):
                e = expert_of(act, i)
                if i == 2:
                    act.wait_ge(h_ps, 1)
                xT_of(e, i, i + 1)
            in_groups(act, group)

        @blk.vector
        def _(dve):
            def hidden_of(e, k, n):
                dve.wait_ge(h_ps, n)
                nc.vector.tensor_tensor(hid[k % 2][:], ps_h[k % 2][:], sh.b1bc[:, bass.ds(e * F, F)],
                                        ALU.add).then_inc(h_ready, 1)

            def group(m, first, last):
                e = {}
                for k in range(count(last)):
                    if not (last and k + 2 >= count(last)):
                        e[k + 2] = expert_of(dve, m * GT + k + 2)
                        hidden_of(e[k + 2], k + 2, m * GT + k + 3)
                    if k < 2:
                        e[k] = expert_of(dve, m * GT + k)
                    if not (first and k < NX):
                        dve.wait_ge(scattered[k % NX], turn(m, k) * 16)
                    dve.wait_ge(out_ps, m * GT + k + 1)
                    nc.vector.tensor_tensor(yo[k % NX][:], ps_o[k % 2][:, 0:D],
                                            sh.b2bc[:, bass.ds(e[k] * D, D)], ALU.add).then_inc(out_ready, 1)
            def add_half_y(groups):
                for g in groups:
                    xg, yg = [buf[:, 4 * g:4 * g + 4, :].rearrange("p t d -> p (t d)") for buf in (sh.x, sh.y)]
                    nc.vector.scalar_tensor_tensor(out=xg, in0=yg, scalar=0.5, in1=xg, op0=ALU.mult, op1=ALU.add) \
                      .then_inc(x_half, 1)
            add_half_y(range(EARLY))
            dve.wait_ge(sh.expert_loads, 16 * EXPERT_LOADS)
            for i in range(2):
                hidden_of(expert_of(dve, i), i, i + 1)
            in_groups(dve, group)
            add_half_y(range(EARLY, NT // 4))
            dve.wait_ge(x_half, NT // 4)

        @blk.tensor
        def _(pe):
            def transpose_rows(k, gathers):
                pe.wait_ge(gathered[k % NX], gathers)
                nc.tensor.transpose(ps_x[k % 2][:, 0:P], xg[k % NX][:], sh.ident[:]).then_inc(xT_ps, 1)

            def first_product(e, k, n):
                pe.wait_ge(xT_ready, n)
                nc.tensor.matmul(ps_h[k % 2][:], xT[k % 2][:],
                                 sh.w1[:, bass.ds(e, 1), :].rearrange("p o f -> p (o f)"),
                                 start=True, stop=True).then_inc(h_ps, 1)

            def group(m, first, last):
                e = {}
                for k in range(count(last)):
                    more = not (last and k + 2 >= count(last))
                    pe.wait_ge(h_ready, m * GT + k + 1)
                    for c in range(FC):
                        ins = nc.tensor.transpose(ps_t[k % 2][:, c * P:(c + 1) * P],
                                                  hid[k % 2][:, c * P:(c + 1) * P], sh.ident[:])
                    ins.then_inc(hT_ps, 1)
                    if k == 0:
                        e[2] = expert_of(pe, m * GT + 2)
                    if more:
                        first_product(e[k + 2], k + 2, m * GT + k + 3)
                    if k < 2:
                        e[k] = expert_of(pe, m * GT + k)
                    next_more = k + 1 < GT and not (last and k + 3 >= count(last))
                    if next_more and k >= 2:
                        e[k + 3] = expert_of(pe, m * GT + k + 3)
                    if not (last and k + AHEAD >= count(last)):
                        transpose_rows(k + AHEAD, (turn(m, k + AHEAD) + 1) * 16)
                    pe.wait_ge(hT_ready, m * GT + k + 1)
                    if not (first and k < 2):
                        pe.wait_ge(out_ready, m * GT + k - 1)
                    for c in range(FC):
                        ins = nc.tensor.matmul(ps_o[k % 2][:, 0:D], hT[k % 2][:, c * P:(c + 1) * P],
                                               sh.w2[:, bass.ds(e[k], 1), c, :].rearrange("p o d -> p (o d)"),
                                               start=(c == 0), stop=(c == FC - 1))
                    ins.then_inc(out_ps, 1)
                    if next_more and k < 2:
                        e[k + 3] = expert_of(pe, m * GT + k + 3)
            pe.wait_ge(sh.expert_loads, 16 * EXPERT_LOADS)
            e = expert_of(pe, 0)
            transpose_rows(0, 16)
            transpose_rows(1, 16)
            first_product(e, 0, 1)
            transpose_rows(2, 16)
            first_product(expert_of(pe, 1), 1, 2)
            in_groups(pe, group)


def mix_group(nc, dve, sh, g, back, x_ready):
    dve.wait_ge(back[g // 2], 16)
    for t in range(4 * g, 4 * g + 4):
        ins = nc.vector.scalar_tensor_tensor(out=sh.x[:, t, :], in0=sh.xn[:, t, :], scalar=sh.half_alpha[:, t:t + 1],
                                             in1=sh.x[:, t, :], op0=ALU.mult, op1=ALU.add)
    ins.then_inc(x_ready, 1)


def load_back(nc, sp, sh, back):
    src = sh.ys_dram[0:N, :].rearrange("(t p) d -> p t d", p=P)
    for c in range(NCHUNK):
        sp.dma_start(sh.xn[:, chunk(c), :], src[:, chunk(c), :]).then_inc(back[c], 16)


def last_phase(nc, sh, out):
    with ExitStack() as ctx:
        sem = lambda n: ctx.enter_context(nc.semaphore(f"l_{n}"))
        back, x_ready, stored = [sem(f"back{c}") for c in range(NCHUNK)], sem("x_ready"), sem("stored")
        blk = ctx.enter_context(nc.Block())

        @blk.sync
        def _(sp):
            load_back(nc, sp, sh, back)
            dst = out.rearrange("b (t p) d -> p (b t) d", p=P)
            for g in range(NT // 4):
                sp.wait_ge(x_ready, g + 1)
                sp.dma_start(dst[:, 4 * g:4 * g + 4, :], sh.x[:, 4 * g:4 * g + 4, :]).then_inc(stored, 16)
            sp.wait_ge(stored, 16 * (NT // 4))

        @blk.vector
        def _(dve):
            for g in range(NT // 4):
                mix_group(nc, dve, sh, g, back, x_ready)


def qkv_phase(nc, sh):
    with ExitStack() as ctx:
        sem = lambda n: ctx.enter_context(nc.semaphore("q_" + n))
        sb = lambda n, s, d: ctx.enter_context(nc.sbuf_tensor("q_" + n, s, d))
        G = NT // 4
        LEAD = 5
        back, x_ready = [sem(f"back{c}") for c in range(NCHUNK)], sem("x_ready")
        dve_step, pool_step, var_ready, scale_ready = sem("dve_step"), sem("pool_step"), sem("var_ready"), sem("scale_ready")
        z_ready, zT_ps, zT_ready = sem("z_ready"), sem("zT_ps"), sem("zT_ready")
        qk_ps, v_ps, v_ready, q_op_cleared = sem("qk_ps"), sem("v_ps"), sem("v_ready"), sem("q_op_cleared")
        zero_stored = sem("zero_stored")
        first_ready, rest_ready, second_ready, third_ready = sem("first_ready"), sem("rest_ready"), sem("second_ready"), sem("third_ready")
        NSTORE = 3
        parts_stored = [[sem(f"parts_stored{n}{k}") for k in range(NSTORE)] for n in range(2)]
        pair = lambda n, s, d: [[sb(f"{n}{i}{k}", s, d) for k in range(2)] for i in range(2)]
        zT = [sb(f"zT{k}", [P, 4 * P], F32) for k in range(2)]
        rest = pair("rest", [P, 4 * P], F32)
        parts = [[sb(f"parts{i}{k}", [P, 3, 4 * P], BF16) for k in range(NSTORE)] for i in range(2)]
        ps_z, ps_v = sh.bank[0:2], sh.bank[2:4]
        ps_qk = [sh.bank[4:6], sh.bank[6:8]]
        PART = ((0, 1, 2), (2, 1, 0))
        norm = sh.norms[0]
        four = lambda g: range(4 * g, 4 * g + 4)
        blk = ctx.enter_context(nc.Block())

        @blk.vector
        def _(dve):
            link = serial(dve, dve_step)

            def mix_and_stats(g):
                mix_group(nc, dve, sh, g, back, x_ready)
                dve.wait_ge(x_ready, g + 1)
                norm_stats(nc, link, norm, sh.x, four(g), var_ready)

            def v_and_rest(g):
                for n in range(2):
                    dve.wait_ge(first_ready, 2 * g + n + 1)
                    if g >= 2:
                        dve.wait_ge(third_ready, 2 * (g - 2) + n + 1)
                    nc.vector.scalar_tensor_tensor(out=rest[n][g % 2][:], in0=ps_qk[n][g % 2],
                                                   scalar=sh.bqk[:, n:n + 1], in1=parts[n][g % NSTORE][:, PART[n][0], :],
                                                   op0=ALU.add, op1=ALU.subtract).then_inc(rest_ready, 1)
                dve.wait_ge(v_ps, g + 1)
                nc.vector.tensor_tensor(sh.v[:, 4 * g:4 * g + 4, :], ps_v[g % 2].rearrange("p (t d) -> p t d", d=D),
                                        sh.bvbc[:].rearrange("p (o d) -> p o d", o=1).to_broadcast([P, 4, D]),
                                        ALU.add).then_inc(v_ready, 1)
            dve.wait_ge(sh.attn_loads, 16 * ATTN_LOADS)
            for s in range(-LEAD, G):
                if s >= 0:
                    v_and_rest(s)
                if s + LEAD < G:
                    mix_and_stats(s + LEAD)

        @blk.gpsimd
        def _(pool):
            link = serial(pool, pool_step)

            def third(g):
                for n in range(2):
                    pool.wait_ge(second_ready, 2 * g + n + 1)
                    nc.gpsimd.tensor_tensor(parts[n][g % NSTORE][:, PART[n][2], :], rest[n][g % 2][:], parts[n][g % NSTORE][:, PART[n][1], :],
                                            ALU.subtract).then_inc(third_ready, 1)
            for q_op in sh.q_op:
                nc.gpsimd.memset(q_op[:], 0.0).then_inc(q_op_cleared, 1)
            for s in range(-LEAD, G):
                if s + LEAD < G:
                    pool.wait_ge(var_ready, s + LEAD + 1)
                    norm_scale(nc, link, sh, norm, four(s + LEAD), scale_ready)
                if 0 <= s:
                    third(s)

        @blk.scalar
        def _(act):
            def first(g):
                for n in range(2):
                    act.wait_ge(qk_ps, 2 * g + n + 1)
                    if g >= NSTORE:
                        act.wait_ge(parts_stored[n][g % NSTORE], 16 * (g // NSTORE))
                    nc.scalar.activation(parts[n][g % NSTORE][:, PART[n][0], :], ps_qk[n][g % 2], ACT.Identity,
                                         bias=sh.bqk[:, n:n + 1]).then_inc(first_ready, 1)

            def second(g):
                for n in range(2):
                    act.wait_ge(rest_ready, 2 * g + n + 1)
                    nc.scalar.activation(parts[n][g % NSTORE][:, PART[n][1], :], rest[n][g % 2][:], ACT.Copy) \
                      .then_inc(second_ready, 1)
            act.wait_ge(sh.attn_loads, 16 * ATTN_LOADS)
            for s in range(-3, G):
                if 0 <= s + 1 < G:
                    act.wait_ge(zT_ps, s + 2)
                    if s + 1 >= 2:
                        act.wait_ge(v_ps, s)
                    nc.scalar.activation(zT[(s + 1) % 2][:], ps_z[(s + 1) % 2], ACT.Copy).then_inc(zT_ready, 1)
                if 0 <= s:
                    first(s)
                if s + 3 < G:
                    act.wait_ge(scale_ready, s + 4)
                    norm_rows(nc, norm, sh.x, sh.y, four(s + 3), z_ready)
                if 0 <= s:
                    second(s)

        @blk.sync
        def _(sp):
            load_back(nc, sp, sh, back)
            for g in range(G):
                b, half = g // 2, g % 2
                if g == G // 2:
                    for n in range(2):
                        for k in range(2):
                            sp.wait_ge(parts_stored[n][k], 16)
                    sp.wait_ge(q_op_cleared, NG)
                    sp.dma_start(sh.zero_dram, sh.q_op[1][0:MROWS, :, :]).then_inc(zero_stored, 16)
                    sp.wait_ge(zero_stored, 16)
                if g >= G // 2:
                    for dst, src in operand_rows(sh, 0, 0)[g - G // 2::G - G // 2]:
                        sp.dma_start(dst, src).then_inc(sh.op_loaded[0], 16)
                for n in range(2):
                    sp.wait_ge(third_ready, 2 * g + n + 1)
                    sp.dma_start((sh.q_dram, sh.k_dram)[n][b, :, :, :, half * QW:(half + 1) * QW]
                                 .rearrange("h d m t -> (h d) m t"), parts[n][g % NSTORE][:]) \
                      .then_inc(parts_stored[n][g % NSTORE], 16)
            for n in range(2):
                for k in range(NSTORE):
                    sp.wait_ge(parts_stored[n][k], 16 * len(range(k, G, NSTORE)))
            sp.wait_ge(sh.op_loaded[0], 16 * OP_LOADS)

        @blk.tensor
        def _(pe):
            def transposes(g):
                pe.wait_ge(z_ready, g + 1)
                if g >= 2:
                    pe.wait_ge(zT_ready, g - 1)
                for j in range(4):
                    ins = nc.tensor.transpose(ps_z[g % 2][:, j * P:(j + 1) * P], sh.y[:, 4 * g + j, :], sh.ident[:])
                ins.then_inc(zT_ps, 1)
            pe.wait_ge(sh.attn_loads, 16 * ATTN_LOADS)
            transposes(0)
            for g in range(G):
                if g < G - 1:
                    transposes(g + 1)
                pe.wait_ge(zT_ready, g + 1)
                for n, name in enumerate(("Wq", "Wk")):
                    if g >= 2:
                        pe.wait_ge(rest_ready, 2 * (g - 2) + n + 1)
                    nc.tensor.matmul(ps_qk[n][g % 2], sh.w[name][:], zT[g % 2][:], start=True, stop=True) \
                      .then_inc(qk_ps, 1)
                if g >= 2:
                    pe.wait_ge(v_ready, g - 1)
                for j in range(4):
                    ins = nc.tensor.matmul(ps_v[g % 2][:, j * D:(j + 1) * D], zT[g % 2][:, j * P:(j + 1) * P],
                                           sh.w["Wv"][:], start=True, stop=True)
                ins.then_inc(v_ps, 1)


def maximum_units(half):
    t0 = HT * half
    rows = []
    for par in range(2):
        pair = (par, par + 2)
        row = [[(h, t, 0, 4)] for h in pair for t in range(t0, t0 + HT) if half]
        row += [[(h, t0 + 2, t0, 2), (h, t0 + 3, t0, 2)] for h in pair]
        row += [[(h, t0 + i, t0 + i, 1) for i in range(HT)] for h in pair]
        row.append([(h, t0 + i + 1, t0 + i, 1) for h in pair for i in (0, 2)])
        rows.append(row)
    return [u for both in zip(*rows) for u in both]


def operand_rows(sh, b, g):
    pairs = []
    for par in range(2):
        for src, dst, k_side in ((sh.q_dram, sh.q_op[g], 0), (sh.k_dram, sh.k_op[g], 1)):
            rows = src[bass.ds(b, 1), g * GH:(g + 1) * GH, :, :, :].rearrange("o (s r) d m t -> r d m (o s) t", r=2)[par]
            at = 64 * par
            for n in (3, 2, 1):
                first = (3 - n) * k_side
                for heads in ((slice(0, 1), slice(1, 2)) if n == 2 else (slice(0, 2),)):
                    pairs.append((dst[at:at + n * HD, heads, :], rows[:, first:first + n, heads]))
                at += n * HD
        pairs.append((sh.q_op[g][64 * par + TERMS:64 * par + TERMS + MROWS, :, :], sh.zero_dram))
    return pairs


def load_ops(sp, sh, b, g):
    for dst, src in operand_rows(sh, b, g):
        sp.dma_start(dst, src).then_inc(sh.op_loaded[g], 16)


def attention_phase(nc, sh):
    low, high = maximum_units(0), maximum_units(1)
    prologue_ring = [("S", u) for u in low + high]
    prologue_ring.insert(len(low) + 8, ("M", 0))
    step_ring = list(prologue_ring)
    step_ring.insert(5, ("M", 1))
    step_ring.insert(7, ("E", 0))
    step_ring.insert(9, ("E", 1))
    NPRO, NRING = len(prologue_ring), len(step_ring)
    prologue_banks = [i % 3 for i in range(NPRO - 1)] + [1]
    step_banks = [i % 3 for i in range(NRING - 1)] + [1]
    assert prologue_banks[-4:] == step_banks[-4:] == [0, 1, 2, 1]

    def since(banks, i, before):
        line = before + banks[:i]
        return line[::-1].index(banks[i]) + 1 if banks[i] in line else None
    segments = [[(0, 0, 512)], [(1, 128, 384), (3, 384, 128)], [(2, 256, 256)],
                [(0, 512, 512)], [(1, 512, 512)], [(2, 512, 512)], [(3, 512, 512)], [(4, 512, 512)],
                [(5, 640, 384), (7, 896, 128)], [(6, 768, 256)]]
    NU = len(segments)
    diagonals = [[sum(w for _, _, w in unit[:i]) for i, (kt, q0, _) in enumerate(unit) if q0 == kt * P]
                 for unit in segments]
    ND = sum(len(d) for d in diagonals)
    FIRST_HIGH, LAST_LOW = 3, 2
    unit_columns = [sum(width for _, _, width in unit) for unit in segments]
    share = [(NRING * u // NU, NRING * (u + 1) // NU) for u in range(NU)]

    with ExitStack() as ctx:
        sem = lambda n: ctx.enter_context(nc.semaphore("a_" + n))
        sb = lambda n, s, d: ctx.enter_context(nc.sbuf_tensor("a_" + n, s, d))
        neg_max_loaded = [sem(f"neg_max_loaded{h}") for h in range(2)]
        neg_max_stored = [sem(f"neg_max_stored{h}") for h in range(2)]
        ring_full, ring_empty = sem("ring_full"), sem("ring_empty")
        split_step, split_ready, neg_maxT_ready, rden_ready = sem("split_step"), sem("split_ready"), sem("neg_maxT_ready"), sem("rden_ready")
        scores_ready, probs_ready = sem("scores_ready"), sem("probs_ready")
        o_low_done, o_high_done, o_low_read, o_high_read = sem("o_low_done"), sem("o_high_done"), sem("o_low_read"), sem("o_high_read")
        v_aug_ready, bias_added, split_cleared = sem("v_aug_ready"), sem("bias_added"), sem("split_cleared")
        masked, probs_seen = sem("masked"), sem("probs_seen")
        neg_max = sb("neg_max", [P, 2, GH, HT], F32)
        remain = sb("remain", [P, 2, GH, HT], F32)
        split = sb("split", [P, 2, P], BF16)
        split_view = split[:, :, 0:GH * MROWS * HT].rearrange("p a (h m t) -> p a h m t", h=GH, m=MROWS)
        neg_maxT = [sb(f"neg_maxT{h}", [GH * MROWS * HT, P], BF16) for h in range(2)]
        probs = [sb(f"probs{k}", [P, 2, 2, QW], F32) for k in range(2)]
        rden = [sb(f"rden{h}", [P, HT * GH], F32) for h in range(2)]
        q_op, k_op, v_aug, op_loaded = sh.q_op, sh.k_op, sh.v_aug, sh.op_loaded
        nm_dram = [nc.dram_tensor(f"neg_max_dram{h}", (GH, MROWS, HT * P), BF16, kind="Internal").ap()
                   for h in range(2)]
        ring_bank, o_bank, scores = sh.bank[0:3], sh.bank[3], sh.two_banks[2:4]
        blk = ctx.enter_context(nc.Block())
        ADDED = P // 4

        @blk.sync
        def _(sp):
            def move_max(group, g, half):
                sp.wait_ge(neg_maxT_ready, group * 2 + half + 1)
                sp.dma_start(nm_dram[half].rearrange("h m (t q) -> (h m t) q", q=P), neg_maxT[half][:]) \
                  .then_inc(neg_max_stored[half], 16)
                sp.wait_ge(neg_max_stored[half], group * 16 + 16)
                for par in range(2):
                    at = 64 * par + TERMS
                    sp.dma_start(q_op[g][at:at + MROWS, :, half * QW:(half + 1) * QW],
                                 nm_dram[half].rearrange("(s r) m q -> r m s q", r=2)[par]) \
                      .then_inc(neg_max_loaded[half], 16)
            load_ops(sp, sh, 0, 1)
            move_max(0, 0, 0)
            with sp.Fori(0, B) as b:
                for g in range(NG):
                    n = b * NG + g
                    move_max(n, g, 1)
                    if g < NG - 2:
                        load_ops(sp, sh, b, g + 2)
                    else:
                        load_ops(sp, sh, (b + 1) % B, g - (NG - 2))
                    move_max(n + 1, (g + 1) % NG, 0)
            for g in range(NG):
                sp.wait_ge(op_loaded[g], 16 * OP_LOADS * (B + (g < 2)))
            sp.wait_ge(neg_max_loaded[0], 32 * (B * NG + 1))
            sp.wait_ge(neg_max_loaded[1], 32 * B * NG)

        @blk.gpsimd
        def _(pool):
            def augment(b, g):
                nc.gpsimd.tensor_copy(v_aug[g % 2][:, :, :, 0:HD],
                                      sh.v[:, bass.ds(b * TB, TB), g * GH * HD:(g + 1) * GH * HD]
                                      .rearrange("p t (h d) -> p t h d", d=HD)).then_inc(v_aug_ready, 1)
            augment(0, 0)
            augment(0, 1)
            nc.gpsimd.tensor_tensor(sh.x[:], sh.x[:], sh.bobc[:].rearrange("p (o d) -> p o d", o=1)
                                    .to_broadcast([P, NT, D]), ALU.add).then_inc(bias_added, 1)
            with pool.Fori(0, B) as b:
                for g in range(NG):
                    for u in range(NU):
                        if diagonals[u]:
                            pool.wait_ge(probs_ready, ((b * NG + g) * NU + u) * 2 + 2)
                            pool.sem_inc(probs_seen, 1)
                        for col in diagonals[u]:
                            block = probs[u % 2][:, :, :, col:col + P]
                            nc.gpsimd.affine_select(out=block, in_=block, compare_op=ALU.is_ge, fill=0.0, base=0,
                                                    pattern=[[0, 2], [0, 2], [1, P]], channel_multiplier=-1) \
                              .then_inc(masked, 1)
                    pool.wait_ge(o_high_done, b * NG + g + 1)
                    if g < NG - 2:
                        augment(b, g + 2)
                    else:
                        augment((b + 1) % B, g - (NG - 2))

        @blk.scalar
        def _(act):
            act.sem_inc(o_low_read, 1)
            act.sem_inc(o_high_read, 1)
            with act.Fori(0, B) as b:
                for g in range(NG):
                    n = b * NG + g
                    for u in range(NU):
                        for pair in range(2):
                            act.wait_ge(scores_ready, (n * NU + u) * 2 + pair + 1)
                            cols = slice(0, unit_columns[u])
                            nc.scalar.activation(probs[u % 2][:, pair, :, cols],
                                                 scores[pair].rearrange("p (h q) -> p h q", q=QW)[:, :, cols],
                                                 ACT.Exp, scale=SCALE).then_inc(probs_ready, 1)
                        if u == LAST_LOW + 1:
                            act.wait_ge(o_low_done, n + 1)
                            nc.scalar.activation(sh.o_sb[:, 0:QW], o_bank, ACT.Copy).then_inc(o_low_read, 1)
                    act.wait_ge(o_high_done, n + 1)
                    nc.scalar.activation(sh.o_sb[:, QW:T], o_bank, ACT.Copy).then_inc(o_high_read, 1)

        @blk.vector
        def _(dve):
            flat = sh.block_max[:].rearrange("p h t j -> p (h t j)")

            def places(unit):
                h, t, j, width = unit[0]
                if width == 4:
                    return sh.block_max[:, h, t, j:j + 4]
                if width == 2:
                    return sh.block_max[:, h, t:t + 2, j:j + 2]
                first = t * TB + j
                if unit[2][0] == h:
                    return flat[:, h * TB * TB + first:h * TB * TB + first + 3 * (TB + 1) + 1:TB + 1]
                both = flat.rearrange("p (s r x) -> p s r x", r=2, x=TB * TB)[:, :, h % 2, :]
                return both[:, :, first:first + 2 * (TB + 1) + 1:2 * (TB + 1)]

            def split_max(group, half, step):
                done = (group * 2 + half) * 4
                nm, rm = neg_max[:, half], remain[:, half]
                part = lambda i: split_view[:, half, :, i, :]
                if step == 0:
                    keys = HT * (half + 1)
                    nc.vector.tensor_reduce(nm, sh.block_max[:, :, HT * half:HT * half + HT, 0:keys], axis=AX.X,
                                            op=ALU.max, negate=True).then_inc(split_step, 1)
                    return
                dve.wait_ge(split_step, done + step)
                if step == 1:
                    nc.vector.tensor_copy(part(0), nm).then_inc(split_step, 1)
                elif step == 2:
                    nc.vector.tensor_tensor(rm, nm, part(0), ALU.subtract).then_inc(split_step, 1)
                elif step == 3:
                    nc.vector.tensor_copy(part(1), rm).then_inc(split_step, 1)
                else:
                    nc.vector.tensor_tensor(part(2), rm, part(1), ALU.subtract).then_inc(split_ready, 1)

            def empty(kind, what, count, at, group, slot, cols, n):
                bank = ring_bank[at]
                dve.wait_ge(ring_full, count + 1)
                if kind == "S":
                    nc.vector.tensor_reduce(places(what), bank.rearrange("p (a q) -> p a q", q=P), axis=AX.X,
                                            op=ALU.max).then_inc(ring_empty, 1)
                elif kind == "M":
                    nc.vector.tensor_copy(neg_maxT[what][:], bank.bitcast(BF16)[0:GH * MROWS * HT, 0:P]) \
                      .then_inc(neg_maxT_ready, 1)
                    dve.wait_ge(neg_maxT_ready, group * 2 + what + 1)
                    dve.sem_inc(ring_empty, 1)
                else:
                    heads = bank.rearrange("p (t h c) -> p t h c", h=GH, c=ADDED)
                    recip = rden[what][:].rearrange("p (t h) -> p t h", h=GH)
                    nc.vector.reciprocal(recip, heads[:, :, :, HD]).then_inc(rden_ready, 1)
                    dve.wait_ge(rden_ready, 2 * n + what + 1)
                    nc.vector.tensor_tensor(sh.att[:, bass.ds(slot * TB + what * HT, HT), cols:cols + GH * HD]
                                            .rearrange("p t (h d) -> p t h d", d=HD),
                                            heads[:, :, :, 0:HD],
                                            rden[what][:].rearrange("p (t h o) -> p t h o", h=GH, o=1)
                                            .to_broadcast([P, HT, GH, HD]), ALU.mult).then_inc(ring_empty, 1)

            def empty_all(entries, banks, first, group, own, slot, cols, n):
                seen = 0
                if own is None:
                    steps = []
                else:
                    dve.wait_ge(ring_empty, first)
                    split_max(own, 1, 0)
                    steps = [(own, 1, k) for k in range(1, 5)]
                for i, (kind, what) in enumerate(entries):
                    whose = own if (kind, what) == ("M", 1) else group
                    empty(kind, what, first + i, banks[i], whose, slot, cols, n)
                    if steps:
                        split_max(*steps.pop(0))
                    seen += kind == "S"
                    if kind == "S" and seen == len(low):
                        dve.wait_ge(ring_empty, first + i + 1)
                        split_max(group, 0, 0)
                        steps = [(group, 0, k) for k in range(1, 5)]
            nc.vector.memset(split[:], 0.0).then_inc(split_cleared, 1)
            dve.wait_ge(split_cleared, 1)
            empty_all(prologue_ring, prologue_banks, 0, 0, None, 0, 0, 0)
            with dve.Fori(0, B) as b:
                for g in range(NG):
                    n = b * NG + g
                    slot, cols = (b + 1, (g - 1) * GH * HD) if g else (b + 0, (NG - 1) * GH * HD)
                    empty_all(step_ring, step_banks, n * NRING + NPRO, n + 1, n, slot, cols, n)
            for i in range(2):
                empty("E", i, NPRO + B * NG * NRING + i, i, None, B, (NG - 1) * GH * HD, B * NG)

        @blk.tensor
        def _(pe):
            def fill(kind, what, count, at, lag, group, g, loads, n):
                bank = ring_bank[at]
                if lag is not None:
                    pe.wait_ge(ring_empty, count - lag + 1)
                if kind == "S":
                    pe.wait_ge(op_loaded[g], loads)
                    col = 0
                    diagonal = what[0][1] == what[0][2]
                    for i, (h, t, j, width) in enumerate(what):
                        rows = slice(64 * (h % 2), 64 * (h % 2) + 64)
                        ins = nc.tensor.matmul(bank[:, col:col + width * P], q_op[g][rows, h // 2, t * P:(t + 1) * P],
                                               k_op[g][rows, h // 2, j * P:(j + width) * P], start=(i == 0),
                                               stop=(i == len(what) - 1 and not diagonal))
                        col += width * P
                    if diagonal:
                        ins = nc.tensor.matmul(bank, sh.identb[:], sh.mask_qk[:].rearrange("p a q -> p (a q)"),
                                               start=False, stop=True)
                elif kind == "M":
                    pe.wait_ge(split_ready, group * 2 + what + 1)
                    ins = nc.tensor.transpose(bank.bitcast(BF16)[:, 0:P], split[:, what, :], sh.identb[:])
                else:
                    pe.wait_ge((o_low_read, o_high_read)[what], n + 1)
                    for j in range(HT):
                        ins = nc.tensor.transpose(bank[:, j * P:(j + 1) * P],
                                                  sh.o_sb[:, what * QW + j * P:what * QW + (j + 1) * P], sh.ident[:])
                ins.then_inc(ring_full, 1)

            def score_pair(n, g, u, pair):
                if u:
                    pe.wait_ge(probs_ready, (n * NU + u) * 2 + pair - 1)
                for r in range(2):
                    rows = slice(64 * r, 64 * r + 64)
                    col = r * QW
                    for i, (kt, q0, width) in enumerate(segments[u]):
                        ins = nc.tensor.matmul(scores[pair][:, col:col + width],
                                               k_op[g][rows, pair, kt * P:(kt + 1) * P],
                                               q_op[g][rows, pair, q0:q0 + width], start=(i == 0),
                                               stop=(i == len(segments[u]) - 1))
                        col += width
                ins.then_inc(scores_ready, 1)

            def products(n, g, u):
                pe.wait_ge(probs_ready, (n * NU + u) * 2 + 2)
                if diagonals[u]:
                    pe.wait_ge(masked, n * ND + sum(len(d) for d in diagonals[:u + 1]))
                if u == 0:
                    pe.wait_ge(v_aug_ready, n + 1)
                    pe.wait_ge(o_high_read, n + 1)
                if u == FIRST_HIGH:
                    pe.wait_ge(o_low_read, n + 2)
                col = 0
                for kt, q0, width in segments[u]:
                    half = q0 // QW
                    at = q0 % QW
                    stop = u in (LAST_LOW, NU - 1)
                    for h in range(GH):
                        ins = nc.tensor.matmul(o_bank[ADDED * h:ADDED * (h + 1), at:at + width],
                                               v_aug[g % 2][:, kt, h, :],
                                               probs[u % 2][:, h // 2, h % 2, col:col + width],
                                               start=(kt == 0), stop=stop, tile_position=(0, ADDED * h))
                    col += width
                    if u == LAST_LOW and half == 0:
                        ins.then_inc(o_low_done, 1)
                if u == NU - 1:
                    ins.then_inc(o_high_done, 1)

            for i, (kind, what) in enumerate(prologue_ring):
                fill(kind, what, i, prologue_banks[i], since(prologue_banks, i, []), 0, 0, 16 * OP_LOADS, 0)
            with pe.Fori(0, B) as b:
                for g in range(NG):
                    n = b * NG + g
                    loads = (b + 1 + (g == NG - 1)) * (16 * OP_LOADS)

                    def fill_next(entries, count):
                        for _ in range(count):
                            i = entries.pop(0)
                            kind, what = step_ring[i]
                            own = (kind, what) == ("M", 1)
                            fill(kind, what, n * NRING + (NPRO + i), step_banks[i],
                                 since(step_banks, i, step_banks), n if own else n + 1, (g + 1) % NG, loads, n)
                    for u in range(NU):
                        if u == 0:
                            pe.wait_ge(neg_max_loaded[0], n * 32 + 32)
                        if u == FIRST_HIGH:
                            pe.wait_ge(neg_max_loaded[1], n * 32 + 32)
                        beside = list(range(*share[u]))
                        score_pair(n, g, u, 0)
                        fill_next(beside, 1)
                        score_pair(n, g, u, 1)
                        fill_next(beside, 1)
                        if u:
                            products(n, g, u - 1)
                        fill_next(beside, len(beside))
                    products(n, g, NU - 1)
            for i in range(2):
                fill("E", i, NPRO + B * NG * NRING + i, i, since([0, 1], i, step_banks), None, None, None, B * NG)


def build(nc, a, out):
    with ExitStack() as ctx:
        sh = Shared()
        sb = lambda n, s, d: ctx.enter_context(nc.sbuf_tensor(n, s, d))
        psum = ctx.enter_context(nc.psum_tensor("psum", [P, 8 * 512], F32))
        sh.bank = [psum[:, 512 * i:512 * (i + 1)] for i in range(8)]
        sh.two_banks = [psum[:, 1024 * i:1024 * (i + 1)] for i in range(4)]
        sem = lambda n: ctx.enter_context(nc.semaphore(n))
        sh.x_loaded = [sem(f"x_loaded{c}") for c in range(NCHUNK)]
        sh.op_loaded = [sem(f"op_loaded{g}") for g in range(NG)]
        sh.expert_loads, sh.attn_loads = sem("expert_loads"), sem("attn_loads")
        sh.x, sh.y, sh.v = [sb(n, [P, NT, D], F32) for n in ("x_sb", "y_sb", "v_sb")]
        sh.att = sb("att_sb", [P, (B + 1) * TB, D], F32)
        sh.xn = sh.att[:, 0:NT, :]
        sh.w = {n: sb(n + "_sb", [D, D], F32) for n in ("Wq", "Wk", "Wv", "Wo")}
        sh.bqk, sh.bvbc, sh.bobc = sb("bqk", [P, 2], F32), sb("bv_bc", [P, D], F32), sb("bo_bc", [P, D], F32)
        sh.w1, sh.w2 = sb("w1_sb", [P, E, F], F32), sb("w2_sb", [P, E, FC, D], F32)
        sh.b1bc, sh.b2bc = sb("b1_bc", [P, E * F], F32), sb("b2_bc", [P, E * D], F32)
        sh.cgbT = sb("cgbT", [P, P // 4], F32)
        sh.ident, sh.identb = sb("ident", [P, P], F32), sb("identb", [P, P], BF16)
        sh.before, sh.onesb = sb("before", [P, P], BF16), sb("onesb", [P, P], BF16)
        sh.mask_qk = sb("mask_qk", [P, 4, P], BF16)
        sh.em8, sh.ones8 = sb("em8", [P, E], F32), sb("ones8", [P, E], F32)
        sh.thr, sh.tile_id, sh.neg_half = [sb(n, [P, NT], F32) for n in ("thr", "tile_id", "neg_half")]
        sh.slot_id = sb("slot_id", [P, SLOTS, E - 1], F32)
        sh.row128, sh.row_slots, sh.part_id = sb("row128", [P, P], F32), sb("row_slots", [P, SLOTS], F32), sb("part_id", [P, 1], F32)
        sh.trash, sh.keep = sb("trash", [P, SLOTS], F32), sb("keep", [P, E, NT], F32)
        sh.norms = [Norm(sb, "norm0"), Norm(sb, "norm1")]
        sh.mx, sh.half_alpha = sb("mx", [P, NT], F32), sb("half_alpha", [P, NT], F32)
        sh.gather_row, sh.scatter_row = sb("gather_row", [P, SLOTS], I32), sb("scatter_row", [P, SLOTS], I32)
        sh.slot_expert = sb("slot_expert", [P, SLOTS], I32)
        sh.block_max = sb("block_max", [P, GH, TB, TB], F32)
        sh.q_op = [sb(f"q_op{g}", [P, 2, T], BF16) for g in range(NG)]
        sh.k_op = [sb(f"k_op{g}", [P, 2, T], BF16) for g in range(NG)]
        sh.v_aug = [sb(f"v_aug{k}", [P, TB, GH, P // 4], F32) for k in range(2)]
        sh.o_sb = sb("o_sb", [P, T], F32)
        sh.q_dram, sh.k_dram = [nc.dram_tensor(n, (B, H, HD, 3, T), BF16, kind="Internal").ap()
                                for n in ("q_dram", "k_dram")]
        sh.zero_dram = nc.dram_tensor("zero_dram", (MROWS, 2, T), BF16, kind="Internal").ap()
        sh.xn_dram = nc.dram_tensor("xn_dram", (N, D), F32, kind="Internal").ap()
        sh.ys_dram = nc.dram_tensor("ys_dram", (N + SLOTS * P, D), F32, kind="Internal").ap()
        setup_phase(nc, sh, a)
        route_phase(nc, sh, 0, a)
        expert_phase(nc, sh, 0)
        qkv_phase(nc, sh)
        attention_phase(nc, sh)
        route_phase(nc, sh, 1, a)
        expert_phase(nc, sh, 1)
        last_phase(nc, sh, out)


_INS = {"x": "L0_attn_x", "Wq": "L0_attn_Wq", "bq": "L0_attn_bq", "Wk": "L0_attn_Wk", "bk": "L0_attn_bk",
        "Wv": "L0_attn_Wv", "bv": "L0_attn_bv", "Wo": "L0_attn_Wo", "bo": "L0_attn_bo",
        "centroids": "L0_ffn_centroids", "ln_g": "L0_ffn_ln_g", "ln_b": "L0_ffn_ln_b", "w1": "L0_ffn_w1",
        "b1": "L0_ffn_b1", "w2": "L0_ffn_w2", "b2": "L0_ffn_b2"}


def kernel(**inputs):
    import concourse.bacc as bacc
    from concourse.bass_utils import run_bass_kernel_spmd

    nc = bacc.Bacc("TRN2", target_bir_lowering=False, num_devices=1)
    arrays, args = {}, {}
    for short, name in _INS.items():
        arrays[f"in_{short}"] = np.ascontiguousarray(inputs[name])
        args[short] = nc.dram_tensor(f"in_{short}", arrays[f"in_{short}"].shape, F32, kind="ExternalInput").ap()
    out = nc.dram_tensor("out", (B, T, D), F32, kind="ExternalOutput").ap()
    build(nc, args, out)
    return run_bass_kernel_spmd(nc, [arrays], core_ids=[0]).results[0]["out"]
```
